# Optimizing a Trainium2 kernel written in Bass

```python
import numpy as np
import jax
import jax.numpy as jnp

def _softmax(x, axis=-1):
    return jax.nn.softmax(x, axis=axis)

def _gelu(x):
    return jax.nn.gelu(x, approximate=True)

def _silu(x):
    return jax.nn.silu(x)

def _sigmoid(x):
    return jax.nn.sigmoid(x)

def _layernorm(x, axis=-1, eps=1e-05):
    m = jnp.mean(x, axis=axis, keepdims=True)
    v = jnp.var(x, axis=axis, keepdims=True)
    return (x - m) / jnp.sqrt(v + eps)

def _scatter_add(tgt, idx, src, axis=0):
    return tgt.at[idx].add(src)

def _segment_sum(src, seg, n):
    return jax.ops.segment_sum(src, seg, n)
kernel_name = 'mk_hybrid_d1_jaxref_r8_ae2a3a'

def setup_inputs(seed: int=0):
    np.random.seed(seed)
    _w = jnp.asarray

    def _L0_attn_a_setup():
        import jax, jax.numpy as jnp
        import numpy as np
        from jax import lax
        BLOCK_LEN = 128
        NEG_INF = -1000000000.0
        key = jax.random.key(seed)
        ks = jax.random.split(key, 8)
        N, L, Dm = (2, 1024, 512)
        W, H, dh = (128, 16, 64)
        s = lambda fan: 1.0 / np.sqrt(fan)
        return {'inputs': jax.random.normal(ks[0], (N, L, Dm), jnp.float32), 'conv_w': jax.random.normal(ks[1], (3, Dm, 3 * W), jnp.float32) * s(3 * Dm), 'conv_b': jnp.zeros((3 * W,), jnp.float32), 'wq': jax.random.normal(ks[2], (W, H, dh), jnp.float32) * s(W), 'bq': jnp.zeros((H, dh), jnp.float32), 'wk': jax.random.normal(ks[3], (W, H, dh), jnp.float32) * s(W), 'bk': jnp.zeros((H, dh), jnp.float32), 'wv': jax.random.normal(ks[4], (W, H, dh), jnp.float32) * s(W), 'bv': jnp.zeros((H, dh), jnp.float32), 'wo': jax.random.normal(ks[5], (H, dh, W), jnp.float32) * s(H * dh), 'bo': jnp.zeros((W,), jnp.float32), 'proj_w': jax.random.normal(ks[6], (W, Dm), jnp.float32) * s(W), 'proj_b': jnp.zeros((Dm,), jnp.float32)}
    _L0_attn_a_in = _L0_attn_a_setup()

    def _L0_attn_b_setup():
        import jax, jax.numpy as jnp
        import numpy as np
        import math
        EMBED_DIM = 512
        NUM_HEADS = 32
        NUM_KV_HEADS = 8
        HEAD_DIM = EMBED_DIM // NUM_HEADS
        GROUP_SIZE = NUM_HEADS // NUM_KV_HEADS
        KV_DIM = EMBED_DIM // GROUP_SIZE
        BATCH, SEQ = (1, 256)

        def softermax(x, axis=-1):
            m = jnp.max(x, axis=axis, keepdims=True)
            p = jnp.exp2(x - m)
            return p / jnp.sum(p, axis=axis, keepdims=True)
        key = jax.random.key(seed)
        ks = jax.random.split(key, 9)
        s = 1.0 / math.sqrt(EMBED_DIM)
        return {'x': jax.random.normal(ks[0], (BATCH, SEQ, EMBED_DIM), jnp.float32), 'q_w': jax.random.normal(ks[1], (EMBED_DIM, EMBED_DIM), jnp.float32) * s, 'q_b': jax.random.normal(ks[2], (EMBED_DIM,), jnp.float32) * s, 'k_w': jax.random.normal(ks[3], (KV_DIM, EMBED_DIM), jnp.float32) * s, 'k_b': jax.random.normal(ks[4], (KV_DIM,), jnp.float32) * s, 'v_w': jax.random.normal(ks[5], (KV_DIM, EMBED_DIM), jnp.float32) * s, 'v_b': jax.random.normal(ks[6], (KV_DIM,), jnp.float32) * s, 'o_w': jax.random.normal(ks[7], (EMBED_DIM, EMBED_DIM), jnp.float32) * s, 'o_b': jax.random.normal(ks[8], (EMBED_DIM,), jnp.float32) * s}
    _L0_attn_b_in = _L0_attn_b_setup()

    def _L0_ffn_setup():
        import jax, jax.numpy as jnp
        import numpy as np
        BATCH, SEQ, D = (2, 256, 512)
        K, TOPK, RANK = (64, 16, 16)
        ALPHA = 32.0
        SCALING = ALPHA / RANK
        key = jax.random.key(seed)
        k1, k2, k3, k4 = jax.random.split(key, 4)
        x = jax.random.normal(k1, (BATCH, SEQ, D), dtype=jnp.float32)
        A = jax.random.normal(k2, (K, RANK, D), dtype=jnp.float32) * 0.02
        B = jax.random.normal(k3, (K, D, RANK), dtype=jnp.float32) * 0.02
        Wr = jax.random.normal(k4, (K, D), dtype=jnp.float32) * 0.02
        return {'x': x, 'A': A, 'B': B, 'Wr': Wr}
    _L0_ffn_in = _L0_ffn_setup()
    _d = {'L0_attn_a_inputs': _L0_attn_a_in['inputs'], 'L0_attn_a_conv_w': _L0_attn_a_in['conv_w'], 'L0_attn_a_conv_b': _L0_attn_a_in['conv_b'], 'L0_attn_a_wq': _L0_attn_a_in['wq'], 'L0_attn_a_bq': _L0_attn_a_in['bq'], 'L0_attn_a_wk': _L0_attn_a_in['wk'], 'L0_attn_a_bk': _L0_attn_a_in['bk'], 'L0_attn_a_wv': _L0_attn_a_in['wv'], 'L0_attn_a_bv': _L0_attn_a_in['bv'], 'L0_attn_a_wo': _L0_attn_a_in['wo'], 'L0_attn_a_bo': _L0_attn_a_in['bo'], 'L0_attn_a_proj_w': _L0_attn_a_in['proj_w'], 'L0_attn_a_proj_b': _L0_attn_a_in['proj_b'], 'L0_attn_b_q_w': _L0_attn_b_in['q_w'], 'L0_attn_b_q_b': _L0_attn_b_in['q_b'], 'L0_attn_b_k_w': _L0_attn_b_in['k_w'], 'L0_attn_b_k_b': _L0_attn_b_in['k_b'], 'L0_attn_b_v_w': _L0_attn_b_in['v_w'], 'L0_attn_b_v_b': _L0_attn_b_in['v_b'], 'L0_attn_b_o_w': _L0_attn_b_in['o_w'], 'L0_attn_b_o_b': _L0_attn_b_in['o_b'], 'L0_ffn_A': _L0_ffn_in['A'], 'L0_ffn_B': _L0_ffn_in['B'], 'L0_ffn_Wr': _L0_ffn_in['Wr']}
    _x0 = _d['L0_attn_a_inputs']
    _d['L0_attn_a_inputs'] = jax.random.normal(jax.random.fold_in(jax.random.key(seed), 1), (1, 1024, 512), dtype=_x0.dtype)
    del _x0
    return _d

def reference(L0_attn_a_inputs, L0_attn_a_conv_w, L0_attn_a_conv_b, L0_attn_a_wq, L0_attn_a_bq, L0_attn_a_wk, L0_attn_a_bk, L0_attn_a_wv, L0_attn_a_bv, L0_attn_a_wo, L0_attn_a_bo, L0_attn_a_proj_w, L0_attn_a_proj_b, L0_attn_b_q_w, L0_attn_b_q_b, L0_attn_b_k_w, L0_attn_b_k_b, L0_attn_b_v_w, L0_attn_b_v_b, L0_attn_b_o_w, L0_attn_b_o_b, L0_ffn_A, L0_ffn_B, L0_ffn_Wr):

    def _L0_attn_a_ref(inputs, conv_w, conv_b, wq, bq, wk, bk, wv, bv, wo, bo, proj_w, proj_b):
        import jax, jax.numpy as jnp
        import numpy as np
        from jax import lax
        BLOCK_LEN = 128
        NEG_INF = -1000000000.0
        N, L, Dm = inputs.shape
        x = lax.conv_general_dilated(inputs, conv_w, window_strides=(1,), padding='SAME', dimension_numbers=('NWC', 'WIO', 'NWC')) + conv_b
        q, k, v = jnp.split(x, 3, axis=-1)
        W_ = q.shape[-1]
        nb = L // BLOCK_LEN
        q = q.reshape(N * nb, BLOCK_LEN, W_)
        k = k.reshape(N * nb, BLOCK_LEN, W_)
        v = v.reshape(N * nb, BLOCK_LEN, W_)
        dh = wq.shape[-1]
        qh = jnp.einsum('btd,dhe->bthe', q, wq) + bq
        kh = jnp.einsum('btd,dhe->bthe', k, wk) + bk
        vh = jnp.einsum('btd,dhe->bthe', v, wv) + bv
        scale = 1.0 / jnp.sqrt(jnp.asarray(dh, qh.dtype))
        scores = jnp.einsum('bqhe,bkhe->bhqk', qh * scale, kh)
        causal = jnp.tril(jnp.ones((BLOCK_LEN, BLOCK_LEN), bool))
        scores = jnp.where(causal, scores, NEG_INF)
        p = jax.nn.softmax(scores, axis=-1)
        o = jnp.einsum('bhqk,bkhe->bqhe', p, vh)
        o = jnp.einsum('bqhe,hed->bqd', o, wo) + bo
        o = o.reshape(N, L, W_)
        return o @ proj_w + proj_b

    def _L0_attn_b_ref(x, q_w, q_b, k_w, k_b, v_w, v_b, o_w, o_b):
        import jax, jax.numpy as jnp
        import numpy as np
        import math
        EMBED_DIM = 512
        NUM_HEADS = 32
        NUM_KV_HEADS = 8
        HEAD_DIM = EMBED_DIM // NUM_HEADS
        GROUP_SIZE = NUM_HEADS // NUM_KV_HEADS
        KV_DIM = EMBED_DIM // GROUP_SIZE
        BATCH, SEQ = (1, 256)

        def softermax(x, axis=-1):
            m = jnp.max(x, axis=axis, keepdims=True)
            p = jnp.exp2(x - m)
            return p / jnp.sum(p, axis=axis, keepdims=True)
        B, S, E = x.shape
        q = (x @ q_w.T + q_b).reshape(B, S, NUM_HEADS, HEAD_DIM).transpose(0, 2, 1, 3)
        k = (x @ k_w.T + k_b).reshape(B, S, NUM_KV_HEADS, HEAD_DIM).transpose(0, 2, 1, 3)
        v = (x @ v_w.T + v_b).reshape(B, S, NUM_KV_HEADS, HEAD_DIM).transpose(0, 2, 1, 3)
        k = jnp.repeat(k, GROUP_SIZE, axis=1)
        v = jnp.repeat(v, GROUP_SIZE, axis=1)
        scale = 1.0 / math.sqrt(HEAD_DIM)
        attn = jnp.einsum('bhqd,bhkd->bhqk', q, k * scale)
        attn = softermax(attn, axis=-1)
        out = jnp.einsum('bhqk,bhkd->bhqd', attn, v)
        out = out.transpose(0, 2, 1, 3).reshape(B, S, E)
        return out @ o_w.T + o_b

    def _L0_ffn_ref(x, A, B, Wr):
        import jax, jax.numpy as jnp
        import numpy as np
        BATCH, SEQ, D = (2, 256, 512)
        K, TOPK, RANK = (64, 16, 16)
        ALPHA = 32.0
        SCALING = ALPHA / RANK
        prefix = x.shape[:-1]
        xf = x.reshape(-1, x.shape[-1])
        N = xf.shape[0]
        scores = xf @ Wr.T
        top_vals, top_idx = jax.lax.top_k(scores, TOPK)
        gates = jax.nn.softmax(top_vals, axis=-1)
        G = jnp.zeros((N, K), xf.dtype).at[jnp.arange(N)[:, None], top_idx].set(gates)
        h = jnp.einsum('nd,krd->nkr', xf, A)
        out = jnp.einsum('nkr,kdr->nd', h * G[:, :, None], B)
        return (out * SCALING).reshape(*prefix, -1)
    x = L0_attn_a_inputs
    x = x + _L0_attn_a_ref(_layernorm(x, axis=-1), L0_attn_a_conv_w, L0_attn_a_conv_b, L0_attn_a_wq, L0_attn_a_bq, L0_attn_a_wk, L0_attn_a_bk, L0_attn_a_wv, L0_attn_a_bv, L0_attn_a_wo, L0_attn_a_bo, L0_attn_a_proj_w, L0_attn_a_proj_b)
    x = x + _L0_ffn_ref(_layernorm(x, axis=-1), L0_ffn_A, L0_ffn_B, L0_ffn_Wr)
    x = x + _L0_attn_b_ref(_layernorm(x, axis=-1), L0_attn_b_q_w, L0_attn_b_q_b, L0_attn_b_k_w, L0_attn_b_k_b, L0_attn_b_v_w, L0_attn_b_v_b, L0_attn_b_o_w, L0_attn_b_o_b)
    x = x + _L0_ffn_ref(_layernorm(x, axis=-1), L0_ffn_A, L0_ffn_B, L0_ffn_Wr)
    return x

_drawn_inputs = setup_inputs


def setup_inputs(seed=0):
    import zlib

    import numpy as np

    out = dict(_drawn_inputs(seed))
    spreads = {'L0_attn_a_conv_b': (0.0, 0.1),
     'L0_attn_a_bq': (0.0, 0.364),
     'L0_attn_a_bk': (0.0, 2.0),
     'L0_attn_a_bv': (0.0, 0.1),
     'L0_attn_a_bo': (0.0, 0.1),
     'L0_attn_a_proj_b': (0.0, 0.1)}
    factors = {'L0_attn_b_q_b': 27.331, 'L0_attn_b_k_b': 64.0}
    for name, (base, spread) in spreads.items():
        noise = np.random.default_rng([zlib.crc32(name.encode()), seed]).standard_normal(out[name].shape)
        drawn = base * np.exp(spread * noise) if base else spread * noise
        out[name] = jnp.asarray(drawn.astype(out[name].dtype))
    for name, factor in factors.items():
        out[name] = (out[name] * factor).astype(out[name].dtype)
    return out
```

```python
from contextlib import ExitStack

import concourse.bass as bass
from concourse import mybir

F32 = mybir.dt.float32
F32R = mybir.dt.float32r
BF16 = mybir.dt.bfloat16
ALU = mybir.AluOpType
ACT = mybir.ActivationFunctionType
AX_X = mybir.AxisListType.X

P = 128
HALF = 512
EPS = 1e-5
LN2 = 0.6931471805599453


def bcast(ap, n):
    return ap.unsqueeze(len(ap.shape)).broadcast_to([*ap.shape, n])


def parts_matmul(pe, out, stationary, moving, start, stop):
    pe.matmul(out, stationary[1], moving[0], start=start, stop=False)
    pe.matmul(out, stationary[0], moving[1], start=False, stop=False)
    return pe.matmul(out, stationary[0], moving[0], start=False, stop=stop)


class Core:

    def __init__(self, nc, ctx, T, D):
        self.nc, self.ctx = nc, ctx
        self.T, self.D, self.tiles, self.dk = T, D, T // P, D // P
        self.x = ctx.enter_context(nc.sbuf_tensor("x", [P, self.tiles, D], F32))
        self.ident = ctx.enter_context(nc.sbuf_tensor("ident", [P, P], F32))
        self.eps = ctx.enter_context(nc.sbuf_tensor("eps", [P, 1], F32))
        self.bias_cols = ctx.enter_context(nc.sbuf_tensor("bias_cols", [P, 26], F32))
        self.raw = ctx.enter_context(nc.sbuf_tensor("raw", [P, 8448], F32))

        self.phase_sems = []

    def lasting_sem(self, name):
        return self.ctx.enter_context(self.nc.semaphore(name))

    def sem(self, name):
        self.phase_sems.append(self.nc.alloc_semaphore(name=name))
        return self.phase_sems[-1]

    def end_phase(self):
        self.nc.clear_and_free_semaphores(self.phase_sems)
        self.nc.all_engine_barrier()
        self.phase_sems = []


class Chain:

    def __init__(self, engine, semaphore):
        self.engine, self.semaphore, self.count = engine, semaphore, 0

    def link(self, instruction):
        self.count += 1
        instruction.then_inc(self.semaphore, 1)
        self.engine.wait_ge(self.semaphore, self.count)


class LayerNorm:

    def __init__(self, core, scope, name, pad, banks):
        nc = core.nc
        name += "_ln"
        self.core, self.pad, self.banks = core, pad, banks
        width = core.T + 2 * pad
        self.hi = scope.enter_context(nc.sbuf_tensor(name + "_xT_hi", [P, core.dk, width], F32R))
        self.lo = scope.enter_context(nc.sbuf_tensor(name + "_xT_lo", [P, core.dk, width], F32R))
        self.xn = scope.enter_context(nc.sbuf_tensor(name + "_xn", [P, 2, core.D], F32))
        self.stats = scope.enter_context(nc.sbuf_tensor(name + "_stats", [P, core.tiles, 6], F32))
        self.mv = scope.enter_context(nc.sbuf_tensor(name + "_mv", [P, core.tiles, 2], F32))
        self.std = scope.enter_context(nc.sbuf_tensor(name + "_std", [P, core.tiles], F32))
        self.rstd = scope.enter_context(nc.sbuf_tensor(name + "_rstd", [P, core.tiles], F32))
        self.stats_ready = core.sem(name + "_stats_ready")
        self.std_ready = core.sem(name + "_std_ready")
        self.xn_ready = core.sem(name + "_xn_ready")
        self.turned = core.sem(name + "_turned")
        self.hi_ready = core.sem(name + "_hi_ready")
        self.lo_ready = core.sem(name + "_lo_ready")

    def turned_view(self, i):
        return self.banks[i % len(self.banks)][:, :].rearrange("p (k t) -> p k t", t=P)

    def part(self, which, i):
        a = self.pad + i * P
        return which[:, :, a:a + P]

    def columns(self, k, start, n):
        a = self.pad + start
        return self.hi[:, k, a:a + n], self.lo[:, k, a:a + n]

    def vector_stats(self, dve, chain, tiles, x_loaded=None):
        for i in tiles:
            if x_loaded is not None:
                dve.wait_ge(x_loaded[i], 16)
            dve.bn_stats(self.stats[:, i, :], self.core.x[:, i, :]).then_inc(chain.semaphore, 1)
            chain.count += 1
        dve.wait_ge(chain.semaphore, chain.count)
        for i in tiles:
            dve.bn_aggr(self.mv[:, i, :], self.stats[:, i, :]).then_inc(self.stats_ready, 1)

    def scalar_std(self, act, tiles):
        a, b = tiles[0], tiles[-1] + 1
        act.wait_ge(self.stats_ready, b)
        act.activation(self.std[:, a:b], self.mv[:, a:b, 1], ACT.Sqrt, bias=self.core.eps[:, 0:1])\
           .then_inc(self.std_ready, 1)

    def vector_rstd(self, dve, chain, tiles):
        a, b = tiles[0], tiles[-1] + 1
        dve.wait_ge(self.std_ready, b // 4)
        chain.link(dve.reciprocal(self.rstd[:, a:b], self.std[:, a:b]))

    def vector_all(self, dve, chain, between, x_loaded=None):
        self.vector_stats(dve, chain, range(0, 4), x_loaded)
        self.vector_rstd(dve, chain, range(0, 4))
        for i in range(4):
            self.vector_xn(dve, i)
        self.vector_stats(dve, chain, range(4, 8), x_loaded)
        for i in range(4):
            self.vector_lo(dve, i)
        between()
        self.vector_rstd(dve, chain, range(4, 8))
        self.vector_xn(dve, 4)
        self.vector_xn(dve, 5)
        for i in range(4, 8):
            self.vector_lo(dve, i)
            if i + 2 < 8:
                self.vector_xn(dve, i + 2)

    def vector_xn(self, dve, i):
        if i >= 2:
            dve.wait_ge(self.turned, i - 1)
        dve.tensor_scalar(self.xn[:, i % 2, :], self.core.x[:, i, :], self.mv[:, i, 0:1],
                          self.rstd[:, i:i + 1], ALU.subtract, ALU.mult).then_inc(self.xn_ready, 1)

    def vector_lo(self, dve, i):
        dve.wait_ge(self.hi_ready, i + 1)
        dve.tensor_tensor(self.part(self.lo, i), self.turned_view(i),
                          self.part(self.hi, i).bitcast(F32), ALU.subtract).then_inc(self.lo_ready, 1)

    def tensor_turn(self, pe, i):
        pe.wait_ge(self.xn_ready, i + 1)
        if i >= len(self.banks):
            pe.wait_ge(self.lo_ready, i - len(self.banks) + 1)
        for k in range(self.core.dk):
            last = pe.transpose(self.banks[i % len(self.banks)][:, k * P:(k + 1) * P],
                                self.xn[:, i % 2, k * P:(k + 1) * P], self.core.ident[:, :])
        last.then_inc(self.turned, 1)

    def scalar_hi(self, act, i):
        act.wait_ge(self.turned, i + 1)
        act.copy(self.part(self.hi, i), self.turned_view(i)).then_inc(self.hi_ready, 1)


def phase_conv(core, scope, qkvT, wa, d):
    nc, tiles, dk = core.nc, core.tiles, core.dk
    sb = lambda name, shape, dt: scope.enter_context(nc.sbuf_tensor(name, shape, dt))
    TAPS, M3 = 3, 3
    conv_raw = core.raw[:, 0:TAPS * dk * M3 * P].rearrange("p (s k m) -> p s k m", s=TAPS, k=dk)
    qkv_raw = core.raw[:, 4608:4608 + 3 * 1024].rearrange("p (s n) -> p s n", s=3)
    conv_hi = sb("conv_hi", [P, TAPS, dk, M3 * P], F32R)
    conv_lo = sb("conv_lo", [P, TAPS, dk, M3 * P], F32R)
    out_raw = sb("out_raw", [P, 1536], F32)
    banks = [scope.enter_context(nc.psum_tensor(f"c_turn{i}", [P, HALF], F32)) for i in range(4)]
    conv_ps = [scope.enter_context(nc.psum_tensor(f"c_conv{i}", [P, HALF], F32)) for i in range(4)]
    ln = LayerNorm(core, scope, "c", 1, banks)
    x_loaded = [core.sem(f"x_loaded{i}") for i in range(tiles)]
    conv_loaded = [core.sem(f"conv_loaded{s}") for s in range(TAPS)]
    small_loaded = core.sem("small_loaded")
    proj_loaded = core.sem("proj_loaded")
    consts_ready = core.sem("consts_ready")
    ident_zeroed = core.sem("ident_zeroed")
    pads_ready = core.sem("c_pads_ready")
    conv_hi_ready = core.sem("conv_hi_ready")
    conv_lo_ready = core.sem("conv_lo_ready")
    projw_hi_ready = core.sem("projw_hi_ready")
    projw_lo_ready = core.sem("projw_lo_ready")
    convolved = core.sem("convolved")
    qkv_hi_ready = core.sem("qkv_hi_ready")
    qkv_lo_ready = core.sem("qkv_lo_ready")
    chain_sem = core.sem("c_chain")
    x_dram = d["x"].rearrange("o (i p) d -> (o i) p d", p=P)
    conv_dram = d["conv_w"].rearrange("s (k p) m -> s p k m", p=P)
    projw = [(qkv_raw[:, s, :], wa["qkv_hi"][:, s, :], wa["qkv_lo"][:, s, :]) for s in range(3)]
    projw += [(out_raw[:, 0:1024], wa["wo_hi"], wa["wo_lo"]), (out_raw[:, 1024:1536], wa["pw_hi"], wa["pw_lo"])]
    units = [(h, m) for h in range(2) for m in range(M3)]

    with nc.Block() as block:
        @block.sync
        def _(sp):
            for i in range(0, tiles, 2):
                sp.dma_start(core.x[:, i, :], x_dram[i]).then_inc(x_loaded[i], 16)
                if i < 2 * TAPS:
                    s = i // 2
                    sp.dma_start(conv_raw[:, s], conv_dram[s]).then_inc(conv_loaded[s], 16)
            sp.dma_start(core.bias_cols[:, :], d["bias_cols"]).then_inc(small_loaded, 16)
            for s, name in enumerate(("wq", "wk", "wv")):
                sp.dma_start(qkv_raw[:, s, :], d[name].rearrange("w h e -> w (h e)")).then_inc(proj_loaded, 16)
            sp.dma_start(out_raw[:, 0:1024].rearrange("p (c w) -> p c w", w=P),
                         d["wo"].rearrange("h e w -> (h e) w").rearrange("(c p) w -> p c w", p=P))\
              .then_inc(proj_loaded, 16)
            sp.dma_start(out_raw[:, 1024:1536], d["proj_w"]).then_inc(proj_loaded, 16)

        @block.gpsimd
        def _(pool):
            pool.memset(core.ident[:, :], 0.0).then_inc(ident_zeroed, 1)
            pool.memset(core.eps[:, :], EPS).then_inc(consts_ready, 1)
            pool.wait_ge(ident_zeroed, 1)
            pool.affine_select(out=core.ident[:, :], in_=core.ident[:, :], compare_op=ALU.not_equal, fill=1.0,
                               base=0, pattern=[[-1, P]], channel_multiplier=1).then_inc(consts_ready, 1)
            for part in (ln.hi, ln.lo):
                for column in (0, core.T + 1):
                    pool.memset(part[:, :, column:column + 1].bitcast(F32), 0.0).then_inc(pads_ready, 1)
            for s in range(TAPS):
                for k in range(dk):
                    pool.wait_ge(conv_hi_ready, s * dk + k + 1)
                    pool.tensor_tensor(conv_lo[:, s, k, :], conv_raw[:, s, k, :],
                                       conv_hi[:, s, k, :].bitcast(F32), ALU.subtract).then_inc(conv_lo_ready, 1)
            for n, (raw, hi, lo) in enumerate(projw):
                pool.wait_ge(projw_hi_ready, n + 1)
                pool.tensor_tensor(lo, raw, hi.bitcast(F32), ALU.subtract).then_inc(projw_lo_ready, 1)
            pool.wait_ge(projw_lo_ready, len(projw))

        @block.vector
        def _(dve):
            chain = Chain(dve, chain_sem)
            ln.vector_all(dve, chain, lambda: None, x_loaded)
            dve.wait_ge(proj_loaded, 16 * len(projw))
            for n, (raw, hi, lo) in enumerate(projw):
                dve.tensor_copy(hi, raw).then_inc(projw_hi_ready, 1)
            dve.wait_ge(small_loaded, 16)
            for u, (h, m) in enumerate(units):
                dve.wait_ge(qkv_hi_ready, u + 1)
                dve.scalar_tensor_tensor(
                    out=qkvT[1][:, m, h * HALF:(h + 1) * HALF], in0=conv_ps[u % 4][:, :],
                    scalar=core.bias_cols[:, m:m + 1], in1=qkvT[0][:, m, h * HALF:(h + 1) * HALF].bitcast(F32),
                    op0=ALU.add, op1=ALU.subtract).then_inc(qkv_lo_ready, 1)
            dve.wait_ge(qkv_lo_ready, len(units))

        @block.scalar
        def _(act):
            for i in range(1, tiles, 2):
                act.dma_start(core.x[:, i, :], x_dram[i]).then_inc(x_loaded[i], 16)
            act.wait_ge(consts_ready, 2)
            for s in range(TAPS):
                act.wait_ge(conv_loaded[s], 16)
                for k in range(dk):
                    act.copy(conv_hi[:, s, k, :], conv_raw[:, s, k, :]).then_inc(conv_hi_ready, 1)
                if s == 0:
                    ln.scalar_std(act, range(0, 4))
                    for i in range(0, 4):
                        ln.scalar_hi(act, i)
            ln.scalar_std(act, range(4, 8))
            for i in range(4, tiles):
                ln.scalar_hi(act, i)
            act.wait_ge(small_loaded, 16)
            for u, (h, m) in enumerate(units):
                act.wait_ge(convolved, u + 1)
                act.activation(qkvT[0][:, m, h * HALF:(h + 1) * HALF], conv_ps[u % 4][:, :], ACT.Identity,
                               bias=core.bias_cols[:, m:m + 1]).then_inc(qkv_hi_ready, 1)
            act.wait_ge(qkv_hi_ready, len(units))

        @block.tensor
        def _(pe):
            pe.wait_ge(consts_ready, 2)
            for i in range(5):
                ln.tensor_turn(pe, i)
            for u, (h, m) in enumerate(units):
                if u >= 4:
                    pe.wait_ge(qkv_lo_ready, u - 3)
                pe.wait_ge(pads_ready, 4)
                for s in range(TAPS):
                    pe.wait_ge(ln.lo_ready, (4, 4, 5)[s] if h == 0 else tiles)
                    for k in range(dk):
                        pe.wait_ge(conv_lo_ready, s * dk + k + 1)
                        w = slice(m * P, (m + 1) * P)
                        last = parts_matmul(pe, conv_ps[u % 4][:, :],
                                            (conv_hi[:, s, k, w], conv_lo[:, s, k, w]),
                                            ln.columns(k, h * HALF + s - 1, HALF),
                                            start=(s == 0 and k == 0), stop=(s == TAPS - 1 and k == dk - 1))
                last.then_inc(convolved, 1)
                if u == 0:
                    for i in range(5, tiles):
                        ln.tensor_turn(pe, i)
    return


def phase_block_attention(core, scope, qkvT, wa, d, ffn_raw_loaded):
    nc, tiles = core.nc, core.tiles
    sb = lambda name, shape, dt: scope.enter_context(nc.sbuf_tensor(name, shape, dt))
    ps = lambda name: scope.enter_context(nc.psum_tensor(name, [P, HALF], F32))
    CH = 8
    G = 4 * CH
    V = sb("a_v", [P, tiles, 1024], F32)
    bv_row = sb("bv_row", [P, 1024], F32)
    pb_row = sb("pb_row", [P, HALF], F32)
    q_pad = sb("q_pad", [P, 2, 2, core.T], F32)
    kT = sb("a_kT", [P, 2, core.T], F32)
    prob = sb("a_prob", [P, 3, HALF], F32)
    probT = sb("a_probT", [P, 2, HALF], F32)
    neg_max = sb("a_neg_max", [P, G, 4], F32)
    row_sum = sb("a_row_sum", [P, G, 4], F32)
    row_inv = sb("a_row_inv", [P, G, 4], F32)
    oT_hi = sb("a_oT_hi", [P, 2, HALF], F32R)
    oT_lo = sb("a_oT_lo", [P, 2, HALF], F32R)
    yT_hi = sb("a_yT_hi", [P, core.T], F32R)
    yT_lo = sb("a_yT_lo", [P, core.T], F32R)
    ident16 = sb("ident16", [P, P], BF16)
    mask = sb("a_mask", [P, 4, P], BF16)
    S_ps = [ps(f"a_S{i}") for i in range(2)]
    T_ps = ps("a_T")
    O_ps = ps("a_O")
    proj_ps = [ps(f"a_proj{i}") for i in range(2)]
    acc_ps = [ps(f"a_acc{i}") for i in range(2)]

    rows_loaded = core.sem("a_rows_loaded")
    consts = core.sem("a_consts")
    const_chain = core.sem("a_const_chain")
    v_done = core.sem("a_v_done")
    v_ready = core.sem("a_v_ready")
    q_done = core.sem("a_q_done")
    k_done = core.sem("a_k_done")
    q_ready = core.sem("a_q_ready")
    k_ready = core.sem("a_k_ready")
    scored = core.sem("a_scored")
    max_ready = core.sem("a_max_ready")
    exp_ready = core.sem("a_exp_ready")
    inv_ready = core.sem("a_inv_ready")
    prob_ready = core.sem("a_prob_ready")
    prob_turned = core.sem("a_prob_turned")
    probT_ready = core.sem("a_probT_ready")
    mixed = core.sem("a_mixed")
    oT_hi_ready = core.sem("a_oT_hi_ready")
    oT_lo_ready = core.sem("a_oT_lo_ready")
    projected = core.sem("a_projected")
    yT_hi_ready = core.sem("a_yT_hi_ready")
    yT_lo_ready = core.sem("a_yT_lo_ready")
    expanded = core.sem("a_expanded")
    residual = core.sem("a_residual")
    x_biased = core.sem("a_x_biased")

    def pair(j):
        return j // 2, j % 2

    def q_bank(c, h):
        return proj_ps[0]

    def k_bank(c, h):
        return proj_ps[1]

    LAG_T, LAG_O = 2, 3

    with nc.Block() as block:
        @block.sync
        def _(sp):
            for dst, a, n in ((bv_row, 0, 1024), (pb_row, 1024, HALF)):
                sp.dma_start(dst[:, :], d["bias_rows"][0:1, a:a + n].broadcast_to([P, n])).then_inc(rows_loaded, 16)
            load_ffn_weights(core, sp, d, ffn_raw_loaded)

        @block.gpsimd
        def _(pool):
            count = [0]

            def link(instruction):
                count[0] += 1
                instruction.then_inc(const_chain, 1)
                pool.wait_ge(const_chain, count[0])

            link(pool.tensor_copy(ident16[:, :], core.ident[:, :]))
            link(pool.memset(mask[:, :, :], 0.0))
            pool.affine_select(out=mask[:, :, :], in_=mask[:, :, :], compare_op=ALU.is_ge, fill=-1e9,
                               base=0, pattern=[[0, 4], [-1, P]], channel_multiplier=1).then_inc(consts, 1)
            for slot in range(2):
                pool.wait_ge(consts, 1 + 2 * slot)
                pool.memset(q_pad[64:128, slot, 0, :], 0.0).then_inc(consts, 1)
                pool.wait_ge(consts, 2 + 2 * slot)
                pool.memset(q_pad[0:64, slot, 1, :], 0.0).then_inc(consts, 1)
            pool.wait_ge(consts, 5)
            pool.wait_ge(rows_loaded, 32)
            for i in range(tiles):
                pool.tensor_tensor(core.x[:, i, :], core.x[:, i, :], pb_row[:, :], ALU.add).then_inc(x_biased, 1)
            for n in range(G):
                pool.wait_ge(inv_ready, n + 1)
                p = prob[:, n % 3, :].rearrange("p (j k) -> p j k", k=P)
                pool.tensor_tensor(p, p, bcast(row_inv[:, n, :], P), ALU.mult).then_inc(prob_ready, 1)

        @block.tensor
        def _(pe):
            for u in range(2 * tiles):
                i, c = u // 2, u % 2
                if u >= 4:
                    pe.wait_ge(v_ready, u - 3)
                bank = (*S_ps, T_ps, O_ps)[u % 4]
                cols = slice(c * HALF, (c + 1) * HALF)
                parts_matmul(pe, bank[:, :], (qkvT[0][:, 2, i * P:(i + 1) * P], qkvT[1][:, 2, i * P:(i + 1) * P]),
                             (wa["qkv_hi"][:, 2, cols], wa["qkv_lo"][:, 2, cols]), True, True).then_inc(v_done, 1)

            def project_qk(c, h):
                w, t = slice(c * P, (c + 1) * P), slice(h * HALF, (h + 1) * HALF)
                n = 2 * c + h
                if n >= 1:
                    pe.wait_ge(q_ready, 2 * n)
                parts_matmul(pe, q_bank(c, h)[:, :], (wa["qkv_hi"][:, 0, w], wa["qkv_lo"][:, 0, w]),
                             (qkvT[0][:, 0, t], qkvT[1][:, 0, t]), True, True).then_inc(q_done, 1)
                if n >= 1:
                    pe.wait_ge(k_ready, n)
                parts_matmul(pe, k_bank(c, h)[:, :], (wa["qkv_hi"][:, 1, w], wa["qkv_lo"][:, 1, w]),
                             (qkvT[0][:, 1, t], qkvT[1][:, 1, t]), True, True).then_inc(k_done, 1)

            def score(n):
                c, g = n // 4, n % 4
                bank = S_ps[n % 2]
                if n < 2:
                    pe.wait_ge(v_ready, 2 * tiles)
                    pe.wait_ge(consts, 5)
                else:
                    pe.wait_ge(exp_ready, n - 1)
                pe.wait_ge(q_ready, 2 * (2 * c + g // 2 + 1))
                pe.wait_ge(k_ready, 2 * c + g // 2 + 1)
                pe.matmul(bank[:, :], ident16[:, :], mask[:, :, :].rearrange("p j k -> p (j k)"),
                          start=True, stop=True, skip_group_check=True)
                for j in range(4):
                    b, head = pair(j)
                    t = slice((2 * g + b) * P, (2 * g + b + 1) * P)
                    last = pe.matmul(bank[:, j * P:(j + 1) * P], q_pad[:, c % 2, head, t], kT[:, c % 2, t],
                                     start=False, stop=True, skip_group_check=True)
                last.then_inc(scored, 1)

            def turn(n):
                pe.wait_ge(prob_ready, n + 1)
                if n >= 1:
                    pe.wait_ge(probT_ready, n)
                for j in range(4):
                    last = pe.transpose(T_ps[:, j * P:(j + 1) * P], prob[:, n % 3, j * P:(j + 1) * P], core.ident[:, :])
                last.then_inc(prob_turned, 1)

            def mix(n):
                c, g = n // 4, n % 4
                pe.wait_ge(probT_ready, n + 1)
                if n >= 1:
                    pe.wait_ge(oT_lo_ready, n)
                for j in range(4):
                    b, head = pair(j)
                    e = (2 * c + head) * 64
                    last = pe.matmul(O_ps[64 * head:64 * head + 64, b * P:(b + 1) * P], V[:, 2 * g + b, e:e + 64],
                                     probT[:, n % 2, j * P:(j + 1) * P], start=True, stop=True,
                                     skip_group_check=True)
                last.then_inc(mixed, 1)

            def project_out(c, h):
                pe.wait_ge(oT_lo_ready, 4 * c + 2 * h + 2)
                w = slice(c * P, (c + 1) * P)
                parts_matmul(pe, acc_ps[h][:, :], (wa["wo_hi"][:, w], wa["wo_lo"][:, w]),
                             (oT_hi[:, h, :], oT_lo[:, h, :]), start=(c == 0), stop=(c == CH - 1))\
                    .then_inc(projected, 1)

            project_qk(0, 0)
            project_qk(0, 1)
            for n in range(G + LAG_O + 1):
                if n < G:
                    score(n)
                if n % 4 in (2, 3) and n // 4 + 1 < CH:
                    project_qk(n // 4 + 1, n % 4 - 2)
                if LAG_T <= n < G + LAG_T:
                    turn(n - LAG_T)
                if LAG_O <= n < G + LAG_O:
                    mix(n - LAG_O)
                done = n - LAG_O - 1
                if done >= 0 and done % 2 == 1:
                    project_out(done // 4, done % 4 // 2)
            for i in range(tiles):
                pe.wait_ge(yT_lo_ready, i // 4 + 1)
                if i >= 4:
                    pe.wait_ge(residual, i - 3)
                t = slice(i * P, (i + 1) * P)
                bank = (*S_ps, *proj_ps)[i % 4]
                parts_matmul(pe, bank[:, :], (yT_hi[:, t], yT_lo[:, t]), (wa["pw_hi"], wa["pw_lo"]),
                             True, True).then_inc(expanded, 1)

        @block.scalar
        def _(act):
            def k_out(c, h):
                n = 2 * c + h
                act.wait_ge(k_done, n + 1)
                if c >= 2:
                    act.wait_ge(scored, 4 * (c - 1))
                act.activation(kT[:, c % 2, h * HALF:(h + 1) * HALF], k_bank(c, h)[:, :], ACT.Identity,
                               bias=core.bias_cols[:, 11 + c:12 + c]).then_inc(k_ready, 1)

            def exponent(n):
                act.wait_ge(max_ready, n + 1)
                if n >= 3:
                    act.wait_ge(prob_turned, n - 2)
                for j in range(4):
                    last = act.activation(prob[:, n % 3, j * P:(j + 1) * P], S_ps[n % 2][:, j * P:(j + 1) * P],
                                          ACT.Exp, bias=neg_max[:, n, j:j + 1], accum_out=row_sum[:, n, j:j + 1])
                last.then_inc(exp_ready, 1)

            def turned_out(n):
                act.wait_ge(prob_turned, n + 1)
                if n >= 2:
                    act.wait_ge(mixed, n - 1)
                act.copy(probT[:, n % 2, :], T_ps[:, :]).then_inc(probT_ready, 1)

            def mixed_out(n):
                c, g = n // 4, n % 4
                act.wait_ge(mixed, n + 1)
                if c >= 1:
                    act.wait_ge(projected, 2 * (c - 1) + g // 2 + 1)
                act.copy(oT_hi[:, g // 2, (g % 2) * 256:(g % 2) * 256 + 256], O_ps[:, 0:256]).then_inc(oT_hi_ready, 1)

            k_out(0, 0)
            k_out(0, 1)
            for n in range(G + LAG_O + 1):
                if n < G:
                    exponent(n)
                if n % 4 in (2, 3) and n // 4 + 1 < CH:
                    k_out(n // 4 + 1, n % 4 - 2)
                if LAG_T <= n < G + LAG_T:
                    turned_out(n - LAG_T)
                if LAG_O <= n < G + LAG_O:
                    mixed_out(n - LAG_O)
            for h in range(2):
                act.wait_ge(projected, 2 * (CH - 1) + h + 1)
                act.activation(yT_hi[:, h * HALF:(h + 1) * HALF], acc_ps[h][:, :], ACT.Identity,
                               bias=core.bias_cols[:, 19:20]).then_inc(yT_hi_ready, 1)

        @block.vector
        def _(dve):
            def q_out(c, h):
                n = 2 * c + h
                dve.wait_ge(q_done, n + 1)
                if c >= 2:
                    dve.wait_ge(scored, 4 * (c - 1))
                for head in range(2):
                    r = slice(64 * head, 64 * head + 64)
                    dve.tensor_scalar(q_pad[r, c % 2, head, h * HALF:(h + 1) * HALF], q_bank(c, h)[r, :],
                                      core.bias_cols[r, 3 + c:4 + c], 0.125, ALU.add, ALU.mult).then_inc(q_ready, 1)

            def maximum(n):
                dve.wait_ge(scored, n + 1)
                dve.tensor_reduce(neg_max[:, n, :], S_ps[n % 2][:, :].rearrange("p (j k) -> p j k", k=P),
                                  AX_X, ALU.max, negate=True).then_inc(max_ready, 1)

            def inverse(n):
                dve.wait_ge(exp_ready, n + 1)
                dve.reciprocal(row_inv[:, n, :], row_sum[:, n, :]).then_inc(inv_ready, 1)

            def mixed_lo(n):
                g = n % 4
                dve.wait_ge(oT_hi_ready, n + 1)
                cols = slice((g % 2) * 256, (g % 2) * 256 + 256)
                dve.tensor_tensor(oT_lo[:, g // 2, cols], O_ps[:, 0:256], oT_hi[:, g // 2, cols].bitcast(F32),
                                  ALU.subtract).then_inc(oT_lo_ready, 1)

            dve.wait_ge(rows_loaded, 32)
            for u in range(2 * tiles):
                i, c = u // 2, u % 2
                dve.wait_ge(v_done, u + 1)
                bank = (*S_ps, T_ps, O_ps)[u % 4]
                cols = slice(c * HALF, (c + 1) * HALF)
                dve.tensor_tensor(V[:, i, cols], bank[:, :], bv_row[:, cols], ALU.add).then_inc(v_ready, 1)
            q_out(0, 0)
            q_out(0, 1)
            for n in range(G + LAG_O + 1):
                if n < G:
                    maximum(n)
                if n % 4 in (2, 3) and n // 4 + 1 < CH:
                    q_out(n // 4 + 1, n % 4 - 2)
                if n < G:
                    inverse(n)
                if LAG_O <= n < G + LAG_O:
                    mixed_lo(n - LAG_O)
            for h in range(2):
                t = slice(h * HALF, (h + 1) * HALF)
                dve.wait_ge(yT_hi_ready, h + 1)
                dve.scalar_tensor_tensor(out=yT_lo[:, t], in0=acc_ps[h][:, :], scalar=core.bias_cols[:, 19:20],
                                         in1=yT_hi[:, t].bitcast(F32), op0=ALU.add, op1=ALU.subtract)\
                   .then_inc(yT_lo_ready, 1)
            dve.wait_ge(x_biased, tiles)
            for i in range(tiles):
                dve.wait_ge(expanded, i + 1)
                bank = (*S_ps, *proj_ps)[i % 4]
                dve.tensor_tensor(core.x[:, i, :], bank[:, :], core.x[:, i, :], ALU.add).then_inc(residual, 1)
            dve.wait_ge(residual, tiles)


RAW_WR, RAW_A, RAW_B = 0, 256, 4352


def load_ffn_weights(core, sp, d, loaded, pieces=(0, 1, 2)):
    places = ((RAW_WR, "WrT", 64), (RAW_A, "AT", 1024), (RAW_B, "Bm", 512))
    for s in pieces:
        at, name, n = places[s]
        chunks = d[name].shape[0] // P
        sp.dma_start(core.raw[:, at:at + chunks * n].rearrange("p (k n) -> p k n", n=n),
                     d[name].rearrange("(k p) n -> p k n", p=P)).then_inc(loaded[s], 16)


def phase_ffn(core, scope, name, loaded, after_split=None, store=None):
    nc, tiles, dk = core.nc, core.tiles, core.dk
    sb = lambda what, shape, dt: scope.enter_context(nc.sbuf_tensor(f"{name}_{what}", shape, dt))
    ps = lambda what: scope.enter_context(nc.psum_tensor(f"{name}_{what}", [P, HALF], F32))
    sem = lambda what: core.sem(f"{name}_{what}")
    K, C = 64, 8
    UNITS = 2 * C
    AHEAD = 4
    wr_hi, wr_lo = (sb(f"wr_{s}", [P, dk, 2 * K], F32R) for s in ("hi", "lo"))
    a_hi, a_lo = (sb(f"a_{s}", [P, dk, C * P], F32R) for s in ("hi", "lo"))
    b_hi, b_lo = (sb(f"b_{s}", [P, C, HALF], F32R) for s in ("hi", "lo"))
    spread_f = sb("spread_f", [P, C, P], F32)
    spread = sb("spread", [P, C, P], F32R)
    scoreT = sb("scoreT", [K, HALF], F32)
    score = sb("score", [P, 4, K], F32)
    rest = sb("rest", [P, 4, K], F32)
    top = sb("top", [P, 4, 16], F32)
    gate = sb("gate", [P, 4, K], F32)
    chosen = sb("chosen", [P, 4, K], F32)
    total = sb("total", [P, 8], F32)
    gate2 = sb("gate2", [P, 4, 2, K], F32)
    gateT = sb("gateT", [P, 2, HALF], F32R)
    h_sb = sb("h_sb", [P, AHEAD + 1, HALF], F32)
    hg = sb("hg", [P, 2, HALF], F32)
    hg_hi = sb("hg_hi", [P, 2, HALF], F32R)
    hg_lo = sb("hg_lo", [P, 2, HALF], F32R)
    acc = [ps(f"acc{i}") for i in range(4)]
    up_ps = [ps(f"up{i}") for i in range(2)]
    spread_ps = ps("spread_ps")
    aux = ps("aux")
    ln = LayerNorm(core, scope, name, 0, acc)

    w_hi, w_lo = sem("w_hi"), sem("w_lo")
    spread_chain, spread_built, spread_ready = sem("spread_chain"), sem("spread_built"), sem("spread_ready")
    routed, scoreT_ready, score_turned = sem("routed"), sem("scoreT_ready"), sem("score_turned")
    shifted, expd, gate_ready, gate_turned = sem("shifted"), sem("expd"), sem("gate_ready"), sem("gate_turned")
    gateT_hi_ready, gateT_ready = sem("gateT_hi"), sem("gateT_ready")
    up_done, h_ready, spread_done = sem("up_done"), sem("h_ready"), sem("spread_done")
    hg_ready, hg_hi_ready, hg_lo_ready = sem("hg_ready"), sem("hg_hi_ready"), sem("hg_lo_ready")
    down_done, residual, chain_sem = sem("down_done"), sem("residual"), sem("chain")

    wr_raw = core.raw[:, RAW_WR:RAW_A].rearrange("p (k n) -> p k n", k=dk)
    a_raw = core.raw[:, RAW_A:RAW_B].rearrange("p (k n) -> p k n", k=dk)
    b_raw = core.raw[:, RAW_B:RAW_B + 4096].rearrange("p (c n) -> p c n", c=C)
    pieces = [(wr_raw, wr_hi[:, :, 0:K], wr_lo[:, :, 0:K], 0), (wr_raw, wr_hi[:, :, K:], wr_lo[:, :, K:], 0)]
    for c in range(C):
        cols = slice(c * P, (c + 1) * P)
        pieces.append((a_raw[:, :, cols], a_hi[:, :, cols], a_lo[:, :, cols], 1))
        pieces.append((b_raw[:, c, :], b_hi[:, c, :], b_lo[:, c, :], 2))
    A_AT = lambda c: 2 + 2 * c + 1
    B_AT = lambda c: 2 + 2 * c + 2

    with nc.Block() as block:
        @block.sync
        def _(sp):
            if after_split is not None:
                sp.wait_ge(w_lo, len(pieces))
                after_split(sp)
            if store is not None:
                stored, out = store
                for i in range(tiles):
                    sp.wait_ge(residual, i + 1)
                    sp.dma_start(out[i], core.x[:, i, :]).then_inc(stored, 16)
                sp.wait_ge(stored, 16 * tiles)

        @block.gpsimd
        def _(pool):
            def split_lo(n):
                raw, hi, lo, _ = pieces[n]
                pool.wait_ge(w_hi, n + 1)
                pool.tensor_tensor(lo, raw, hi.bitcast(F32), ALU.subtract).then_inc(w_lo, 1)

            for n in range(3):
                split_lo(n)
            pool.memset(spread_f[:, :, :], 0.0).then_inc(spread_chain, 1)
            for r in range(2):
                pool.wait_ge(spread_chain, r + 1)
                v = spread_f[:, :, :].rearrange("p c (k r) -> p c k r", r=16)
                pool.affine_select(out=v, in_=v, compare_op=ALU.not_equal, fill=1.0, base=-K * r,
                                   pattern=[[-8, C], [-1, 8], [0, 16]], channel_multiplier=1)\
                    .then_inc(spread_chain if r == 0 else spread_built, 1)
            for n in range(3, len(pieces)):
                split_lo(n)

        @block.vector
        def _(dve):
            chain = Chain(dve, chain_sem)

            def split_hi(n):
                raw, hi, lo, load = pieces[n]
                dve.wait_ge(loaded[load], 16)
                dve.tensor_copy(hi, raw).then_inc(w_hi, 1)

            def top16(half):
                dve.wait_ge(score_turned, half + 1)
                chain.link(dve.tensor_copy(score[:, :, :], aux[:, 0:4 * K].rearrange("p (i k) -> p i k", k=K)))
                for i in range(4):
                    last = dve.max(top[:, i, 0:8], score[:, i, :])
                chain.link(last)
                for i in range(4):
                    last = dve.match_replace(out=rest[:, i, :], in_to_replace=top[:, i, 0:8],
                                             in_values=score[:, i, :], imm_value=-3e38)
                chain.link(last)
                for i in range(4):
                    last = dve.max(top[:, i, 8:16], rest[:, i, :])
                chain.link(last)
                for i in range(4):
                    last = dve.match_replace(out=rest[:, i, :], in_to_replace=top[:, i, 8:16],
                                             in_values=rest[:, i, :], imm_value=-3e38)
                chain.link(last)
                dve.tensor_tensor(gate[:, :, :], score[:, :, :], bcast(top[:, :, 0], K), ALU.subtract)\
                   .then_inc(shifted, 1)
                chain.link(dve.tensor_tensor(chosen[:, :, :], rest[:, :, :], score[:, :, :], ALU.not_equal))
                dve.wait_ge(expd, half + 1)
                chain.link(dve.tensor_tensor(gate[:, :, :], gate[:, :, :], chosen[:, :, :], ALU.mult))
                chain.link(dve.tensor_reduce(total[:, 0:4], gate[:, :, :], AX_X, ALU.add))
                chain.link(dve.reciprocal(total[:, 4:8], total[:, 0:4]))
                for r in range(2):
                    dve.scalar_tensor_tensor(out=gate2[:, :, r, :], in0=gate[:, :, :], scalar=2.0,
                                             in1=bcast(total[:, 4:8], K), op0=ALU.mult, op1=ALU.mult)\
                       .then_inc(gate_ready, 1)

            def gateT_lo(half):
                dve.wait_ge(gateT_hi_ready, half + 1)
                g = gateT[K:2 * K, half, :]
                dve.tensor_tensor(g, aux[K:2 * K, :], g.bitcast(F32), ALU.subtract).then_inc(gateT_ready, 1)

            def scale(u):
                dve.wait_ge(h_ready, u + 1)
                dve.wait_ge(spread_done, u + 1)
                if u >= 2:
                    dve.wait_ge(hg_hi_ready, u - 1)
                dve.tensor_tensor(hg[:, u % 2, :], spread_ps[:, :], h_sb[:, u % (AHEAD + 1), :], ALU.mult).then_inc(hg_ready, 1)

            def scale_lo(u):
                dve.wait_ge(hg_hi_ready, u + 1)
                dve.tensor_tensor(hg_lo[:, u % 2, :], hg[:, u % 2, :], hg_hi[:, u % 2, :].bitcast(F32),
                                  ALU.subtract).then_inc(hg_lo_ready, 1)

            for n in range(3):
                split_hi(n)
            ln.vector_all(dve, chain, lambda: [split_hi(n) for n in range(3, 2 + 2 * AHEAD)])
            dve.wait_ge(spread_built, 1)
            dve.tensor_copy(spread[:, :, :], spread_f[:, :, :]).then_inc(spread_ready, 1)
            top16(0)
            gateT_lo(0)
            for u in range(UNITS):
                for n in range(2 + 2 * (u + AHEAD), min(4 + 2 * (u + AHEAD), len(pieces))):
                    split_hi(n)
                scale(u)
                scale_lo(u)
                if u == 3:
                    top16(1)
                    gateT_lo(1)
                if u % C == C - 1:
                    half = u // C
                    dve.wait_ge(down_done, u + 1)
                    for i in range(4 * half, 4 * half + 4):
                        dve.tensor_tensor(core.x[:, i, :], acc[i % 4][:, :], core.x[:, i, :], ALU.add)\
                           .then_inc(residual, 1)
            dve.wait_ge(residual, tiles)

        @block.scalar
        def _(act):
            def scoreT_out(half):
                act.wait_ge(routed, half + 1)
                if half:
                    act.wait_ge(score_turned, half)
                act.copy(scoreT[:, :], aux[0:K, :]).then_inc(scoreT_ready, 1)

            def exponent(half):
                act.wait_ge(shifted, half + 1)
                act.activation(gate[:, :, :], gate[:, :, :], ACT.Exp).then_inc(expd, 1)

            def gateT_hi(half):
                act.wait_ge(gate_turned, half + 1)
                act.copy(gateT[:, half, :], aux[:, :]).then_inc(gateT_hi_ready, 1)

            def h_out(u):
                act.wait_ge(up_done, u + 1)
                if u > AHEAD:
                    act.wait_ge(hg_ready, u - AHEAD)
                act.copy(h_sb[:, u % (AHEAD + 1), :], up_ps[u % 2][:, :]).then_inc(h_ready, 1)

            def hg_high(u):
                act.wait_ge(hg_ready, u + 1)
                if u >= 2:
                    act.wait_ge(down_done, u - 1)
                act.copy(hg_hi[:, u % 2, :], hg[:, u % 2, :]).then_inc(hg_hi_ready, 1)

            ln.scalar_std(act, range(0, 4))
            for i in range(0, 4):
                ln.scalar_hi(act, i)
            ln.scalar_std(act, range(4, 8))
            scoreT_out(0)
            h_out(0)
            for i in range(4, 8):
                ln.scalar_hi(act, i)
            for u in range(1, AHEAD):
                h_out(u)
            exponent(0)
            gateT_hi(0)
            for u in range(UNITS):
                hg_high(u)
                if u + AHEAD < UNITS:
                    h_out(u + AHEAD)
                if u == 2:
                    scoreT_out(1)
                if u == 3:
                    exponent(1)
                    gateT_hi(1)

        @block.tensor
        def _(pe):
            def route(half):
                pe.wait_ge(ln.lo_ready, 4 * half + 4)
                pe.wait_ge(w_lo, 2)
                if half:
                    pe.wait_ge(gateT_ready, half)
                for k in range(dk):
                    last = parts_matmul(pe, aux[:, :], (wr_hi[:, k, :], wr_lo[:, k, :]),
                                        ln.columns(k, half * HALF, HALF), start=(k == 0), stop=(k == dk - 1))
                last.then_inc(routed, 1)

            def turn_scores(half):
                pe.wait_ge(scoreT_ready, half + 1)
                for i in range(4):
                    last = pe.transpose(aux[:, i * K:(i + 1) * K], scoreT[:, i * P:(i + 1) * P], core.ident[0:K, 0:K])
                last.then_inc(score_turned, 1)

            def turn_gates(half):
                pe.wait_ge(gate_ready, 2 * half + 2)
                for i in range(4):
                    last = pe.transpose(aux[:, i * P:(i + 1) * P],
                                        gate2[:, i, :, :].rearrange("p r k -> p (r k)"), core.ident[:, :])
                last.then_inc(gate_turned, 1)

            def up(u):
                half, c = u // C, u % C
                pe.wait_ge(ln.lo_ready, 4 * half + 4)
                if half == 0:
                    pe.wait_ge(w_lo, A_AT(c))
                if u >= 2:
                    pe.wait_ge(h_ready, u - 1)
                cols = slice(c * P, (c + 1) * P)
                for k in range(dk):
                    last = parts_matmul(pe, up_ps[u % 2][:, :], (a_hi[:, k, cols], a_lo[:, k, cols]),
                                        ln.columns(k, half * HALF, HALF), start=(k == 0), stop=(k == dk - 1))
                last.then_inc(up_done, 1)

            def spread_gates(u):
                half, c = u // C, u % C
                pe.wait_ge(gateT_ready, half + 1)
                if u >= 1:
                    pe.wait_ge(hg_ready, u)
                pe.matmul(spread_ps[:, :], spread[:, c, :], gateT[:, half, :], start=True, stop=True)\
                  .then_inc(spread_done, 1)

            def down(u):
                half, c = u // C, u % C
                pe.wait_ge(hg_lo_ready, u + 1)
                if half == 0:
                    pe.wait_ge(w_lo, B_AT(c))
                for i in range(4):
                    t = slice(i * P, (i + 1) * P)
                    if c == 0 and half:
                        pe.wait_ge(residual, i + 1)
                    last = parts_matmul(pe, acc[i][:, :], (hg_hi[:, u % 2, t], hg_lo[:, u % 2, t]),
                                        (b_hi[:, c, :], b_lo[:, c, :]), start=(c == 0), stop=(c == C - 1))
                last.then_inc(down_done, 1)

            for i in range(4):
                ln.tensor_turn(pe, i)
            route(0)
            up(0)
            turn_scores(0)
            for i in range(4, 8):
                ln.tensor_turn(pe, i)
            for u in range(1, AHEAD):
                up(u)
            turn_gates(0)
            pe.wait_ge(spread_ready, 1)
            pe.wait_ge(ln.lo_ready, tiles)
            for u in range(UNITS):
                spread_gates(u)
                if u + AHEAD < UNITS:
                    up(u + AHEAD)
                down(u)
                if u == 1:
                    route(1)
                if u == 2:
                    turn_scores(1)
                if u == 3:
                    turn_gates(1)


RAW_Q, RAW_K, RAW_V, RAW_O = 0, 2048, 2560, 6400
HEADS, GROUPS, DH = 32, 8, 16
PER = HEADS // GROUPS
OPERAND = 96


def load_gqa_weights(core, sp, d, loaded):
    for s, (at, name, n) in enumerate(((RAW_K, "kwT", 128), (RAW_V, "vwT", 128), (RAW_Q, "qwT", 512),
                                       (RAW_O, "owT", 512))):
        sp.dma_start(core.raw[:, at:at + core.dk * n].rearrange("p (k n) -> p k n", n=n),
                     d[name].rearrange("(k p) n -> p k n", p=P)).then_inc(loaded[s], 16)


def phase_gqa_projections(core, scope, b, loaded):
    nc, tiles, dk = core.nc, core.tiles, core.dk
    sb = lambda what, shape, dt: scope.enter_context(nc.sbuf_tensor(f"p_{what}", shape, dt))
    ps = lambda what: scope.enter_context(nc.psum_tensor(f"p_{what}", [P, HALF], F32))
    w_hi, w_lo = (sb(f"w_{s}", [P, 6, dk, P], F32R) for s in ("hi", "lo"))
    kT_hi, kT_lo = (sb(f"kT_{s}", [P, core.T], F32R) for s in ("hi", "lo"))
    vT = sb("vT", [P, core.T], F32)
    turn_ps = [ps(f"turn{i}") for i in range(4)]
    out_ps = [ps(f"out{i}") for i in range(3)]
    v_ps = ps("v")
    ln = LayerNorm(core, scope, "p", 0, turn_ps)
    sem = lambda what: core.sem(f"p_{what}")
    w_hi_ready, w_lo_ready, projected = sem("w_hi"), sem("w_lo"), sem("projected")
    hi_ready, lo_ready, v_turned, v_ready = sem("hi_ready"), sem("lo_ready"), sem("v_turned"), sem("v_ready")
    zeroed, chain_sem = sem("zeroed"), sem("chain")
    b["consts_ready"] = sem("consts_ready")
    b["k_loaded"] = sem("k_loaded")
    raw = lambda at, n: core.raw[:, at:at + dk * n].rearrange("p (k n) -> p k n", n=n)
    pieces = [(raw(RAW_K, P), 0), (raw(RAW_V, P), 1)]
    pieces += [(raw(RAW_Q, 512)[:, :, m * P:(m + 1) * P], 2) for m in range(4)]
    units = [(w, h) for w in range(6) for h in range(2)]
    bias = lambda w: core.bias_cols[:, (24, 25, 20, 21, 22, 23)[w]:(24, 25, 20, 21, 22, 23)[w] + 1]

    def target(w, h, part):
        t = slice(h * HALF, (h + 1) * HALF)
        return (kT_hi, kT_lo)[part][:, t] if w == 0 else b["qT"][part][:, w - 2, t]

    with nc.Block() as block:
        @block.sync
        def _(sp):
            sp.wait_ge(lo_ready, 2)
            for g in range(GROUPS):
                for r in range(4):
                    src = (kT_hi, kT_lo)[r % 2][DH * g:DH * (g + 1), :].bitcast(F32)
                    sp.dma_start(b["k_op"][DH * r:DH * (r + 1), g, :].bitcast(F32), src).then_inc(b["k_loaded"], 16)
            sp.wait_ge(b["k_loaded"], 16 * 4 * GROUPS)

        @block.gpsimd
        def _(pool):
            for n, (piece, _) in enumerate(pieces):
                pool.wait_ge(w_hi_ready, n + 1)
                pool.tensor_tensor(w_lo[:, n, :, :], piece, w_hi[:, n, :, :].bitcast(F32), ALU.subtract)\
                    .then_inc(w_lo_ready, 1)
                if n == 1:
                    pool.memset(b["v"][:, :, :, :], 0.0).then_inc(zeroed, 1)
            pool.wait_ge(zeroed, 1)
            pool.memset(b["v"][:, :, :, DH:DH + 1], 1.0).then_inc(b["consts_ready"], 1)
            pool.wait_ge(b["consts_ready"], 1)
            pool.memset(b["k_op"][64:OPERAND, :, :].bitcast(F32), 0.0).then_inc(zeroed, 1)
            pool.wait_ge(zeroed, 2)
            pool.memset(b["k_op"][64:66, :, :].bitcast(F32), 1.0).then_inc(b["consts_ready"], 1)
            pool.wait_ge(b["consts_ready"], 2)

        @block.vector
        def _(dve):
            chain = Chain(dve, chain_sem)

            def split_hi(n):
                piece, load = pieces[n]
                dve.wait_ge(loaded[load], 16)
                dve.tensor_copy(w_hi[:, n, :, :], piece).then_inc(w_hi_ready, 1)

            split_hi(0)
            split_hi(1)
            ln.vector_all(dve, chain, lambda: [split_hi(n) for n in range(2, 6)])
            dve.wait_ge(b["consts_ready"], 1)
            n = 0
            for u, (w, h) in enumerate(units):
                if w == 1:
                    dve.wait_ge(v_turned, h + 1)
                    dve.tensor_copy(b["v"][:, 4 * h:4 * h + 4, :, 0:DH],
                                    v_ps[:, :].rearrange("p (i g e) -> p i g e", i=4, g=GROUPS)).then_inc(v_ready, 1)
                    continue
                dve.wait_ge(hi_ready, u + 1)
                dve.scalar_tensor_tensor(out=target(w, h, 1), in0=out_ps[u % 3][:, :], scalar=bias(w),
                                         in1=target(w, h, 0).bitcast(F32), op0=ALU.add, op1=ALU.subtract)\
                   .then_inc(lo_ready, 1)
                n += 1
            dve.wait_ge(lo_ready, n)
            dve.wait_ge(v_ready, 2)

        @block.scalar
        def _(act):
            ln.scalar_std(act, range(0, 4))
            for i in range(4):
                ln.scalar_hi(act, i)
            ln.scalar_std(act, range(4, 8))
            for i in range(4, 8):
                ln.scalar_hi(act, i)
            for u, (w, h) in enumerate(units):
                act.wait_ge(projected, u + 1)
                out = vT[:, h * HALF:(h + 1) * HALF] if w == 1 else target(w, h, 0)
                act.activation(out, out_ps[u % 3][:, :], ACT.Identity, bias=bias(w)).then_inc(hi_ready, 1)

        @block.tensor
        def _(pe):
            def turn_v(h):
                pe.wait_ge(hi_ready, 2 + h + 1)
                if h:
                    pe.wait_ge(v_ready, h)
                for i in range(4):
                    t = slice((4 * h + i) * P, (4 * h + i + 1) * P)
                    last = pe.transpose(v_ps[:, i * P:(i + 1) * P], vT[:, t], core.ident[:, :])
                last.then_inc(v_turned, 1)

            for i in range(4):
                ln.tensor_turn(pe, i)
            pe.wait_ge(w_lo_ready, 2)
            for u, (w, h) in enumerate(units):
                if u == 1:
                    for i in range(4, 8):
                        ln.tensor_turn(pe, i)
                pe.wait_ge(ln.lo_ready, 4 * h + 4)
                pe.wait_ge(w_lo_ready, w + 1)
                if u >= 3:
                    before = units[u - 3][0]
                    if before == 1:
                        pe.wait_ge(hi_ready, u - 2)
                    else:
                        pe.wait_ge(lo_ready, u - 2 - (2 if before > 1 else 0))
                for k in range(dk):
                    last = parts_matmul(pe, out_ps[u % 3][:, :], (w_hi[:, w, k, :], w_lo[:, w, k, :]),
                                        ln.columns(k, h * HALF, HALF), start=(k == 0), stop=(k == dk - 1))
                last.then_inc(projected, 1)
                if u in (4, 5):
                    turn_v(u - 4)


def phase_gqa_core(core, scope, b, d, ffn_loaded, ob_row):
    nc, tiles = core.nc, core.tiles
    sb = lambda what, shape, dt: scope.enter_context(nc.sbuf_tensor(f"g_{what}", shape, dt))
    sem = lambda what: core.sem(f"g_{what}")
    STAGES, UNITS = 2 * GROUPS, tiles
    SCALE = 0.25 * LN2
    q_op = sb("q_op", [OPERAND, 2, 2, PER, HALF], F32R)
    prob = sb("prob", [P, 2, PER, HALF], F32)
    neg_max = sb("neg_max", [P, 2, 16], F32)
    maxT_hi, maxT_lo = (sb(f"maxT_{s}", [16, 2, P], F32R) for s in ("hi", "lo"))
    mixT = sb("mixT", [P, HALF], F32)
    den_inv = sb("den_inv", [P, 16], F32)
    S_ps = [scope.enter_context(nc.psum_tensor(f"g_S{i}", [P, 2 * HALF], F32)) for i in range(2)]
    E_ps = [scope.enter_context(nc.psum_tensor(f"g_E{i}", [P, HALF], F32)) for i in range(2)]
    mix_ps = scope.enter_context(nc.psum_tensor("g_mix", [P, HALF], F32))
    turn_ps = scope.enter_context(nc.psum_tensor("g_turn", [P, HALF], F32))
    q_loaded = [sem(f"q_loaded{s}") for s in range(2)]
    m_loaded = [sem(f"m_loaded{s}") for s in range(2)]
    rows_zeroed, scored, max_ready = sem("rows_zeroed"), sem("scored"), sem("max_ready")
    max_turned, maxT_ready, maxT_hi_ready = sem("max_turned"), sem("maxT_ready"), sem("maxT_hi_ready")
    keyed, exp_ready, mixed, mixT_ready = sem("keyed"), sem("exp_ready"), sem("mixed"), sem("mixT_ready")
    mix_turned, inv_ready, o_ready = sem("mix_turned"), sem("inv_ready"), sem("o_ready")
    ob_loaded, x_biased = sem("ob_loaded"), sem("x_biased")
    LEAD = UNITS + 2
    SLOTS = STAGES * UNITS + LEAD + 1
    turns_maxima = lambda s: s // UNITS - 1 if s % UNITS == 0 and 1 <= s // UNITS <= STAGES else -1
    turns_mix = lambda s: (s - LEAD - 2) // UNITS - 1 if (s - LEAD - 2) % UNITS == 0 else -1

    with nc.Block() as block:
        @block.sync
        def _(sp):
            def load_queries(g):
                slot = g % 2
                if g >= 2:
                    sp.wait_ge(keyed, PER * UNITS * 2 * (g - 1))
                for j in range(PER):
                    head = PER * g + j
                    rows = slice(DH * (head % 8), DH * (head % 8) + DH)
                    for r in range(4):
                        src = b["qT"][r // 2][rows, head // 8, :].bitcast(F32).rearrange("d (h t) -> d h t", h=2)
                        sp.dma_start(q_op[DH * r:DH * (r + 1), slot, :, j, :].bitcast(F32), src)\
                          .then_inc(q_loaded[slot], 16)
                if g >= 2:
                    sp.dma_start(q_op[64:66, slot].bitcast(F32), q_op[66:68, slot].bitcast(F32))\
                      .then_inc(q_loaded[slot], 16)

            def load_maxima(n):
                slot, half = n // 2 % 2, n % 2
                sp.wait_ge(maxT_ready, n + 1)
                for r, part in enumerate((maxT_hi, maxT_lo)):
                    sp.dma_start(q_op[64 + r:65 + r, slot, half, :, :].bitcast(F32).rearrange("p j t -> p (j t)"),
                                 part[:, n % 2, :].bitcast(F32)).then_inc(m_loaded[n % 2], 16)

            load_queries(0)
            sp.dma_start(ob_row[:, :], d["bias_rows"][0:1, 1536:2048].broadcast_to([P, HALF])).then_inc(ob_loaded, 16)
            load_queries(1)
            load_ffn_weights(core, sp, d, ffn_loaded, pieces=(0, 1))
            for n in range(STAGES):
                load_maxima(n)
                if n % 2 == 0 and 2 <= n // 2 + 1 < GROUPS:
                    load_queries(n // 2 + 1)

        @block.gpsimd
        def _(pool):
            pool.memset(q_op[64:OPERAND].bitcast(F32), 0.0).then_inc(rows_zeroed, 1)
            pool.wait_ge(rows_zeroed, 1)
            pool.wait_ge(ob_loaded, 16)
            for i in range(tiles):
                pool.tensor_tensor(core.x[:, i, :], core.x[:, i, :], ob_row[:, :], ALU.add).then_inc(x_biased, 1)
            pool.wait_ge(x_biased, tiles)

        @block.tensor
        def _(pe):
            def score(s, h):
                n, t = s // 16, s % 16
                g, half, i, j = n // 2, n % 2, t // PER, t % PER
                if t == 0 and h == 0:
                    slot_loads = [16 * (16 + (1 if k >= 2 else 0)) for k in range(GROUPS)]
                    pe.wait_ge(q_loaded[g % 2], sum(slot_loads[g % 2:g + 1:2]))
                if s == 0 and h == 0:
                    pe.wait_ge(rows_zeroed, 1)
                if s >= 2 and h == 0:
                    pe.wait_ge(max_ready, s - 1)
                product = pe.matmul(S_ps[s % 2][:, h * HALF:(h + 1) * HALF],
                                    q_op[:, g % 2, half, j, i * P:(i + 1) * P],
                                    b["k_op"][:, g, h * HALF:(h + 1) * HALF], start=True, stop=True)
                if h == 1:
                    product.then_inc(scored, 1)

            def key_scores(n, u, j):
                g, half = n // 2, n % 2
                e = PER * (UNITS * n + u) + j
                if u == 0 and j == 0:
                    pe.wait_ge(m_loaded[n % 2], 32 * (n // 2 + 1))
                if e >= 2:
                    pe.wait_ge(exp_ready, e - 1)
                pe.matmul(E_ps[e % 2][:, :], b["k_op"][:, g, u * P:(u + 1) * P], q_op[:, g % 2, half, j, :],
                          start=True, stop=True).then_inc(keyed, 1)

            def mix(k):
                n, u = k // UNITS, k % UNITS
                pe.wait_ge(exp_ready, PER * (k + 1))
                if u == 0 and n >= 1:
                    pe.wait_ge(mixT_ready, n)
                for j in range(PER):
                    last = pe.matmul(mix_ps[32 * j:32 * j + 32, :], b["v"][:, u, n // 2, :], prob[:, k % 2, j, :],
                                     start=(u == 0), stop=(u == UNITS - 1), skip_group_check=True)
                last.then_inc(mixed, 1)

            def turn_maxima(n):
                pe.wait_ge(max_ready, 16 * (n + 1))
                if n >= 2:
                    pe.wait_ge(o_ready, n - 1)
                pe.transpose(turn_ps[0:16, 0:P], neg_max[:, n % 2, :], core.ident[:, :]).then_inc(max_turned, 1)

            def turn_mix(n):
                pe.wait_ge(mixT_ready, n + 1)
                pe.wait_ge(maxT_ready, min(n + 2, STAGES))
                if n >= 1:
                    pe.wait_ge(o_ready, n)
                for i in range(4):
                    last = pe.transpose(turn_ps[:, i * P:(i + 1) * P], mixT[:, i * P:(i + 1) * P], core.ident[:, :])
                last.then_inc(mix_turned, 1)

            for s in range(SLOTS):
                k = s - LEAD
                keys = 0 <= k < STAGES * UNITS
                queries = s < STAGES * UNITS
                if keys:
                    key_scores(k // UNITS, k % UNITS, 0)
                if queries:
                    score(2 * s, 0)
                    score(2 * s, 1)
                if keys:
                    key_scores(k // UNITS, k % UNITS, 1)
                if queries:
                    score(2 * s + 1, 0)
                    score(2 * s + 1, 1)
                if keys:
                    key_scores(k // UNITS, k % UNITS, 2)
                if k >= 1:
                    mix(k - 1)
                if turns_maxima(s) >= 0:
                    turn_maxima(turns_maxima(s))
                if turns_mix(s) >= 0:
                    turn_mix(turns_mix(s))
                if keys:
                    key_scores(k // UNITS, k % UNITS, 3)
            turn_mix(STAGES - 1)

        @block.scalar
        def _(act):
            for n in range(STAGES):
                for u in range(UNITS):
                    for j in range(PER):
                        k = UNITS * n + u
                        e = PER * k + j
                        act.wait_ge(keyed, e + 1)
                        if k >= 2 and j == 0:
                            act.wait_ge(mixed, k - 1)
                        act.activation(prob[:, k % 2, j, :], E_ps[e % 2][:, :], ACT.Exp, scale=SCALE)\
                           .then_inc(exp_ready, 1)
                    if u == 0 and n >= 1:
                        act.wait_ge(mixed, UNITS * n)
                        if n >= 2:
                            act.wait_ge(mix_turned, n - 1)
                        act.copy(mixT[:, :], mix_ps[:, :]).then_inc(mixT_ready, 1)
            act.wait_ge(mixed, UNITS * STAGES)
            act.wait_ge(mix_turned, STAGES - 1)
            act.copy(mixT[:, :], mix_ps[:, :]).then_inc(mixT_ready, 1)

        @block.vector
        def _(dve):
            def maximum(n, t):
                i, j = t // PER, t % PER
                s = 16 * n + t
                dve.wait_ge(scored, s + 1)
                if t == 0 and n >= 2:
                    dve.wait_ge(max_turned, n - 1)
                dve.tensor_reduce(neg_max[:, n % 2, 4 * j + i:4 * j + i + 1], S_ps[s % 2][:, :], AX_X, ALU.max,
                                  negate=True).then_inc(max_ready, 1)

            def maxima_out(n):
                dve.wait_ge(max_turned, n + 1)
                if n >= 2:
                    dve.wait_ge(m_loaded[n % 2], 32 * (n // 2))
                hi, lo = maxT_hi[:, n % 2, :], maxT_lo[:, n % 2, :]
                dve.tensor_copy(hi, turn_ps[0:16, 0:P]).then_inc(maxT_hi_ready, 1)
                dve.wait_ge(maxT_hi_ready, n + 1)
                dve.tensor_tensor(lo, turn_ps[0:16, 0:P], hi.bitcast(F32), ALU.subtract).then_inc(maxT_ready, 1)

            def normalise(n):
                g, half = n // 2, n % 2
                dve.wait_ge(mix_turned, n + 1)
                v = turn_ps[:, :].rearrange("p (i j e) -> p i j e", i=4, e=32)
                dve.reciprocal(den_inv[:, :], turn_ps[:, :].rearrange("p (a e) -> p a e", e=32)[:, :, DH])\
                   .then_inc(inv_ready, 1)
                dve.wait_ge(inv_ready, n + 1)
                out = b["o"][:, 4 * half:4 * half + 4, PER * DH * g:PER * DH * (g + 1)]
                inv = den_inv[:, :].rearrange("p (i j) -> p i j", j=PER)
                for i in range(4):
                    last = dve.tensor_tensor(out[:, i, :].rearrange("p (j e) -> p j e", e=DH), v[:, i, :, 0:DH],
                                             bcast(inv[:, i, :], DH), ALU.mult)
                last.then_inc(o_ready, 1)

            for s in range(SLOTS):
                if s < STAGES * UNITS:
                    for j in range(2):
                        maximum(s // UNITS, 2 * (s % UNITS) + j)
                if turns_maxima(s) >= 0:
                    maxima_out(turns_maxima(s))
                if turns_mix(s) >= 0:
                    normalise(turns_mix(s))
            normalise(STAGES - 1)
            dve.wait_ge(o_ready, STAGES)


def phase_gqa_output(core, scope, o, d, loaded, ffn_loaded):
    nc, tiles, dk = core.nc, core.tiles, core.dk
    sb = lambda what, shape, dt: scope.enter_context(nc.sbuf_tensor(f"o_{what}", shape, dt))
    ps = lambda what: scope.enter_context(nc.psum_tensor(f"o_{what}", [P, HALF], F32))
    sem = lambda what: core.sem(f"o_{what}")
    w_hi, w_lo = (sb(f"w_{s}", [P, dk, HALF], F32R) for s in ("hi", "lo"))
    oT_hi, oT_lo = (sb(f"oT_{s}", [P, dk, core.T], F32R) for s in ("hi", "lo"))
    turn_ps = [ps(f"turn{i}") for i in range(4)]
    out_ps = [ps(f"out{i}") for i in range(4)]
    w_hi_ready, w_lo_ready, turned = sem("w_hi"), sem("w_lo"), sem("turned")
    hi_ready, lo_ready, projected, residual = sem("hi_ready"), sem("lo_ready"), sem("projected"), sem("residual")
    raw = core.raw[:, RAW_O:RAW_O + 2048].rearrange("p (k n) -> p k n", k=dk)
    view = lambda i: turn_ps[i % 4][:, :].rearrange("p (k t) -> p k t", t=P)

    with nc.Block() as block:
        @block.sync
        def _(sp):
            sp.wait_ge(w_lo_ready, dk)
            load_ffn_weights(core, sp, d, ffn_loaded, pieces=(2,))

        @block.gpsimd
        def _(pool):
            for k in range(dk):
                pool.wait_ge(w_hi_ready, k + 1)
                pool.tensor_tensor(w_lo[:, k, :], raw[:, k, :], w_hi[:, k, :].bitcast(F32), ALU.subtract)\
                    .then_inc(w_lo_ready, 1)

        @block.tensor
        def _(pe):
            def turn(i):
                if i >= 4:
                    pe.wait_ge(lo_ready, i - 3)
                for k in range(dk):
                    last = pe.transpose(turn_ps[i % 4][:, k * P:(k + 1) * P], o[:, i, k * P:(k + 1) * P],
                                        core.ident[:, :])
                last.then_inc(turned, 1)

            for i in range(4):
                turn(i)
            for i in range(tiles):
                pe.wait_ge(lo_ready, i + 1)
                if i >= 4:
                    pe.wait_ge(residual, i - 3)
                t = slice(i * P, (i + 1) * P)
                for k in range(dk):
                    pe.wait_ge(w_lo_ready, k + 1)
                    last = parts_matmul(pe, out_ps[i % 4][:, :], (oT_hi[:, k, t], oT_lo[:, k, t]),
                                        (w_hi[:, k, :], w_lo[:, k, :]), start=(k == 0), stop=(k == dk - 1))
                last.then_inc(projected, 1)
                if i + 4 < tiles:
                    turn(i + 4)

        @block.scalar
        def _(act):
            for i in range(tiles):
                act.wait_ge(turned, i + 1)
                act.copy(oT_hi[:, :, i * P:(i + 1) * P], view(i)).then_inc(hi_ready, 1)

        @block.vector
        def _(dve):
            dve.wait_ge(loaded[3], 16)
            for k in range(dk):
                dve.tensor_copy(w_hi[:, k, :], raw[:, k, :]).then_inc(w_hi_ready, 1)
            for i in range(tiles):
                t = slice(i * P, (i + 1) * P)
                dve.wait_ge(hi_ready, i + 1)
                dve.tensor_tensor(oT_lo[:, :, t], view(i), oT_hi[:, :, t].bitcast(F32), ALU.subtract)\
                   .then_inc(lo_ready, 1)
                if i >= 4:
                    dve.wait_ge(projected, i - 3)
                    dve.tensor_tensor(core.x[:, i - 4, :], out_ps[i % 4][:, :], core.x[:, i - 4, :], ALU.add)\
                       .then_inc(residual, 1)
            for i in range(tiles - 4, tiles):
                dve.wait_ge(projected, i + 1)
                dve.tensor_tensor(core.x[:, i, :], out_ps[i % 4][:, :], core.x[:, i, :], ALU.add)\
                   .then_inc(residual, 1)
            dve.wait_ge(residual, tiles)


def hybrid_layer(nc, d, out, T, D, until=99):
    out_dram = out.rearrange("o (i p) d -> (o i) p d", p=P)
    with ExitStack() as ctx:
        core = Core(nc, ctx, T, D)
        ffn1_loaded = [core.lasting_sem(f"ffn1_loaded{s}") for s in range(3)]
        ffn2_loaded = [core.lasting_sem(f"ffn2_loaded{s}") for s in range(3)]
        gqa_loaded = [core.lasting_sem(f"gqa_loaded{s}") for s in range(4)]
        stored = core.lasting_sem("stored")
        with ExitStack() as a:
            t = lambda name, shape: a.enter_context(nc.sbuf_tensor(name, shape, F32R))
            wa = {"qkv_hi": t("qkv_hi", [P, 3, 1024]), "qkv_lo": t("qkv_lo", [P, 3, 1024]),
                  "wo_hi": t("wo_hi", [P, 1024]), "wo_lo": t("wo_lo", [P, 1024]),
                  "pw_hi": t("pw_hi", [P, D]), "pw_lo": t("pw_lo", [P, D])}
            wa = {k: v[:] for k, v in wa.items()}
            qkvT = (t("qkvT_hi", [P, 3, T]), t("qkvT_lo", [P, 3, T]))
            with ExitStack() as scope:
                phase_conv(core, scope, qkvT, wa, d)
                core.end_phase()
            with ExitStack() as scope:
                phase_block_attention(core, scope, qkvT, wa, d, ffn1_loaded)
                core.end_phase()
        if until > 1:
            with ExitStack() as scope:
                phase_ffn(core, scope, "f1", ffn1_loaded,
                          after_split=lambda sp: load_gqa_weights(core, sp, d, gqa_loaded))
                core.end_phase()
        if until > 2:
            with ExitStack() as outer:
                t = lambda name, shape, dt: outer.enter_context(nc.sbuf_tensor(name, shape, dt))
                b = {"v": t("b_v", [P, core.tiles, GROUPS, 32], F32), "k_op": t("b_k_op", [OPERAND, GROUPS, T], F32R),
                     "qT": (t("b_qT_hi", [P, core.dk, T], F32R), t("b_qT_lo", [P, core.dk, T], F32R))}
                with ExitStack() as scope:
                    phase_gqa_projections(core, scope, b, gqa_loaded)
                    core.end_phase()
                with ExitStack() as scope:
                    b["o"] = t("b_o", [P, core.tiles, D], F32)
                    ob_row = scope.enter_context(nc.sbuf_tensor("ob_row", [P, D], F32))
                    phase_gqa_core(core, scope, b, d, ffn2_loaded, ob_row)
                    core.end_phase()
                with ExitStack() as scope:
                    phase_gqa_output(core, scope, b["o"], d, gqa_loaded, ffn2_loaded)
                    core.end_phase()
        if until > 3:
            with ExitStack() as scope:
                phase_ffn(core, scope, "f2", ffn2_loaded, store=(stored, out_dram))
                core.end_phase()
        else:
            with nc.Block() as block:
                @block.sync
                def _(sp):
                    for i in range(core.tiles):
                        sp.dma_start(out_dram[i], core.x[:, i, :]).then_inc(stored, 16)
                    sp.wait_ge(stored, 16 * core.tiles)


def kernel(**inputs):
    import numpy as np

    import concourse.bacc as bacc
    from concourse.bass_utils import run_bass_kernel_spmd

    w = {name: np.asarray(a) for name, a in inputs.items()}
    x = w["L0_attn_a_inputs"]
    A, B = w["L0_ffn_A"], w["L0_ffn_B"]
    D = x.shape[-1]
    a, g = "L0_attn_a_", "L0_attn_b_"
    columns = [w[a + "conv_b"], w[a + "bq"], w[a + "bk"], w[a + "bo"], w[g + "q_b"], w[g + "k_b"], w[g + "v_b"]]
    rows = [w[a + "bv"], w[a + "proj_b"], w[g + "o_b"]]
    arrays = {
        "x": x,
        "conv_w": w[a + "conv_w"],
        "wq": w[a + "wq"],
        "wk": w[a + "wk"],
        "wv": w[a + "wv"],
        "wo": w[a + "wo"],
        "proj_w": w[a + "proj_w"],
        "bias_cols": np.concatenate([c.reshape(-1, P) for c in columns]).T,
        "bias_rows": np.concatenate([r.reshape(1, -1) for r in rows], axis=1),
        "WrT": w["L0_ffn_Wr"].T,
        "AT": A.reshape(-1, D).T,
        "Bm": B.transpose(0, 2, 1).reshape(-1, D),
        "qwT": w[g + "q_w"].T,
        "kwT": w[g + "k_w"].T,
        "vwT": w[g + "v_w"].T,
        "owT": w[g + "o_w"].T,
    }
    arrays = {"in_" + name: np.ascontiguousarray(v) for name, v in arrays.items()}
    nc = bacc.Bacc("TRN2", target_bir_lowering=False, num_devices=1)
    d = {name[3:]: nc.dram_tensor(name, v.shape, mybir.dt.from_np(v.dtype), kind="ExternalInput").ap()
         for name, v in arrays.items()}
    out = nc.dram_tensor("out", x.shape, F32, kind="ExternalOutput").ap()
    hybrid_layer(nc, d, out, x.shape[1], D)
    result = run_bass_kernel_spmd(nc, [arrays], core_ids=[0])
    return result.results[0]["out"]
```

```python
from contextlib import ExitStack

import concourse.bass as bass
from concourse import mybir

F32 = mybir.dt.float32
F32R = mybir.dt.float32r
BF16 = mybir.dt.bfloat16
ALU = mybir.AluOpType
ACT = mybir.ActivationFunctionType
AX_X = mybir.AxisListType.X

P = 128
HALF = 512
EPS = 1e-5
LN2 = 0.6931471805599453


def bcast(ap, n):
    return ap.unsqueeze(len(ap.shape)).broadcast_to([*ap.shape, n])


def parts_matmul(pe, out, stationary, moving, start, stop):
    pe.matmul(out, stationary[1], moving[0], start=start, stop=False)
    pe.matmul(out, stationary[0], moving[1], start=False, stop=False)
    return pe.matmul(out, stationary[0], moving[0], start=False, stop=stop)


class Core:

    def __init__(self, nc, ctx, T, D):
        self.nc, self.ctx = nc, ctx
        self.T, self.D, self.tiles, self.dk = T, D, T // P, D // P
        self.x = ctx.enter_context(nc.sbuf_tensor("x", [P, self.tiles, D], F32))
        self.ident = ctx.enter_context(nc.sbuf_tensor("ident", [P, P], F32))
        self.eps = ctx.enter_context(nc.sbuf_tensor("eps", [P, 1], F32))
        self.bias_cols = ctx.enter_context(nc.sbuf_tensor("bias_cols", [P, 26], F32))
        self.raw = ctx.enter_context(nc.sbuf_tensor("raw", [P, 8448], F32))
        self.stats = ctx.enter_context(nc.sbuf_tensor("stats", [P, self.tiles, 6], F32))
        self.mv = ctx.enter_context(nc.sbuf_tensor("mv", [P, self.tiles, 2], F32))
        self.std = ctx.enter_context(nc.sbuf_tensor("std", [P, self.tiles], F32))
        self.rstd = ctx.enter_context(nc.sbuf_tensor("rstd", [P, self.tiles], F32))

        self.phase_sems = []

    def lasting_sem(self, name):
        return self.ctx.enter_context(self.nc.semaphore(name))

    def sem(self, name):
        self.phase_sems.append(self.nc.alloc_semaphore(name=name))
        return self.phase_sems[-1]

    def end_phase(self):
        self.nc.clear_and_free_semaphores(self.phase_sems)
        self.nc.all_engine_barrier()
        self.phase_sems = []


class Chain:

    def __init__(self, engine, semaphore):
        self.engine, self.semaphore, self.count = engine, semaphore, 0

    def link(self, instruction):
        self.count += 1
        instruction.then_inc(self.semaphore, 1)
        self.engine.wait_ge(self.semaphore, self.count)


class RowStats:

    def __init__(self, core, name):
        self.core, self.groups = core, 0
        self.stats_ready = core.sem(name + "_stats_ready")
        self.std_ready = core.sem(name + "_std_ready")

    def vector_stats(self, dve, chain, tiles, x_loaded=None):
        core = self.core
        for i in tiles:
            if x_loaded is not None:
                dve.wait_ge(x_loaded[i], 16)
            dve.bn_stats(core.stats[:, i, :], core.x[:, i, :]).then_inc(chain.semaphore, 1)
            chain.count += 1
        dve.wait_ge(chain.semaphore, chain.count)
        for i in tiles:
            dve.bn_aggr(core.mv[:, i, :], core.stats[:, i, :]).then_inc(self.stats_ready, 1)

    def scalar_std(self, act, tiles, count):
        core, a, b = self.core, tiles[0], tiles[-1] + 1
        act.wait_ge(self.stats_ready, count)
        act.activation(core.std[:, a:b], core.mv[:, a:b, 1], ACT.Sqrt, bias=core.eps[:, 0:1])\
           .then_inc(self.std_ready, 1)

    def vector_rstd(self, dve, chain, tiles):
        core, a, b = self.core, tiles[0], tiles[-1] + 1
        self.groups += 1
        dve.wait_ge(self.std_ready, self.groups)
        chain.link(dve.reciprocal(core.rstd[:, a:b], core.std[:, a:b]))


class LayerNorm:

    def __init__(self, core, scope, name, pad, banks, xT=None):
        nc = core.nc
        name += "_ln"
        self.core, self.pad, self.banks = core, pad, banks
        width = core.T + 2 * pad
        if xT is None:
            xT = [scope.enter_context(nc.sbuf_tensor(f"{name}_xT_{s}", [P, core.dk, width], F32R)) for s in ("hi", "lo")]
        self.hi, self.lo = xT
        self.xn = scope.enter_context(nc.sbuf_tensor(name + "_xn", [P, 2, core.D], F32))
        self.xn_ready = core.sem(name + "_xn_ready")
        self.turned = core.sem(name + "_turned")
        self.hi_ready = core.sem(name + "_hi_ready")
        self.lo_ready = core.sem(name + "_lo_ready")

    def turned_view(self, i):
        return self.banks[i % len(self.banks)][:, :].rearrange("p (k t) -> p k t", t=P)

    def part(self, which, i):
        a = self.pad + i * P
        return which[:, :, a:a + P]

    def columns(self, k, start, n):
        a = self.pad + start
        return self.hi[:, k, a:a + n], self.lo[:, k, a:a + n]

    def vector_all(self, dve, chain, rows, early, between, x_loaded=None):
        if x_loaded is not None:
            rows.vector_stats(dve, chain, range(0, 4), x_loaded)
            rows.vector_rstd(dve, chain, range(0, 4))
        self.vector_xn(dve, 0)
        self.vector_xn(dve, 1)
        early()
        self.vector_xn(dve, 2)
        self.vector_lo(dve, 0)
        self.vector_xn(dve, 3)
        for i in range(1, 4):
            self.vector_lo(dve, i)
        rows.vector_stats(dve, chain, range(4, 8), x_loaded)
        between()
        rows.vector_rstd(dve, chain, range(4, 8))
        self.vector_xn(dve, 4)
        self.vector_xn(dve, 5)
        for i in range(4, 8):
            self.vector_lo(dve, i)
            if i + 2 < 8:
                self.vector_xn(dve, i + 2)

    def vector_xn(self, dve, i):
        if i >= 2:
            dve.wait_ge(self.turned, i - 1)
        dve.tensor_scalar(self.xn[:, i % 2, :], self.core.x[:, i, :], self.core.mv[:, i, 0:1],
                          self.core.rstd[:, i:i + 1], ALU.subtract, ALU.mult).then_inc(self.xn_ready, 1)

    def vector_lo(self, dve, i):
        dve.wait_ge(self.hi_ready, i + 1)
        dve.tensor_tensor(self.part(self.lo, i), self.turned_view(i),
                          self.part(self.hi, i).bitcast(F32), ALU.subtract).then_inc(self.lo_ready, 1)

    def tensor_turn(self, pe, i):
        pe.wait_ge(self.xn_ready, i + 1)
        if i >= len(self.banks):
            pe.wait_ge(self.lo_ready, i - len(self.banks) + 1)
        for k in range(self.core.dk):
            last = pe.transpose(self.banks[i % len(self.banks)][:, k * P:(k + 1) * P],
                                self.xn[:, i % 2, k * P:(k + 1) * P], self.core.ident[:, :])
        last.then_inc(self.turned, 1)

    def scalar_hi(self, act, i):
        act.wait_ge(self.turned, i + 1)
        act.copy(self.part(self.hi, i), self.turned_view(i)).then_inc(self.hi_ready, 1)


def phase_conv(core, scope, qkvT, wa, d):
    nc, tiles, dk = core.nc, core.tiles, core.dk
    sb = lambda name, shape, dt: scope.enter_context(nc.sbuf_tensor(name, shape, dt))
    TAPS, M3 = 3, 3
    conv_raw = core.raw[:, 0:TAPS * dk * M3 * P].rearrange("p (s k m) -> p s k m", s=TAPS, k=dk)
    qkv_raw = core.raw[:, 4608:4608 + 3 * 1024].rearrange("p (s n) -> p s n", s=3)
    conv_hi = sb("conv_hi", [P, TAPS, dk, M3 * P], F32R)
    conv_lo = sb("conv_lo", [P, TAPS, dk, M3 * P], F32R)
    out_raw = sb("out_raw", [P, 1536], F32)
    banks = [scope.enter_context(nc.psum_tensor(f"c_turn{i}", [P, HALF], F32)) for i in range(4)]
    conv_ps = [scope.enter_context(nc.psum_tensor(f"c_conv{i}", [P, HALF], F32)) for i in range(4)]
    ln = LayerNorm(core, scope, "c", 1, banks)
    rows = RowStats(core, "c")
    x_loaded = [core.sem(f"x_loaded{i}") for i in range(tiles)]
    conv_loaded = [core.sem(f"conv_loaded{s}") for s in range(TAPS)]
    small_loaded = core.sem("small_loaded")
    proj_loaded = core.sem("proj_loaded")
    rows_loaded = core.sem("rows_loaded")
    consts_ready = core.sem("consts_ready")
    ident_zeroed = core.sem("ident_zeroed")
    pads_ready = core.sem("c_pads_ready")
    conv_hi_ready = core.sem("conv_hi_ready")
    conv_lo_ready = core.sem("conv_lo_ready")
    projw_hi_ready = core.sem("projw_hi_ready")
    projw_lo_ready = core.sem("projw_lo_ready")
    convolved = core.sem("convolved")
    qkv_hi_ready = core.sem("qkv_hi_ready")
    qkv_lo_ready = core.sem("qkv_lo_ready")
    chain_sem = core.sem("c_chain")
    x_dram = d["x"].rearrange("o (i p) d -> (o i) p d", p=P)
    conv_dram = d["conv_w"].rearrange("s (k p) m -> s p k m", p=P)
    projw = [(qkv_raw[:, s, :], wa["qkv_hi"][:, s, :], wa["qkv_lo"][:, s, :]) for s in range(3)]
    projw += [(out_raw[:, 0:1024], wa["wo_hi"], wa["wo_lo"]), (out_raw[:, 1024:1536], wa["pw_hi"], wa["pw_lo"])]
    units = [(h, m) for h in range(2) for m in range(M3)]

    with nc.Block() as block:
        @block.sync
        def _(sp):
            for i in (0, 2):
                sp.dma_start(core.x[:, i, :], x_dram[i]).then_inc(x_loaded[i], 16)
            for s in range(TAPS):
                sp.dma_start(conv_raw[:, s], conv_dram[s]).then_inc(conv_loaded[s], 16)
                if s == 0:
                    for i in (4, 6):
                        sp.dma_start(core.x[:, i, :], x_dram[i]).then_inc(x_loaded[i], 16)
            sp.dma_start(core.bias_cols[:, :], d["bias_cols"]).then_inc(small_loaded, 16)
            for s, name in enumerate(("wq", "wk", "wv")):
                sp.dma_start(qkv_raw[:, s, :], d[name].rearrange("w h e -> w (h e)")).then_inc(proj_loaded, 16)
            sp.dma_start(out_raw[:, 0:1024].rearrange("p (c w) -> p c w", w=P),
                         d["wo"].rearrange("h e w -> (h e) w").rearrange("(c p) w -> p c w", p=P))\
              .then_inc(proj_loaded, 16)
            sp.dma_start(out_raw[:, 1024:1536], d["proj_w"]).then_inc(proj_loaded, 16)
            for dst, a, n in ((wa["bv_row"], 0, 1024), (wa["pb_row"], 1024, HALF)):
                sp.dma_start(dst, d["bias_rows"][0:1, a:a + n].broadcast_to([P, n])).then_inc(rows_loaded, 16)
            sp.wait_ge(rows_loaded, 32)

        @block.gpsimd
        def _(pool):
            pool.memset(core.ident[:, :], 0.0).then_inc(ident_zeroed, 1)
            pool.memset(core.eps[:, :], EPS).then_inc(consts_ready, 1)
            pool.wait_ge(ident_zeroed, 1)
            pool.affine_select(out=core.ident[:, :], in_=core.ident[:, :], compare_op=ALU.not_equal, fill=1.0,
                               base=0, pattern=[[-1, P]], channel_multiplier=1).then_inc(consts_ready, 1)
            for part in (ln.hi, ln.lo):
                for column in (0, core.T + 1):
                    pool.memset(part[:, :, column:column + 1].bitcast(F32), 0.0).then_inc(pads_ready, 1)
            for s in range(TAPS):
                for k in range(dk):
                    pool.wait_ge(conv_hi_ready, s * dk + k + 1)
                    pool.tensor_tensor(conv_lo[:, s, k, :], conv_raw[:, s, k, :],
                                       conv_hi[:, s, k, :].bitcast(F32), ALU.subtract).then_inc(conv_lo_ready, 1)
            for n, (raw, hi, lo) in enumerate(projw):
                pool.wait_ge(projw_hi_ready, n + 1)
                pool.tensor_tensor(lo, raw, hi.bitcast(F32), ALU.subtract).then_inc(projw_lo_ready, 1)
            pool.wait_ge(projw_lo_ready, len(projw))

        @block.vector
        def _(dve):
            chain = Chain(dve, chain_sem)
            ln.vector_all(dve, chain, rows, lambda: None, lambda: None, x_loaded)
            dve.wait_ge(proj_loaded, 16 * len(projw))
            for n, (raw, hi, lo) in enumerate(projw):
                dve.tensor_copy(hi, raw).then_inc(projw_hi_ready, 1)
            dve.wait_ge(small_loaded, 16)
            for u, (h, m) in enumerate(units):
                dve.wait_ge(qkv_hi_ready, u + 1)
                dve.scalar_tensor_tensor(
                    out=qkvT[1][:, m, h * HALF:(h + 1) * HALF], in0=conv_ps[u % 4][:, :],
                    scalar=core.bias_cols[:, m:m + 1], in1=qkvT[0][:, m, h * HALF:(h + 1) * HALF].bitcast(F32),
                    op0=ALU.add, op1=ALU.subtract).then_inc(qkv_lo_ready, 1)
            dve.wait_ge(qkv_lo_ready, len(units))

        @block.scalar
        def _(act):
            for i in range(1, tiles, 2):
                act.dma_start(core.x[:, i, :], x_dram[i]).then_inc(x_loaded[i], 16)
            act.wait_ge(consts_ready, 2)
            rows.scalar_std(act, range(0, 4), 4)
            for s in range(TAPS):
                act.wait_ge(conv_loaded[s], 16)
                for k in range(dk):
                    act.copy(conv_hi[:, s, k, :], conv_raw[:, s, k, :]).then_inc(conv_hi_ready, 1)
                if s == 0:
                    for i in range(0, 4):
                        ln.scalar_hi(act, i)
            rows.scalar_std(act, range(4, 8), 8)
            for i in range(4, tiles):
                ln.scalar_hi(act, i)
            act.wait_ge(small_loaded, 16)
            for u, (h, m) in enumerate(units):
                act.wait_ge(convolved, u + 1)
                act.activation(qkvT[0][:, m, h * HALF:(h + 1) * HALF], conv_ps[u % 4][:, :], ACT.Identity,
                               bias=core.bias_cols[:, m:m + 1]).then_inc(qkv_hi_ready, 1)
            act.wait_ge(qkv_hi_ready, len(units))

        @block.tensor
        def _(pe):
            pe.wait_ge(consts_ready, 2)
            for i in range(4):
                ln.tensor_turn(pe, i)
            turns_before = {(0, 2): 4, (1, 0): 5, (1, 1): 6, (1, 2): 7}
            for u, (h, m) in enumerate(units):
                if u >= 4:
                    pe.wait_ge(qkv_lo_ready, u - 3)
                pe.wait_ge(pads_ready, 4)
                for s in range(TAPS):
                    if (u, s) in turns_before:
                        ln.tensor_turn(pe, turns_before[u, s])
                    pe.wait_ge(ln.lo_ready, (4, 4, 5)[s] if h == 0 else tiles)
                    for k in range(dk):
                        pe.wait_ge(conv_lo_ready, s * dk + k + 1)
                        w = slice(m * P, (m + 1) * P)
                        last = parts_matmul(pe, conv_ps[u % 4][:, :],
                                            (conv_hi[:, s, k, w], conv_lo[:, s, k, w]),
                                            ln.columns(k, h * HALF + s - 1, HALF),
                                            start=(s == 0 and k == 0), stop=(s == TAPS - 1 and k == dk - 1))
                last.then_inc(convolved, 1)


def phase_block_attention(core, scope, qkvT, wa, d, ffn_raw_loaded):
    nc, tiles = core.nc, core.tiles
    sb = lambda name, shape, dt: scope.enter_context(nc.sbuf_tensor(name, shape, dt))
    ps = lambda name: scope.enter_context(nc.psum_tensor(name, [P, HALF], F32))
    CH = 8
    G = 4 * CH
    V = sb("a_v", [P, tiles, 1024], F32)
    bv_row, pb_row = wa["bv_row"], wa["pb_row"]
    q_pad = sb("q_pad", [P, 2, 2, core.T], F32)
    kT = sb("a_kT", [P, 2, core.T], F32)
    prob = sb("a_prob", [P, 3, HALF], F32)
    probT = sb("a_probT", [P, 2, HALF], F32)
    neg_max = sb("a_neg_max", [P, G, 4], F32)
    row_sum = sb("a_row_sum", [P, G, 4], F32)
    row_inv = sb("a_row_inv", [P, G, 4], F32)
    oT_hi = sb("a_oT_hi", [P, 2, HALF], F32R)
    oT_lo = sb("a_oT_lo", [P, 2, HALF], F32R)
    yT_hi = sb("a_yT_hi", [P, core.T], F32R)
    yT_lo = sb("a_yT_lo", [P, core.T], F32R)
    ident16 = sb("ident16", [P, P], BF16)
    mask = sb("a_mask", [P, 4, P], BF16)
    S_ps = [ps(f"a_S{i}") for i in range(2)]
    T_ps = ps("a_T")
    O_ps = [ps(f"a_O{i}") for i in range(2)]
    proj_ps = ps("a_proj")
    acc_ps = [ps(f"a_acc{i}") for i in range(2)]

    consts = core.sem("a_consts")
    const_chain = core.sem("a_const_chain")
    v_done = core.sem("a_v_done")
    v_ready = core.sem("a_v_ready")
    q_done = core.sem("a_q_done")
    k_done = core.sem("a_k_done")
    q_ready = core.sem("a_q_ready")
    k_ready = core.sem("a_k_ready")
    scored = core.sem("a_scored")
    max_ready = core.sem("a_max_ready")
    exp_ready = core.sem("a_exp_ready")
    inv_ready = core.sem("a_inv_ready")
    prob_ready = core.sem("a_prob_ready")
    prob_turned = core.sem("a_prob_turned")
    probT_ready = core.sem("a_probT_ready")
    mixed = core.sem("a_mixed")
    oT_hi_ready = core.sem("a_oT_hi_ready")
    oT_lo_ready = core.sem("a_oT_lo_ready")
    projected = core.sem("a_projected")
    yT_hi_ready = core.sem("a_yT_hi_ready")
    yT_lo_ready = core.sem("a_yT_lo_ready")
    expanded = core.sem("a_expanded")
    residual = core.sem("a_residual")
    x_biased = core.sem("a_x_biased")
    chain_sem = core.sem("a_chain")

    def pair(j):
        return j // 2, j % 2

    rows = RowStats(core, "a")

    LAG_T, LAG_O = 2, 3

    with nc.Block() as block:
        @block.sync
        def _(sp):
            load_ffn_weights(core, sp, d, ffn_raw_loaded)

        @block.gpsimd
        def _(pool):
            count = [0]

            def link(instruction):
                count[0] += 1
                instruction.then_inc(const_chain, 1)
                pool.wait_ge(const_chain, count[0])

            link(pool.tensor_copy(ident16[:, :], core.ident[:, :]))
            link(pool.memset(mask[:, :, :], 0.0))
            pool.affine_select(out=mask[:, :, :], in_=mask[:, :, :], compare_op=ALU.is_ge, fill=-1e9,
                               base=0, pattern=[[0, 4], [-1, P]], channel_multiplier=1).then_inc(consts, 1)
            for slot in range(2):
                pool.wait_ge(consts, 1 + 2 * slot)
                pool.memset(q_pad[64:128, slot, 0, :], 0.0).then_inc(consts, 1)
                pool.wait_ge(consts, 2 + 2 * slot)
                pool.memset(q_pad[0:64, slot, 1, :], 0.0).then_inc(consts, 1)
            pool.wait_ge(consts, 5)
            for i in range(tiles):
                pool.tensor_tensor(core.x[:, i, :], core.x[:, i, :], pb_row[:, :], ALU.add).then_inc(x_biased, 1)
            for n in range(G):
                pool.wait_ge(inv_ready, n + 1)
                p = prob[:, n % 3, :].rearrange("p (j k) -> p j k", k=P)
                pool.tensor_tensor(p, p, bcast(row_inv[:, n, :], P), ALU.mult).then_inc(prob_ready, 1)

        @block.tensor
        def _(pe):
            def project_q(c, h):
                w, t = slice(c * P, (c + 1) * P), slice(h * HALF, (h + 1) * HALF)
                if c or h:
                    pe.wait_ge(k_ready, 2 * c + h)
                parts_matmul(pe, proj_ps[:, :], (wa["qkv_hi"][:, 0, w], wa["qkv_lo"][:, 0, w]),
                             (qkvT[0][:, 0, t], qkvT[1][:, 0, t]), True, True).then_inc(q_done, 1)

            def project_k(c, h):
                w, t = slice(c * P, (c + 1) * P), slice(h * HALF, (h + 1) * HALF)
                pe.wait_ge(q_ready, 2 * (2 * c + h + 1))
                parts_matmul(pe, proj_ps[:, :], (wa["qkv_hi"][:, 1, w], wa["qkv_lo"][:, 1, w]),
                             (qkvT[0][:, 1, t], qkvT[1][:, 1, t]), True, True).then_inc(k_done, 1)

            def score(n):
                c, g = n // 4, n % 4
                bank = S_ps[n % 2]
                if n < 2:
                    pe.wait_ge(v_ready, 2 * tiles)
                    pe.wait_ge(consts, 5)
                else:
                    pe.wait_ge(exp_ready, n - 1)
                pe.wait_ge(q_ready, 2 * (2 * c + g // 2 + 1))
                pe.wait_ge(k_ready, 2 * c + g // 2 + 1)
                pe.matmul(bank[:, :], ident16[:, :], mask[:, :, :].rearrange("p j k -> p (j k)"),
                          start=True, stop=True, skip_group_check=True)
                for j in range(4):
                    b, head = pair(j)
                    t = slice((2 * g + b) * P, (2 * g + b + 1) * P)
                    last = pe.matmul(bank[:, j * P:(j + 1) * P], q_pad[:, c % 2, head, t], kT[:, c % 2, t],
                                     start=False, stop=True, skip_group_check=True)
                last.then_inc(scored, 1)

            def turn(n):
                pe.wait_ge(prob_ready, n + 1)
                if n >= 1:
                    pe.wait_ge(probT_ready, n)
                for j in range(4):
                    last = pe.transpose(T_ps[:, j * P:(j + 1) * P], prob[:, n % 3, j * P:(j + 1) * P], core.ident[:, :])
                last.then_inc(prob_turned, 1)

            def mix(n):
                c, g = n // 4, n % 4
                pe.wait_ge(probT_ready, n + 1)
                if n >= 2:
                    pe.wait_ge(oT_lo_ready, n - 1)
                for j in range(4):
                    b, head = pair(j)
                    e = (2 * c + head) * 64
                    last = pe.matmul(O_ps[n % 2][64 * head:64 * head + 64, b * P:(b + 1) * P], V[:, 2 * g + b, e:e + 64],
                                     probT[:, n % 2, j * P:(j + 1) * P], start=True, stop=True,
                                     skip_group_check=True)
                last.then_inc(mixed, 1)

            def project_out(c, h):
                pe.wait_ge(oT_lo_ready, 4 * c + 2 * h + 2)
                w = slice(c * P, (c + 1) * P)
                parts_matmul(pe, acc_ps[h][:, :], (wa["wo_hi"][:, w], wa["wo_lo"][:, w]),
                             (oT_hi[:, h, :], oT_lo[:, h, :]), start=(c == 0), stop=(c == CH - 1))\
                    .then_inc(projected, 1)

            for u in range(2 * tiles):
                i, c = u // 2, u % 2
                if u >= 4:
                    pe.wait_ge(v_ready, u - 3)
                bank = (*S_ps, T_ps, O_ps[0])[u % 4]
                cols = slice(c * HALF, (c + 1) * HALF)
                parts_matmul(pe, bank[:, :], (qkvT[0][:, 2, i * P:(i + 1) * P], qkvT[1][:, 2, i * P:(i + 1) * P]),
                             (wa["qkv_hi"][:, 2, cols], wa["qkv_lo"][:, 2, cols]), True, True).then_inc(v_done, 1)
                if u % 4 == 3:
                    (project_q, project_k)[u // 4 % 2](0, u // 8)

            for n in range(G + LAG_O + 1):
                if n < G:
                    score(n)
                if n // 4 + 1 < CH:
                    (project_q, project_k)[n % 2](n // 4 + 1, n % 4 // 2)
                if LAG_O <= n < G + LAG_O:
                    mix(n - LAG_O)
                if LAG_T <= n < G + LAG_T:
                    turn(n - LAG_T)
                done = n - LAG_O - 1
                if done >= 0 and done % 2 == 1:
                    project_out(done // 4, done % 4 // 2)
            for i in range(tiles):
                pe.wait_ge(yT_lo_ready, i // 4 + 1)
                if i >= 4:
                    pe.wait_ge(residual, i - 3)
                t = slice(i * P, (i + 1) * P)
                bank = (*S_ps, T_ps, proj_ps)[i % 4]
                parts_matmul(pe, bank[:, :], (yT_hi[:, t], yT_lo[:, t]), (wa["pw_hi"], wa["pw_lo"]),
                             True, True).then_inc(expanded, 1)

        @block.scalar
        def _(act):
            def k_out(c, h):
                n = 2 * c + h
                act.wait_ge(k_done, n + 1)
                if c >= 2:
                    act.wait_ge(scored, 4 * (c - 1))
                act.activation(kT[:, c % 2, h * HALF:(h + 1) * HALF], proj_ps[:, :], ACT.Identity,
                               bias=core.bias_cols[:, 11 + c:12 + c]).then_inc(k_ready, 1)

            def exponent(n):
                act.wait_ge(max_ready, n + 1)
                if n >= 3:
                    act.wait_ge(prob_turned, n - 2)
                for j in range(4):
                    last = act.activation(prob[:, n % 3, j * P:(j + 1) * P], S_ps[n % 2][:, j * P:(j + 1) * P],
                                          ACT.Exp, bias=neg_max[:, n, j:j + 1], accum_out=row_sum[:, n, j:j + 1])
                last.then_inc(exp_ready, 1)

            def turned_out(n):
                act.wait_ge(prob_turned, n + 1)
                if n >= 2:
                    act.wait_ge(mixed, n - 1)
                act.copy(probT[:, n % 2, :], T_ps[:, :]).then_inc(probT_ready, 1)

            def mixed_out(n):
                c, g = n // 4, n % 4
                act.wait_ge(mixed, n + 1)
                if c >= 1:
                    act.wait_ge(projected, 2 * (c - 1) + g // 2 + 1)
                act.copy(oT_hi[:, g // 2, (g % 2) * 256:(g % 2) * 256 + 256], O_ps[n % 2][:, 0:256]).then_inc(oT_hi_ready, 1)

            k_out(0, 0)
            k_out(0, 1)
            for n in range(G + LAG_O + 1):
                if n >= LAG_O + 1:
                    mixed_out(n - LAG_O - 1)
                if n < G:
                    exponent(n)
                if n % 2 == 1 and n // 4 + 1 < CH:
                    k_out(n // 4 + 1, n % 4 // 2)
                if LAG_T <= n < G + LAG_T:
                    turned_out(n - LAG_T)
            for h in range(2):
                act.wait_ge(projected, 2 * (CH - 1) + h + 1)
                act.activation(yT_hi[:, h * HALF:(h + 1) * HALF], acc_ps[h][:, :], ACT.Identity,
                               bias=core.bias_cols[:, 19:20]).then_inc(yT_hi_ready, 1)
            rows.scalar_std(act, range(0, 4), 4)

        @block.vector
        def _(dve):
            def q_out(c, h):
                n = 2 * c + h
                dve.wait_ge(q_done, n + 1)
                if c >= 2:
                    dve.wait_ge(scored, 4 * (c - 1))
                for head in range(2):
                    r = slice(64 * head, 64 * head + 64)
                    dve.tensor_scalar(q_pad[r, c % 2, head, h * HALF:(h + 1) * HALF], proj_ps[r, :],
                                      core.bias_cols[r, 3 + c:4 + c], 0.125, ALU.add, ALU.mult).then_inc(q_ready, 1)

            def maximum(n):
                dve.wait_ge(scored, n + 1)
                dve.tensor_reduce(neg_max[:, n, :], S_ps[n % 2][:, :].rearrange("p (j k) -> p j k", k=P),
                                  AX_X, ALU.max, negate=True).then_inc(max_ready, 1)

            def inverse(n):
                dve.wait_ge(exp_ready, n + 1)
                dve.reciprocal(row_inv[:, n, :], row_sum[:, n, :]).then_inc(inv_ready, 1)

            def mixed_lo(n):
                g = n % 4
                dve.wait_ge(oT_hi_ready, n + 1)
                cols = slice((g % 2) * 256, (g % 2) * 256 + 256)
                dve.tensor_tensor(oT_lo[:, g // 2, cols], O_ps[n % 2][:, 0:256], oT_hi[:, g // 2, cols].bitcast(F32),
                                  ALU.subtract).then_inc(oT_lo_ready, 1)

            chain = Chain(dve, chain_sem)
            for u in range(2 * tiles):
                i, c = u // 2, u % 2
                dve.wait_ge(v_done, u + 1)
                bank = (*S_ps, T_ps, O_ps[0])[u % 4]
                cols = slice(c * HALF, (c + 1) * HALF)
                dve.tensor_tensor(V[:, i, cols], bank[:, :], bv_row[:, cols], ALU.add).then_inc(v_ready, 1)
                if u % 8 == 3:
                    q_out(0, u // 8)
            for n in range(G + LAG_O + 1):
                if n < G:
                    maximum(n)
                if n >= LAG_O + 1:
                    mixed_lo(n - LAG_O - 1)
                if 1 <= n <= G:
                    inverse(n - 1)
                if n % 2 == 0 and n // 4 + 1 < CH:
                    q_out(n // 4 + 1, n % 4 // 2)
            for h in range(2):
                t = slice(h * HALF, (h + 1) * HALF)
                dve.wait_ge(yT_hi_ready, h + 1)
                dve.scalar_tensor_tensor(out=yT_lo[:, t], in0=acc_ps[h][:, :], scalar=core.bias_cols[:, 19:20],
                                         in1=yT_hi[:, t].bitcast(F32), op0=ALU.add, op1=ALU.subtract)\
                   .then_inc(yT_lo_ready, 1)
            dve.wait_ge(x_biased, tiles)
            for i in range(tiles):
                dve.wait_ge(expanded, i + 1)
                bank = (*S_ps, T_ps, proj_ps)[i % 4]
                dve.tensor_tensor(core.x[:, i, :], bank[:, :], core.x[:, i, :], ALU.add).then_inc(residual, 1)
                if i == 3:
                    dve.wait_ge(residual, 4)
                    rows.vector_stats(dve, chain, range(0, 4))
            rows.vector_rstd(dve, chain, range(0, 4))
            dve.wait_ge(residual, tiles)


RAW_WR, RAW_A, RAW_B = 0, 256, 4352


def load_ffn_weights(core, sp, d, loaded, pieces=(0, 1, 2)):
    places = ((RAW_WR, "WrT", 64), (RAW_A, "AT", 1024), (RAW_B, "Bm", 512))
    for s in pieces:
        at, name, n = places[s]
        chunks = d[name].shape[0] // P
        sp.dma_start(core.raw[:, at:at + chunks * n].rearrange("p (k n) -> p k n", n=n),
                     d[name].rearrange("(k p) n -> p k n", p=P)).then_inc(loaded[s], 16)


def phase_ffn(core, scope, name, loaded, after_split=None, store=None):
    nc, tiles, dk = core.nc, core.tiles, core.dk
    sb = lambda what, shape, dt: scope.enter_context(nc.sbuf_tensor(f"{name}_{what}", shape, dt))
    ps = lambda what: scope.enter_context(nc.psum_tensor(f"{name}_{what}", [P, HALF], F32))
    sem = lambda what: core.sem(f"{name}_{what}")
    K, C = 64, 8
    UNITS = 2 * C
    AHEAD = 4
    wr_hi, wr_lo = (sb(f"wr_{s}", [P, dk, 2 * K], F32R) for s in ("hi", "lo"))
    a_hi, a_lo = (sb(f"a_{s}", [P, dk, C * P], F32R) for s in ("hi", "lo"))
    b_hi, b_lo = (sb(f"b_{s}", [P, C, HALF], F32R) for s in ("hi", "lo"))
    spread_f = sb("spread_f", [P, C, P], F32)
    spread = sb("spread", [P, C, P], F32R)
    scoreT = sb("scoreT", [K, HALF], F32)
    score = sb("score", [P, 4, K], F32)
    rest = sb("rest", [P, 4, K], F32)
    top = sb("top", [P, 4, 16], F32)
    gate = sb("gate", [P, 4, K], F32)
    chosen = sb("chosen", [P, 4, K], F32)
    total = sb("total", [P, 8], F32)
    gate2 = sb("gate2", [P, 4, 2, K], F32)
    gateT = sb("gateT", [P, 2, HALF], F32R)
    h_sb = sb("h_sb", [P, AHEAD + 2, HALF], F32)
    hg = sb("hg", [P, 2, HALF], F32)
    hg_hi = sb("hg_hi", [P, 2, HALF], F32R)
    hg_lo = sb("hg_lo", [P, 2, HALF], F32R)
    acc = [ps(f"acc{i}") for i in range(4)]
    up_ps = [ps(f"up{i}") for i in range(2)]
    spread_ps = ps("spread_ps")
    aux = ps("aux")
    ln = LayerNorm(core, scope, name, 0, acc)
    rows, next_rows = RowStats(core, name), RowStats(core, name + "_next")

    w_hi, w_lo = sem("w_hi"), sem("w_lo")
    spread_chain, spread_built, spread_ready = sem("spread_chain"), sem("spread_built"), sem("spread_ready")
    routed, scoreT_ready, score_turned = sem("routed"), sem("scoreT_ready"), sem("score_turned")
    shifted, expd, gate_ready, gate_turned = sem("shifted"), sem("expd"), sem("gate_ready"), sem("gate_turned")
    gateT_hi_ready, gateT_ready = sem("gateT_hi"), sem("gateT_ready")
    up_done, h_ready, spread_done = sem("up_done"), sem("h_ready"), sem("spread_done")
    hg_ready, hg_hi_ready, hg_lo_ready = sem("hg_ready"), sem("hg_hi_ready"), sem("hg_lo_ready")
    acc_done = sem("acc_done")
    down_done, residual, chain_sem = sem("down_done"), sem("residual"), sem("chain")

    wr_raw = core.raw[:, RAW_WR:RAW_A].rearrange("p (k n) -> p k n", k=dk)
    a_raw = core.raw[:, RAW_A:RAW_B].rearrange("p (k n) -> p k n", k=dk)
    b_raw = core.raw[:, RAW_B:RAW_B + 4096].rearrange("p (c n) -> p c n", c=C)
    pieces = [(wr_raw, wr_hi[:, :, 0:K], wr_lo[:, :, 0:K], 0), (wr_raw, wr_hi[:, :, K:], wr_lo[:, :, K:], 0)]
    for c in range(C):
        cols = slice(c * P, (c + 1) * P)
        pieces.append((a_raw[:, :, cols], a_hi[:, :, cols], a_lo[:, :, cols], 1))
        pieces.append((b_raw[:, c, :], b_hi[:, c, :], b_lo[:, c, :], 2))
    A_AT = lambda c: 2 + 2 * c + 1
    B_AT = lambda c: 2 + 2 * c + 2

    with nc.Block() as block:
        @block.sync
        def _(sp):
            if after_split is not None:
                sp.wait_ge(w_lo, len(pieces))
                after_split(sp)
            if store is not None:
                stored, out = store
                for i in range(tiles):
                    sp.wait_ge(residual, i + 1)
                    sp.dma_start(out[i], core.x[:, i, :]).then_inc(stored, 16)
                sp.wait_ge(stored, 16 * tiles)

        @block.gpsimd
        def _(pool):
            def split_lo(n):
                raw, hi, lo, _ = pieces[n]
                pool.wait_ge(w_hi, n + 1)
                pool.tensor_tensor(lo, raw, hi.bitcast(F32), ALU.subtract).then_inc(w_lo, 1)

            for n in range(3):
                split_lo(n)
            pool.memset(spread_f[:, :, :], 0.0).then_inc(spread_chain, 1)
            for r in range(2):
                pool.wait_ge(spread_chain, r + 1)
                v = spread_f[:, :, :].rearrange("p c (k r) -> p c k r", r=16)
                pool.affine_select(out=v, in_=v, compare_op=ALU.not_equal, fill=1.0, base=-K * r,
                                   pattern=[[-8, C], [-1, 8], [0, 16]], channel_multiplier=1)\
                    .then_inc(spread_chain if r == 0 else spread_built, 1)
            for n in range(3, len(pieces)):
                split_lo(n)

        @block.vector
        def _(dve):
            chain = Chain(dve, chain_sem)

            def split_hi(n):
                raw, hi, lo, load = pieces[n]
                dve.wait_ge(loaded[load], 16)
                dve.tensor_copy(hi, raw).then_inc(w_hi, 1)

            def top8(half):
                dve.wait_ge(score_turned, half + 1)
                chain.link(dve.tensor_copy(score[:, :, :], aux[:, 0:4 * K].rearrange("p (i k) -> p i k", k=K)))
                for i in range(4):
                    last = dve.max(top[:, i, 0:8], score[:, i, :])
                chain.link(last)
                for i in range(4):
                    last = dve.match_replace(out=rest[:, i, :], in_to_replace=top[:, i, 0:8],
                                             in_values=score[:, i, :], imm_value=-3e38)
                chain.link(last)

            def top16(half):
                for i in range(4):
                    last = dve.max(top[:, i, 8:16], rest[:, i, :])
                chain.link(last)
                for i in range(4):
                    last = dve.match_replace(out=rest[:, i, :], in_to_replace=top[:, i, 8:16],
                                             in_values=rest[:, i, :], imm_value=-3e38)
                chain.link(last)
                dve.tensor_tensor(gate[:, :, :], score[:, :, :], bcast(top[:, :, 0], K), ALU.subtract)\
                   .then_inc(shifted, 1)
                chain.link(dve.tensor_tensor(chosen[:, :, :], rest[:, :, :], score[:, :, :], ALU.not_equal))

            def weigh(half):
                dve.wait_ge(expd, half + 1)
                chain.link(dve.tensor_tensor(gate[:, :, :], gate[:, :, :], chosen[:, :, :], ALU.mult))
                chain.link(dve.tensor_reduce(total[:, 0:4], gate[:, :, :], AX_X, ALU.add))
                chain.link(dve.reciprocal(total[:, 4:8], total[:, 0:4]))
                for r in range(2):
                    dve.scalar_tensor_tensor(out=gate2[:, :, r, :], in0=gate[:, :, :], scalar=2.0,
                                             in1=bcast(total[:, 4:8], K), op0=ALU.mult, op1=ALU.mult)\
                       .then_inc(gate_ready, 1)

            def gateT_lo(half):
                dve.wait_ge(gateT_hi_ready, half + 1)
                g = gateT[K:2 * K, half, :]
                dve.tensor_tensor(g, aux[K:2 * K, :], g.bitcast(F32), ALU.subtract).then_inc(gateT_ready, 1)

            def scale(u):
                dve.wait_ge(h_ready, u + 1)
                dve.wait_ge(spread_done, u + 1)
                if u >= 2:
                    dve.wait_ge(hg_hi_ready, u - 1)
                dve.tensor_tensor(hg[:, u % 2, :], spread_ps[:, :], h_sb[:, u % (AHEAD + 2), :], ALU.mult).then_inc(hg_ready, 1)

            def scale_lo(u):
                dve.wait_ge(hg_hi_ready, u + 1)
                dve.tensor_tensor(hg_lo[:, u % 2, :], hg[:, u % 2, :], hg_hi[:, u % 2, :].bitcast(F32),
                                  ALU.subtract).then_inc(hg_lo_ready, 1)

            def add_residual(half):
                for i in range(4 * half, 4 * half + 4):
                    dve.wait_ge(acc_done, i + 1)
                    dve.tensor_tensor(core.x[:, i, :], acc[i % 4][:, :], core.x[:, i, :], ALU.add)\
                       .then_inc(residual, 1)

            ln.vector_all(dve, chain, rows, lambda: [split_hi(n) for n in range(3)],
                          lambda: [split_hi(n) for n in range(3, A_AT(AHEAD))])
            dve.wait_ge(spread_built, 1)
            dve.tensor_copy(spread[:, :, :], spread_f[:, :, :]).then_inc(spread_ready, 1)
            top8(0)
            top16(0)
            weigh(0)
            gateT_lo(0)
            for u in range(UNITS):
                for n in range(A_AT(u + AHEAD), min(A_AT(u + AHEAD + 1), len(pieces))):
                    split_hi(n)
                scale(u)
                scale_lo(u)
                if u == 3:
                    top8(1)
                if u == 4:
                    top16(1)
                if u == 5:
                    weigh(1)
                if u == 6:
                    gateT_lo(1)
                if u == C:
                    add_residual(0)
                if u == C + 2 and store is None:
                    next_rows.vector_stats(dve, chain, range(0, 4))
                if u == C + 4 and store is None:
                    next_rows.vector_rstd(dve, chain, range(0, 4))
            add_residual(1)
            dve.wait_ge(residual, tiles)

        @block.scalar
        def _(act):
            def scoreT_out(half):
                act.wait_ge(routed, half + 1)
                if half:
                    act.wait_ge(score_turned, half)
                act.copy(scoreT[:, :], aux[0:K, :]).then_inc(scoreT_ready, 1)

            def exponent(half):
                act.wait_ge(shifted, half + 1)
                act.activation(gate[:, :, :], gate[:, :, :], ACT.Exp).then_inc(expd, 1)

            def gateT_hi(half):
                act.wait_ge(gate_turned, half + 1)
                act.copy(gateT[:, half, :], aux[:, :]).then_inc(gateT_hi_ready, 1)

            def h_out(u):
                act.wait_ge(up_done, u + 1)
                if u > AHEAD + 1:
                    act.wait_ge(hg_ready, u - AHEAD - 1)
                act.copy(h_sb[:, u % (AHEAD + 2), :], up_ps[u % 2][:, :]).then_inc(h_ready, 1)

            def hg_high(u):
                act.wait_ge(hg_ready, u + 1)
                if u >= 2 and u % C == 1:
                    act.wait_ge(acc_done, 4 * (u // C))
                elif u >= 2:
                    act.wait_ge(down_done, u - 1 - (u - 2) // C)
                act.copy(hg_hi[:, u % 2, :], hg[:, u % 2, :]).then_inc(hg_hi_ready, 1)

            for i in range(0, 4):
                ln.scalar_hi(act, i)
            rows.scalar_std(act, range(4, 8), 4)
            scoreT_out(0)
            h_out(0)
            for i in range(4, 8):
                ln.scalar_hi(act, i)
            h_out(1)
            exponent(0)
            for u in range(2, AHEAD):
                h_out(u)
            gateT_hi(0)
            h_out(AHEAD)
            for u in range(UNITS):
                hg_high(u)
                if u + AHEAD + 1 < UNITS:
                    h_out(u + AHEAD + 1)
                if u == 2:
                    scoreT_out(1)
                if u == 4:
                    exponent(1)
                if u == 5:
                    gateT_hi(1)
                if u == C + 3 and store is None:
                    next_rows.scalar_std(act, range(0, 4), 4)

        @block.tensor
        def _(pe):
            def route(half):
                pe.wait_ge(ln.lo_ready, 4 * half + 4)
                pe.wait_ge(w_lo, 2)
                if half:
                    pe.wait_ge(gateT_ready, half)
                for k in range(dk):
                    last = parts_matmul(pe, aux[:, :], (wr_hi[:, k, :], wr_lo[:, k, :]),
                                        ln.columns(k, half * HALF, HALF), start=(k == 0), stop=(k == dk - 1))
                last.then_inc(routed, 1)

            def turn_scores(half):
                pe.wait_ge(scoreT_ready, half + 1)
                for i in range(4):
                    last = pe.transpose(aux[:, i * K:(i + 1) * K], scoreT[:, i * P:(i + 1) * P], core.ident[0:K, 0:K])
                last.then_inc(score_turned, 1)

            def turn_gates(half):
                pe.wait_ge(gate_ready, 2 * half + 2)
                for i in range(4):
                    last = pe.transpose(aux[:, i * P:(i + 1) * P],
                                        gate2[:, i, :, :].rearrange("p r k -> p (r k)"), core.ident[:, :])
                last.then_inc(gate_turned, 1)

            def up(u):
                half, c = u // C, u % C
                pe.wait_ge(ln.lo_ready, 4 * half + 4)
                if half == 0:
                    pe.wait_ge(w_lo, A_AT(c))
                if u >= 2:
                    pe.wait_ge(h_ready, u - 1)
                cols = slice(c * P, (c + 1) * P)
                for k in range(dk):
                    last = parts_matmul(pe, up_ps[u % 2][:, :], (a_hi[:, k, cols], a_lo[:, k, cols]),
                                        ln.columns(k, half * HALF, HALF), start=(k == 0), stop=(k == dk - 1))
                last.then_inc(up_done, 1)

            def spread_gates(u):
                half, c = u // C, u % C
                pe.wait_ge(gateT_ready, half + 1)
                if u >= 1:
                    pe.wait_ge(hg_ready, u)
                pe.matmul(spread_ps[:, :], spread[:, c, :], gateT[:, half, :], start=True, stop=True)\
                  .then_inc(spread_done, 1)

            def down(u):
                half, c = u // C, u % C
                pe.wait_ge(hg_lo_ready, u + 1)
                if half == 0:
                    pe.wait_ge(w_lo, B_AT(c))
                for i in range(4):
                    t = slice(i * P, (i + 1) * P)
                    if c == 0 and half:
                        pe.wait_ge(residual, i + 1)
                    last = parts_matmul(pe, acc[i][:, :], (hg_hi[:, u % 2, t], hg_lo[:, u % 2, t]),
                                        (b_hi[:, c, :], b_lo[:, c, :]), start=(c == 0), stop=(c == C - 1))
                    if c == C - 1:
                        last.then_inc(acc_done, 1)
                    elif i == 3:
                        last.then_inc(down_done, 1)

            for i in range(4):
                ln.tensor_turn(pe, i)
            route(0)
            up(0)
            turn_scores(0)
            for i in range(4, 8):
                ln.tensor_turn(pe, i)
            for u in range(1, AHEAD):
                up(u)
            turn_gates(0)
            up(AHEAD)
            pe.wait_ge(spread_ready, 1)
            pe.wait_ge(ln.lo_ready, tiles)
            spread_gates(0)
            for u in range(UNITS):
                if u + AHEAD + 1 < UNITS:
                    up(u + AHEAD + 1)
                if u + 1 < UNITS:
                    spread_gates(u + 1)
                down(u)
                if u == 1:
                    route(1)
                if u == 2:
                    turn_scores(1)
                if u == 5:
                    turn_gates(1)


RAW_Q, RAW_K, RAW_V, RAW_O = 0, 2048, 2560, 6400
HEADS, GROUPS, DH = 32, 8, 16
PER = HEADS // GROUPS
OPERAND = 96


def load_gqa_weights(core, sp, d, loaded):
    for s, (at, name, n) in enumerate(((RAW_K, "kwT", 128), (RAW_V, "vwT", 128), (RAW_Q, "qwT", 512),
                                       (RAW_O, "owT", 512))):
        sp.dma_start(core.raw[:, at:at + core.dk * n].rearrange("p (k n) -> p k n", n=n),
                     d[name].rearrange("(k p) n -> p k n", p=P)).then_inc(loaded[s], 16)


def stack_keys(queue, b, g, loaded):
    for r in range(4):
        src = b["kT"][r % 2][DH * g:DH * (g + 1), :].bitcast(F32)
        queue.dma_start(b["k_op"][DH * r:DH * (r + 1), g, :].bitcast(F32), src).then_inc(loaded, 16)


def stack_queries(queue, b, g, rows, loaded):
    for j in range(PER):
        head = PER * g + j
        at = slice(DH * (head % 8), DH * (head % 8) + DH)
        for r in rows:
            src = b["qT"][r // 2][at, head // 8, :].bitcast(F32).rearrange("d (h t) -> d h t", h=2)
            to = (b["q_op"], b["q_op_odd"])[g % 2] if g else b["q_op"]
            queue.dma_start(to[DH * r:DH * (r + 1), :, j, :].bitcast(F32), src).then_inc(loaded, 16)


def phase_gqa_projections(core, scope, b, loaded):
    nc, tiles, dk = core.nc, core.tiles, core.dk
    sb = lambda what, shape, dt: scope.enter_context(nc.sbuf_tensor(f"p_{what}", shape, dt))
    ps = lambda what: scope.enter_context(nc.psum_tensor(f"p_{what}", [P, HALF], F32))
    kT_hi, kT_lo = b["kT"] = [sb(f"kT_{s}", [P, core.T], F32R) for s in ("hi", "lo")]
    w_hi, w_lo = (sb(f"w_{s}", [P, 3, dk, P], F32R) for s in ("hi", "lo"))
    turn_ps = [ps(f"turn{i}") for i in range(4)]
    out_ps = [ps(f"out{i}") for i in range(3)]
    v_ps = ps("v")
    ln = LayerNorm(core, scope, "p", 0, turn_ps, b["xT"])
    rows = RowStats(core, "p")
    vT = ln.xn[:, :, :].rearrange("p s t -> p (s t)")
    sem = lambda what: core.sem(f"p_{what}")
    w_hi_ready, w_lo_ready, projected = sem("w_hi"), sem("w_lo"), sem("projected")
    hi_ready, lo_ready, v_turned, v_ready = sem("hi_ready"), sem("lo_ready"), sem("v_turned"), sem("v_ready")
    zeroed, chain_sem = sem("zeroed"), sem("chain")
    b["consts_ready"] = sem("consts_ready")
    raw = lambda at, n: core.raw[:, at:at + dk * n].rearrange("p (k n) -> p k n", n=n)
    K, Q, V = range(3)
    q_piece = lambda m: (raw(RAW_Q, 512)[:, :, m * P:(m + 1) * P], 2)
    pieces = [(raw(RAW_K, P), 0), q_piece(0), (raw(RAW_V, P), 1), q_piece(1), q_piece(2), q_piece(3)]
    parts_of = lambda n, w, later: w[:, n, :, :] if n < 3 else later[:, n - 3, :, :]
    hi_of = lambda n: parts_of(n, w_hi, b["qw"][0])
    lo_of = lambda n: parts_of(n, w_lo, b["qw"][1])
    units = [(w, h) for w in (K, Q, V) for h in range(2)]
    bias = lambda w: core.bias_cols[:, (24, 20, 25)[w]:(24, 20, 25)[w] + 1]

    def target(w, h, part):
        t = slice(h * HALF, (h + 1) * HALF)
        return (kT_hi, kT_lo)[part][:, t] if w == K else b["qT"][part][:, 0, t]

    with nc.Block() as block:
        @block.sync
        def _(sp):
            sp.wait_ge(lo_ready, 2)
            stack_keys(sp, b, 0, b["first_k_loaded"])
            sp.wait_ge(lo_ready, 4)
            stack_queries(sp, b, 0, range(2, 4), b["q_loaded"][0])

        @block.gpsimd
        def _(pool):
            def split_lo(n):
                pool.wait_ge(w_hi_ready, n + 1)
                pool.tensor_tensor(lo_of(n), pieces[n][0], hi_of(n).bitcast(F32), ALU.subtract)\
                    .then_inc(w_lo_ready, 1)

            split_lo(0)
            pool.wait_ge(w_lo_ready, 1)
            pool.memset(b["k_op"][64:OPERAND, :, :].bitcast(F32), 0.0).then_inc(zeroed, 1)
            pool.wait_ge(zeroed, 1)
            split_lo(1)
            split_lo(2)
            pool.memset(b["v"][:, :, :, :], 0.0).then_inc(zeroed, 1)
            pool.wait_ge(zeroed, 2)
            pool.wait_ge(w_lo_ready, 3)
            pool.memset(b["v"][:, :, :, DH:DH + 1], 1.0).then_inc(b["consts_ready"], 1)
            pool.wait_ge(b["consts_ready"], 1)
            pool.memset(b["k_op"][64:66, :, :].bitcast(F32), 1.0).then_inc(b["consts_ready"], 1)
            pool.wait_ge(b["consts_ready"], 2)
            pool.memset(b["q_op"][64:OPERAND, :, :, :].bitcast(F32), 0.0).then_inc(b["consts_ready"], 1)
            pool.wait_ge(hi_ready, 4)
            stack_queries(pool, b, 0, range(0, 2), b["first_q_loaded"])
            pool.wait_ge(b["consts_ready"], 3)
            for n in range(3, 6):
                split_lo(n)
            pool.wait_ge(w_lo_ready, 6)

        @block.vector
        def _(dve):
            chain = Chain(dve, chain_sem)

            def split_hi(n):
                piece, load = pieces[n]
                dve.wait_ge(loaded[load], 16)
                dve.tensor_copy(hi_of(n), piece).then_inc(w_hi_ready, 1)

            ln.vector_all(dve, chain, rows, lambda: [split_hi(n) for n in range(3)],
                          lambda: [split_hi(n) for n in range(3, 6)])
            dve.wait_ge(b["consts_ready"], 1)
            n = 0
            for u, (w, h) in enumerate(units):
                if w == V:
                    dve.wait_ge(v_turned, h + 1)
                    dve.tensor_copy(b["v"][:, 4 * h:4 * h + 4, :, 0:DH],
                                    v_ps[:, :].rearrange("p (i g e) -> p i g e", i=4, g=GROUPS)).then_inc(v_ready, 1)
                    continue
                dve.wait_ge(hi_ready, u + 1)
                dve.scalar_tensor_tensor(out=target(w, h, 1), in0=out_ps[u % 3][:, :], scalar=bias(w),
                                         in1=target(w, h, 0).bitcast(F32), op0=ALU.add, op1=ALU.subtract)\
                   .then_inc(lo_ready, 1)
                n += 1
            dve.wait_ge(lo_ready, n)
            dve.wait_ge(v_ready, 2)

        @block.scalar
        def _(act):
            for i in range(4):
                ln.scalar_hi(act, i)
            rows.scalar_std(act, range(4, 8), 4)
            for i in range(4, 8):
                ln.scalar_hi(act, i)
            for u, (w, h) in enumerate(units):
                act.wait_ge(projected, u + 1)
                out = vT[:, h * HALF:(h + 1) * HALF] if w == V else target(w, h, 0)
                act.activation(out, out_ps[u % 3][:, :], ACT.Identity, bias=bias(w)).then_inc(hi_ready, 1)

        @block.tensor
        def _(pe):
            def turn_v(h):
                pe.wait_ge(hi_ready, 4 + h + 1)
                if h:
                    pe.wait_ge(v_ready, h)
                for i in range(4):
                    t = slice((4 * h + i) * P, (4 * h + i + 1) * P)
                    last = pe.transpose(v_ps[:, i * P:(i + 1) * P], vT[:, t], core.ident[:, :])
                last.then_inc(v_turned, 1)

            for i in range(4):
                ln.tensor_turn(pe, i)
            for u, (w, h) in enumerate(units):
                if u == 1:
                    for i in range(4, 8):
                        ln.tensor_turn(pe, i)
                pe.wait_ge(ln.lo_ready, 4 * h + 4)
                pe.wait_ge(w_lo_ready, w + 1)
                if u >= 3:
                    pe.wait_ge(lo_ready, u - 2)
                for k in range(dk):
                    last = parts_matmul(pe, out_ps[u % 3][:, :], (w_hi[:, w, k, :], w_lo[:, w, k, :]),
                                        ln.columns(k, h * HALF, HALF), start=(k == 0), stop=(k == dk - 1))
                last.then_inc(projected, 1)
            turn_v(0)
            turn_v(1)


def phase_gqa_core(core, scope, b, d, ffn_loaded):
    nc, tiles = core.nc, core.tiles
    sb = lambda what, shape, dt: scope.enter_context(nc.sbuf_tensor(f"g_{what}", shape, dt))
    sem = lambda what: core.sem(f"g_{what}")
    STAGES, UNITS, RING = 2 * GROUPS, tiles, 3
    SCALE = 0.25 * LN2
    prob = sb("prob", [P, 2, PER, HALF], F32)
    b["q_op_odd"] = sb("q_op_odd", [OPERAND, 2, PER, HALF], F32R)
    q_op = (b["q_op"], b["q_op_odd"])
    neg_part = sb("neg_part", [P, 2, 16], F32)
    neg_max = sb("neg_max", [P, 2, 16], F32)
    ob_row = sb("ob_row", [P, HALF], F32)
    maxT_hi, maxT_lo = (sb(f"maxT_{s}", [16, 2, P], F32R) for s in ("hi", "lo"))
    mixT = sb("mixT", [P, HALF], F32)
    den_inv = sb("den_inv", [P, 16], F32)
    S_ps = [scope.enter_context(nc.psum_tensor(f"g_S{i}", [P, HALF], F32)) for i in range(RING)]
    E_ps = [scope.enter_context(nc.psum_tensor(f"g_E{i}", [P, HALF], F32)) for i in range(RING)]
    mix_ps = scope.enter_context(nc.psum_tensor("g_mix", [P, HALF], F32))
    turn_ps = scope.enter_context(nc.psum_tensor("g_turn", [P, HALF], F32))
    q_loaded = b["q_loaded"]
    projected, hi_ready, lo_ready = sem("projected"), sem("hi_ready"), sem("lo_ready")
    m_loaded = [sem(f"m_loaded{s}") for s in range(2)]
    rows_zeroed, scored, part_ready = sem("rows_zeroed"), sem("scored"), sem("part_ready")
    max_ready = sem("max_ready")
    max_turned, maxT_ready, maxT_hi_ready = sem("max_turned"), sem("maxT_ready"), sem("maxT_hi_ready")
    keyed, exp_ready, mixed, mixT_ready = sem("keyed"), sem("exp_ready"), sem("mixed"), sem("mixT_ready")
    mix_turned, inv_ready, o_ready = sem("mix_turned"), sem("inv_ready"), sem("o_ready")
    ob_loaded, x_biased = sem("ob_loaded"), sem("x_biased")
    LEAD = UNITS + 2
    SLOTS = STAGES * UNITS + LEAD + 1
    turns_maxima = lambda s: s // UNITS - 1 if s % UNITS == 0 and 1 <= s // UNITS <= STAGES else -1
    turns_mix = lambda s: (s - LEAD - 2) // UNITS - 1 if (s - LEAD - 2) % UNITS == 0 else -1

    dk = core.dk
    PROJECTIONS = 2 * (dk - 1)
    projects = lambda s, j: 3 * s + j if j < 3 and 3 * s + j < PROJECTIONS * dk else -1
    splits = lambda s: [x for x in range(PROJECTIONS) if (dk * x + dk - 1) // 3 + 1 == s]
    q_target = lambda x, part: b["qT"][part][:, 1 + x // 2, x % 2 * HALF:(x % 2 + 1) * HALF]
    q_bias = lambda x: core.bias_cols[:, 21 + x // 2:22 + x // 2]

    with nc.Block() as block:
        @block.sync
        def _(sp):
            def load_queries(g):
                slot = g % 2
                if g >= 2:
                    sp.wait_ge(keyed, PER * UNITS * 2 * (g - 1))
                    sp.wait_ge(lo_ready, 2 * (g // 2))
                stack_queries(sp, b, g, range(4), q_loaded[slot])
                if g >= 2:
                    sp.dma_start(q_op[slot][64:66].bitcast(F32), q_op[slot][66:68].bitcast(F32))\
                      .then_inc(q_loaded[slot], 16)

            def load_maxima(n):
                slot, half = n // 2 % 2, n % 2
                sp.wait_ge(maxT_ready, n + 1)
                for r, part in enumerate((maxT_hi, maxT_lo)):
                    sp.dma_start(q_op[slot][64 + r:65 + r, half, :, :].bitcast(F32).rearrange("p j t -> p (j t)"),
                                 part[:, n % 2, :].bitcast(F32)).then_inc(m_loaded[n % 2], 16)

            for g in range(1, GROUPS):
                stack_keys(sp, b, g, b["k_loaded"])
            sp.dma_start(ob_row[:, :], d["bias_rows"][0:1, 1536:2048].broadcast_to([P, HALF])).then_inc(ob_loaded, 16)
            for n in range(STAGES):
                load_maxima(n)
                if n == 0:
                    sp.wait_ge(b["k_loaded"], 16 * 4 * (GROUPS - 1))
                    load_queries(1)
                elif n == 1:
                    sp.wait_ge(rows_zeroed, 1)
                elif n % 2 == 0 and n // 2 + 1 < GROUPS:
                    load_queries(n // 2 + 1)
                if n == 2:
                    load_ffn_weights(core, sp, d, ffn_loaded, pieces=(0, 1))

        @block.gpsimd
        def _(pool):
            pool.wait_ge(b["k_loaded"], 16 * 4 * (GROUPS - 1))
            pool.memset(q_op[1][64:OPERAND].bitcast(F32), 0.0).then_inc(rows_zeroed, 1)
            pool.wait_ge(rows_zeroed, 1)
            pool.wait_ge(ob_loaded, 16)
            for i in range(tiles):
                pool.tensor_tensor(core.x[:, i, :], core.x[:, i, :], ob_row[:, :], ALU.add).then_inc(x_biased, 1)
            pool.wait_ge(x_biased, tiles)

        @block.tensor
        def _(pe):
            def score(m):
                n, t = m // 32, m % 32
                g, half, i, j, h = n // 2, n % 2, t // 8, t // 2 % PER, t % 2
                if t == 0:
                    if n == 0:
                        pe.wait_ge(b["first_k_loaded"], 16 * 4)
                        pe.wait_ge(b["first_q_loaded"], 16 * 8)
                    elif n == 2:
                        pe.wait_ge(rows_zeroed, 1)
                        pe.wait_ge(b["k_loaded"], 16 * 4 * (GROUPS - 1))
                    slot_loads = [16 * (8 if k == 0 else 16 if k == 1 else 17) for k in range(GROUPS)]
                    pe.wait_ge(q_loaded[g % 2], sum(slot_loads[g % 2:g + 1:2]))
                if m >= RING:
                    pe.wait_ge(part_ready, m - RING + 1)
                pe.matmul(S_ps[m % RING][:, :], q_op[g % 2][:, half, j, i * P:(i + 1) * P],
                          b["k_op"][:, g, h * HALF:(h + 1) * HALF], start=True, stop=True).then_inc(scored, 1)

            def project(c):
                x, k = c // dk, c % dk
                w, h = x // 2, x % 2
                if x >= RING and k == 0:
                    pe.wait_ge(lo_ready, x - RING + 1)
                t = slice(h * HALF, (h + 1) * HALF)
                last = parts_matmul(pe, E_ps[x % RING][:, :], (b["qw"][0][:, w, k, :], b["qw"][1][:, w, k, :]),
                                    (b["xT"][0][:, k, t], b["xT"][1][:, k, t]), start=(k == 0), stop=(k == dk - 1))
                if k == dk - 1:
                    last.then_inc(projected, 1)

            def key_scores(n, u, j):
                g, half = n // 2, n % 2
                e = PER * (UNITS * n + u) + j
                if u == 0 and j == 0:
                    pe.wait_ge(m_loaded[n % 2], 32 * (n // 2 + 1))
                if e == 0:
                    pe.wait_ge(lo_ready, PROJECTIONS)
                if e >= RING:
                    pe.wait_ge(exp_ready, e - RING + 1)
                pe.matmul(E_ps[e % RING][:, :], b["k_op"][:, g, u * P:(u + 1) * P], q_op[g % 2][:, half, j, :],
                          start=True, stop=True).then_inc(keyed, 1)

            def mix(k):
                n, u = k // UNITS, k % UNITS
                pe.wait_ge(exp_ready, PER * (k + 1))
                if u == 0 and n >= 1:
                    pe.wait_ge(mixT_ready, n)
                for j in range(PER):
                    last = pe.matmul(mix_ps[32 * j:32 * j + 32, :], b["v"][:, u, n // 2, :], prob[:, k % 2, j, :],
                                     start=(u == 0), stop=(u == UNITS - 1), skip_group_check=True)
                last.then_inc(mixed, 1)

            def turn_maxima(n):
                pe.wait_ge(max_ready, n + 1)
                if n >= 2:
                    pe.wait_ge(o_ready, n - 1)
                pe.transpose(turn_ps[0:16, 0:P], neg_max[:, n % 2, :], core.ident[:, :]).then_inc(max_turned, 1)

            def turn_mix(n):
                pe.wait_ge(mixT_ready, n + 1)
                pe.wait_ge(maxT_ready, min(n + 2, STAGES))
                if n >= 1:
                    pe.wait_ge(o_ready, n)
                for i in range(4):
                    last = pe.transpose(turn_ps[:, i * P:(i + 1) * P], mixT[:, i * P:(i + 1) * P], core.ident[:, :])
                last.then_inc(mix_turned, 1)

            for s in range(SLOTS):
                k = s - LEAD
                keys = 0 <= k < STAGES * UNITS
                queries = s < STAGES * UNITS
                for j in range(PER):
                    if keys:
                        key_scores(k // UNITS, k % UNITS, j)
                    if queries:
                        score(PER * s + j)
                    if projects(s, j) >= 0:
                        project(projects(s, j))
                    if j == 2 and turns_maxima(s) >= 0:
                        turn_maxima(turns_maxima(s))
                if k >= 1:
                    mix(k - 1)
                if turns_mix(s) >= 0:
                    turn_mix(turns_mix(s))
            turn_mix(STAGES - 1)

        @block.scalar
        def _(act):
            for x in range(PROJECTIONS):
                act.wait_ge(projected, x + 1)
                act.activation(q_target(x, 0), E_ps[x % RING][:, :], ACT.Identity, bias=q_bias(x)).then_inc(hi_ready, 1)
            act.wait_ge(lo_ready, PROJECTIONS)
            for n in range(STAGES):
                for u in range(UNITS):
                    for j in range(PER):
                        k = UNITS * n + u
                        e = PER * k + j
                        act.wait_ge(keyed, e + 1)
                        if k >= 2 and j == 0:
                            act.wait_ge(mixed, k - 1)
                        act.activation(prob[:, k % 2, j, :], E_ps[e % RING][:, :], ACT.Exp, scale=SCALE)\
                           .then_inc(exp_ready, 1)
                    if u == 0 and n >= 1:
                        act.wait_ge(mixed, UNITS * n)
                        if n >= 2:
                            act.wait_ge(mix_turned, n - 1)
                        act.copy(mixT[:, :], mix_ps[:, :]).then_inc(mixT_ready, 1)
            act.wait_ge(mixed, UNITS * STAGES)
            act.wait_ge(mix_turned, STAGES - 1)
            act.copy(mixT[:, :], mix_ps[:, :]).then_inc(mixT_ready, 1)

        @block.vector
        def _(dve):
            def maximum(m):
                n, t = m // 32, m % 32
                i, j, h = t // 8, t // 2 % PER, t % 2
                dve.wait_ge(scored, m + 1)
                if t == 0 and n >= 1:
                    dve.wait_ge(max_ready, n)
                at = PER * j + i
                dve.tensor_reduce(neg_part[:, h, at:at + 1], S_ps[m % RING][:, :], AX_X, ALU.max,
                                  negate=True).then_inc(part_ready, 1)
                if t == 31:
                    dve.wait_ge(part_ready, 32 * (n + 1))
                    if n >= 2:
                        dve.wait_ge(max_turned, n - 1)
                    dve.tensor_tensor(neg_max[:, n % 2, :], neg_part[:, 0, :], neg_part[:, 1, :], ALU.min)\
                       .then_inc(max_ready, 1)

            def split_q(x):
                dve.wait_ge(hi_ready, x + 1)
                dve.scalar_tensor_tensor(out=q_target(x, 1), in0=E_ps[x % RING][:, :], scalar=q_bias(x),
                                         in1=q_target(x, 0).bitcast(F32), op0=ALU.add, op1=ALU.subtract)\
                   .then_inc(lo_ready, 1)

            def maxima_out(n):
                dve.wait_ge(max_turned, n + 1)
                if n >= 2:
                    dve.wait_ge(m_loaded[n % 2], 32 * (n // 2))
                hi, lo = maxT_hi[:, n % 2, :], maxT_lo[:, n % 2, :]
                dve.tensor_copy(hi, turn_ps[0:16, 0:P]).then_inc(maxT_hi_ready, 1)
                dve.wait_ge(maxT_hi_ready, n + 1)
                dve.tensor_tensor(lo, turn_ps[0:16, 0:P], hi.bitcast(F32), ALU.subtract).then_inc(maxT_ready, 1)

            def normalise(n):
                g, half = n // 2, n % 2
                dve.wait_ge(mix_turned, n + 1)
                v = turn_ps[:, :].rearrange("p (i j e) -> p i j e", i=4, e=32)
                dve.reciprocal(den_inv[:, :], turn_ps[:, :].rearrange("p (a e) -> p a e", e=32)[:, :, DH])\
                   .then_inc(inv_ready, 1)
                dve.wait_ge(inv_ready, n + 1)
                out = b["o"][:, 4 * half:4 * half + 4, PER * DH * g:PER * DH * (g + 1)]
                inv = den_inv[:, :].rearrange("p (i j) -> p i j", j=PER)
                dve.tensor_tensor(out.rearrange("p i (j e) -> p i j e", e=DH), v[:, :, :, 0:DH], bcast(inv, DH),
                                  ALU.mult).then_inc(o_ready, 1)

            for s in range(SLOTS):
                for j in range(PER):
                    if s < STAGES * UNITS:
                        maximum(PER * s + j)
                    if j == 1:
                        for x in splits(s):
                            split_q(x)
                        if turns_maxima(s) >= 0:
                            maxima_out(turns_maxima(s))
                if turns_mix(s) >= 0:
                    normalise(turns_mix(s))
            normalise(STAGES - 1)
            dve.wait_ge(o_ready, STAGES)


def phase_gqa_output(core, scope, b, d, loaded, ffn_loaded):
    nc, tiles, dk = core.nc, core.tiles, core.dk
    sb = lambda what, shape, dt: scope.enter_context(nc.sbuf_tensor(f"o_{what}", shape, dt))
    ps = lambda what: scope.enter_context(nc.psum_tensor(f"o_{what}", [P, HALF], F32))
    sem = lambda what: core.sem(f"o_{what}")
    w_hi, w_lo = (sb(f"w_{s}", [P, dk, HALF], F32R) for s in ("hi", "lo"))
    o = b["o"]
    oT_hi, oT_lo = b["qT"]
    turn_ps = [ps(f"turn{i}") for i in range(4)]
    out_ps = [ps(f"out{i}") for i in range(4)]
    w_hi_ready, w_lo_ready, turned = sem("w_hi"), sem("w_lo"), sem("turned")
    hi_ready, lo_ready, projected, residual = sem("hi_ready"), sem("lo_ready"), sem("projected"), sem("residual")
    raw = core.raw[:, RAW_O:RAW_O + 2048].rearrange("p (k n) -> p k n", k=dk)
    view = lambda i: turn_ps[i % 4][:, :].rearrange("p (k t) -> p k t", t=P)
    rows = RowStats(core, "o")
    chain_sem = sem("chain")

    with nc.Block() as block:
        @block.sync
        def _(sp):
            sp.wait_ge(w_lo_ready, dk)
            load_ffn_weights(core, sp, d, ffn_loaded, pieces=(2,))

        @block.gpsimd
        def _(pool):
            for k in range(dk):
                pool.wait_ge(w_hi_ready, k + 1)
                pool.tensor_tensor(w_lo[:, k, :], raw[:, k, :], w_hi[:, k, :].bitcast(F32), ALU.subtract)\
                    .then_inc(w_lo_ready, 1)

        @block.tensor
        def _(pe):
            def turn(i):
                if i >= 4:
                    pe.wait_ge(lo_ready, i - 3)
                for k in range(dk):
                    last = pe.transpose(turn_ps[i % 4][:, k * P:(k + 1) * P], o[:, i, k * P:(k + 1) * P],
                                        core.ident[:, :])
                last.then_inc(turned, 1)

            for i in range(4):
                turn(i)
            for i in range(tiles):
                pe.wait_ge(lo_ready, i + 1)
                if i >= 4:
                    pe.wait_ge(residual, i - 3)
                t = slice(i * P, (i + 1) * P)
                for k in range(dk):
                    pe.wait_ge(w_lo_ready, k + 1)
                    last = parts_matmul(pe, out_ps[i % 4][:, :], (oT_hi[:, k, t], oT_lo[:, k, t]),
                                        (w_hi[:, k, :], w_lo[:, k, :]), start=(k == 0), stop=(k == dk - 1))
                last.then_inc(projected, 1)
                if i + 4 < tiles:
                    turn(i + 4)

        @block.scalar
        def _(act):
            for i in range(tiles):
                act.wait_ge(turned, i + 1)
                act.copy(oT_hi[:, :, i * P:(i + 1) * P], view(i)).then_inc(hi_ready, 1)
            rows.scalar_std(act, range(0, 4), 4)

        @block.vector
        def _(dve):
            dve.wait_ge(loaded[3], 16)
            for k in range(dk):
                dve.tensor_copy(w_hi[:, k, :], raw[:, k, :]).then_inc(w_hi_ready, 1)
            for i in range(tiles):
                t = slice(i * P, (i + 1) * P)
                dve.wait_ge(hi_ready, i + 1)
                dve.tensor_tensor(oT_lo[:, :, t], view(i), oT_hi[:, :, t].bitcast(F32), ALU.subtract)\
                   .then_inc(lo_ready, 1)
                if i >= 4:
                    dve.wait_ge(projected, i - 3)
                    dve.tensor_tensor(core.x[:, i - 4, :], out_ps[i % 4][:, :], core.x[:, i - 4, :], ALU.add)\
                       .then_inc(residual, 1)
            chain = Chain(dve, chain_sem)
            dve.wait_ge(residual, 4)
            rows.vector_stats(dve, chain, range(0, 4))
            for i in range(tiles - 4, tiles):
                dve.wait_ge(projected, i + 1)
                dve.tensor_tensor(core.x[:, i, :], out_ps[i % 4][:, :], core.x[:, i, :], ALU.add)\
                   .then_inc(residual, 1)
                if i == 5:
                    rows.vector_rstd(dve, chain, range(0, 4))
            dve.wait_ge(residual, tiles)


def hybrid_layer(nc, d, out, T, D, until=99):
    out_dram = out.rearrange("o (i p) d -> (o i) p d", p=P)
    with ExitStack() as ctx:
        core = Core(nc, ctx, T, D)
        ffn1_loaded = [core.lasting_sem(f"ffn1_loaded{s}") for s in range(3)]
        ffn2_loaded = [core.lasting_sem(f"ffn2_loaded{s}") for s in range(3)]
        gqa_loaded = [core.lasting_sem(f"gqa_loaded{s}") for s in range(4)]
        stored = core.lasting_sem("stored")
        with ExitStack() as a:
            t = lambda name, shape: a.enter_context(nc.sbuf_tensor(name, shape, F32R))
            wa = {"qkv_hi": t("qkv_hi", [P, 3, 1024]), "qkv_lo": t("qkv_lo", [P, 3, 1024]),
                  "wo_hi": t("wo_hi", [P, 1024]), "wo_lo": t("wo_lo", [P, 1024]),
                  "pw_hi": t("pw_hi", [P, D]), "pw_lo": t("pw_lo", [P, D])}
            wa |= {name: a.enter_context(nc.sbuf_tensor(name, [P, n], F32)) for name, n in
                   (("bv_row", 1024), ("pb_row", D))}
            wa = {k: v[:] for k, v in wa.items()}
            qkvT = (t("qkvT_hi", [P, 3, T]), t("qkvT_lo", [P, 3, T]))
            with ExitStack() as scope:
                phase_conv(core, scope, qkvT, wa, d)
                core.end_phase()
            with ExitStack() as scope:
                phase_block_attention(core, scope, qkvT, wa, d, ffn1_loaded)
                core.end_phase()
        if until > 1:
            with ExitStack() as scope:
                phase_ffn(core, scope, "f1", ffn1_loaded,
                          after_split=lambda sp: load_gqa_weights(core, sp, d, gqa_loaded))
                core.end_phase()
        if until > 2:
            with ExitStack() as outer:
                t = lambda name, shape, dt: outer.enter_context(nc.sbuf_tensor(name, shape, dt))
                b = {"v": t("b_v", [P, core.tiles, GROUPS, 32], F32), "k_op": t("b_k_op", [OPERAND, GROUPS, T], F32R),
                     "qT": (t("b_qT_hi", [P, core.dk, T], F32R), t("b_qT_lo", [P, core.dk, T], F32R)),
                     "qw": [t(f"b_qw_{s}", [P, core.dk - 1, core.dk, P], F32R) for s in ("hi", "lo")],
                     "q_op": t("b_q_op", [OPERAND, 2, PER, HALF], F32R),
                     "first_k_loaded": core.lasting_sem("first_k_loaded"),
                     "first_q_loaded": core.lasting_sem("first_q_loaded"),
                     "k_loaded": core.lasting_sem("k_loaded"),
                     "q_loaded": [core.lasting_sem(f"q_loaded{s}") for s in range(2)]}
                with ExitStack() as scope:
                    b["xT"] = [scope.enter_context(nc.sbuf_tensor(f"b_xT_{s}", [P, core.dk, T], F32R))
                               for s in ("hi", "lo")]
                    phase_gqa_projections(core, scope, b, gqa_loaded)
                    core.end_phase()
                b["o"] = t("b_o", [P, core.tiles, D], F32)
                with ExitStack() as scope:
                    phase_gqa_core(core, scope, b, d, ffn2_loaded)
                    core.end_phase()
                with ExitStack() as scope:
                    phase_gqa_output(core, scope, b, d, gqa_loaded, ffn2_loaded)
                    core.end_phase()
        if until > 3:
            with ExitStack() as scope:
                phase_ffn(core, scope, "f2", ffn2_loaded, store=(stored, out_dram))
                core.end_phase()
        else:
            with nc.Block() as block:
                @block.sync
                def _(sp):
                    for i in range(core.tiles):
                        sp.dma_start(out_dram[i], core.x[:, i, :]).then_inc(stored, 16)
                    sp.wait_ge(stored, 16 * core.tiles)


def kernel(**inputs):
    import numpy as np

    import concourse.bacc as bacc
    from concourse.bass_utils import run_bass_kernel_spmd

    w = {name: np.asarray(a) for name, a in inputs.items()}
    x = w["L0_attn_a_inputs"]
    A, B = w["L0_ffn_A"], w["L0_ffn_B"]
    D = x.shape[-1]
    a, g = "L0_attn_a_", "L0_attn_b_"
    columns = [w[a + "conv_b"], w[a + "bq"], w[a + "bk"], w[a + "bo"], w[g + "q_b"], w[g + "k_b"], w[g + "v_b"]]
    rows = [w[a + "bv"], w[a + "proj_b"], w[g + "o_b"]]
    arrays = {
        "x": x,
        "conv_w": w[a + "conv_w"],
        "wq": w[a + "wq"],
        "wk": w[a + "wk"],
        "wv": w[a + "wv"],
        "wo": w[a + "wo"],
        "proj_w": w[a + "proj_w"],
        "bias_cols": np.concatenate([c.reshape(-1, P) for c in columns]).T,
        "bias_rows": np.concatenate([r.reshape(1, -1) for r in rows], axis=1),
        "WrT": w["L0_ffn_Wr"].T,
        "AT": A.reshape(-1, D).T,
        "Bm": B.transpose(0, 2, 1).reshape(-1, D),
        "qwT": w[g + "q_w"].T,
        "kwT": w[g + "k_w"].T,
        "vwT": w[g + "v_w"].T,
        "owT": w[g + "o_w"].T,
    }
    arrays = {"in_" + name: np.ascontiguousarray(v) for name, v in arrays.items()}
    nc = bacc.Bacc("TRN2", target_bir_lowering=False, num_devices=1)
    d = {name[3:]: nc.dram_tensor(name, v.shape, mybir.dt.from_np(v.dtype), kind="ExternalInput").ap()
         for name, v in arrays.items()}
    out = nc.dram_tensor("out", x.shape, F32, kind="ExternalOutput").ap()
    hybrid_layer(nc, d, out, x.shape[1], D)
    result = run_bass_kernel_spmd(nc, [arrays], core_ids=[0])
    return result.results[0]["out"]
```

```python
from contextlib import ExitStack

import concourse.bass as bass
from concourse import mybir

F32 = mybir.dt.float32
F32R = mybir.dt.float32r
BF16 = mybir.dt.bfloat16
ALU = mybir.AluOpType
ACT = mybir.ActivationFunctionType
AX_X = mybir.AxisListType.X

P = 128
HALF = 512
EPS = 1e-5
LN2 = 0.6931471805599453


def bcast(ap, n):
    return ap.unsqueeze(len(ap.shape)).broadcast_to([*ap.shape, n])


def parts_matmul(pe, out, stationary, moving, start, stop):
    pe.matmul(out, stationary[1], moving[0], start=start, stop=False)
    pe.matmul(out, stationary[0], moving[1], start=False, stop=False)
    return pe.matmul(out, stationary[0], moving[0], start=False, stop=stop)


class Core:

    def __init__(self, nc, ctx, T, D):
        self.nc, self.ctx = nc, ctx
        self.T, self.D, self.tiles, self.dk = T, D, T // P, D // P
        self.x = ctx.enter_context(nc.sbuf_tensor("x", [P, self.tiles, D], F32))
        self.ident = ctx.enter_context(nc.sbuf_tensor("ident", [P, P], F32))
        self.eps = ctx.enter_context(nc.sbuf_tensor("eps", [P, 1], F32))
        self.bias_cols = ctx.enter_context(nc.sbuf_tensor("bias_cols", [P, 26], F32))
        self.raw = ctx.enter_context(nc.sbuf_tensor("raw", [P, 8448], F32))
        self.stats = ctx.enter_context(nc.sbuf_tensor("stats", [P, self.tiles, 6], F32))
        self.mv = ctx.enter_context(nc.sbuf_tensor("mv", [P, self.tiles, 2], F32))
        self.std = ctx.enter_context(nc.sbuf_tensor("std", [P, self.tiles], F32))
        self.rstd = ctx.enter_context(nc.sbuf_tensor("rstd", [P, self.tiles], F32))

        self.phase_sems = []

    def lasting_sem(self, name):
        return self.ctx.enter_context(self.nc.semaphore(name))

    def sem(self, name):
        self.phase_sems.append(self.nc.alloc_semaphore(name=name))
        return self.phase_sems[-1]

    def end_phase(self):
        self.nc.clear_and_free_semaphores(self.phase_sems)
        self.nc.all_engine_barrier()
        self.phase_sems = []


class Chain:

    def __init__(self, engine, semaphore):
        self.engine, self.semaphore, self.count = engine, semaphore, 0

    def link(self, instruction):
        self.count += 1
        instruction.then_inc(self.semaphore, 1)
        self.engine.wait_ge(self.semaphore, self.count)


class RowStats:

    def __init__(self, core, name):
        self.core, self.groups = core, 0
        self.stats_ready = core.sem(name + "_stats_ready")
        self.std_ready = core.sem(name + "_std_ready")

    def vector_stats(self, dve, chain, tiles, x_loaded=None):
        core = self.core
        for i in tiles:
            if x_loaded is not None:
                dve.wait_ge(x_loaded[i], 16)
            dve.bn_stats(core.stats[:, i, :], core.x[:, i, :]).then_inc(chain.semaphore, 1)
            chain.count += 1
        dve.wait_ge(chain.semaphore, chain.count)
        for i in tiles:
            dve.bn_aggr(core.mv[:, i, :], core.stats[:, i, :]).then_inc(self.stats_ready, 1)

    def scalar_std(self, act, tiles, count):
        core, a, b = self.core, tiles[0], tiles[-1] + 1
        act.wait_ge(self.stats_ready, count)
        act.activation(core.std[:, a:b], core.mv[:, a:b, 1], ACT.Sqrt, bias=core.eps[:, 0:1])\
           .then_inc(self.std_ready, 1)

    def vector_rstd(self, dve, chain, tiles):
        core, a, b = self.core, tiles[0], tiles[-1] + 1
        self.groups += 1
        dve.wait_ge(self.std_ready, self.groups)
        chain.link(dve.reciprocal(core.rstd[:, a:b], core.std[:, a:b]))


class LayerNorm:

    def __init__(self, core, scope, name, pad, banks, xT=None):
        nc = core.nc
        name += "_ln"
        self.core, self.pad, self.banks = core, pad, banks
        width = core.T + 2 * pad
        if xT is None:
            xT = [scope.enter_context(nc.sbuf_tensor(f"{name}_xT_{s}", [P, core.dk, width], F32R))
                  for s in ("hi", "lo")]
        self.hi, self.lo = xT
        self.xn = scope.enter_context(nc.sbuf_tensor(name + "_xn", [P, 2, core.D], F32))
        self.xn_ready = core.sem(name + "_xn_ready")
        self.turned = core.sem(name + "_turned")
        self.hi_ready = core.sem(name + "_hi_ready")
        self.lo_ready = core.sem(name + "_lo_ready")

    def turned_view(self, i):
        return self.banks[i % len(self.banks)][:, :].rearrange("p (k t) -> p k t", t=P)

    def part(self, which, i):
        a = self.pad + i * P
        return which[:, :, a:a + P]

    def columns(self, k, start, n):
        a = self.pad + start
        return self.hi[:, k, a:a + n], self.lo[:, k, a:a + n]

    def vector_all(self, dve, chain, rows, early=None, middle=None, late=None,
                   x_loaded=None):
        if x_loaded is not None:
            rows.vector_stats(dve, chain, range(0, 4), x_loaded)
            rows.vector_rstd(dve, chain, range(0, 4))
        self.vector_xn(dve, 0)
        self.vector_xn(dve, 1)
        if early is not None:
            early()
        self.vector_xn(dve, 2)
        self.vector_lo(dve, 0)
        self.vector_xn(dve, 3)
        for i in range(1, 4):
            self.vector_lo(dve, i)
        rows.vector_stats(dve, chain, range(4, 8), x_loaded)
        rows.vector_rstd(dve, chain, range(4, 8))
        self.vector_xn(dve, 4)
        self.vector_xn(dve, 5)
        if middle is not None:
            middle()
        for i in range(4, 8):
            if i == 6 and late is not None:
                late()
            self.vector_lo(dve, i)
            if i + 2 < 8:
                self.vector_xn(dve, i + 2)

    def vector_xn(self, dve, i):
        if i >= 2:
            dve.wait_ge(self.turned, i - 1)
        dve.tensor_scalar(self.xn[:, i % 2, :], self.core.x[:, i, :], self.core.mv[:, i, 0:1],
                          self.core.rstd[:, i:i + 1], ALU.subtract, ALU.mult).then_inc(self.xn_ready, 1)

    def vector_lo(self, dve, i):
        dve.wait_ge(self.hi_ready, i + 1)
        dve.tensor_tensor(self.part(self.lo, i), self.turned_view(i),
                          self.part(self.hi, i).bitcast(F32), ALU.subtract).then_inc(self.lo_ready, 1)

    def tensor_turn(self, pe, i):
        pe.wait_ge(self.xn_ready, i + 1)
        if i >= len(self.banks):
            pe.wait_ge(self.lo_ready, i - len(self.banks) + 1)
        for k in range(self.core.dk):
            last = pe.transpose(self.banks[i % len(self.banks)][:, k * P:(k + 1) * P],
                                self.xn[:, i % 2, k * P:(k + 1) * P], self.core.ident[:, :])
        last.then_inc(self.turned, 1)

    def scalar_hi(self, act, i):
        act.wait_ge(self.turned, i + 1)
        act.copy(self.part(self.hi, i), self.turned_view(i)).then_inc(self.hi_ready, 1)


def phase_conv(core, scope, qkvT, wa, d):
    nc, tiles, dk = core.nc, core.tiles, core.dk
    sb = lambda name, shape, dt: scope.enter_context(nc.sbuf_tensor(name, shape, dt))
    TAPS, M3 = 3, 3
    conv_raw = core.raw[:, 0:TAPS * dk * M3 * P].rearrange("p (s k m) -> p s k m", s=TAPS, k=dk)
    qkv_raw = core.raw[:, 4608:4608 + 3 * 1024].rearrange("p (s n) -> p s n", s=3)
    conv_hi = sb("conv_hi", [P, TAPS, dk, M3 * P], F32R)
    conv_lo = sb("conv_lo", [P, TAPS, dk, M3 * P], F32R)
    out_raw = sb("out_raw", [P, 1536], F32)
    banks = [scope.enter_context(nc.psum_tensor(f"c_turn{i}", [P, HALF], F32)) for i in range(4)]
    conv_ps = [scope.enter_context(nc.psum_tensor(f"c_conv{i}", [P, HALF], F32)) for i in range(4)]
    ln = LayerNorm(core, scope, "c", 1, banks)
    rows = RowStats(core, "c")
    x_loaded = [core.sem(f"x_loaded{i}") for i in range(tiles)]
    conv_loaded = [core.sem(f"conv_loaded{s}") for s in range(TAPS)]
    small_loaded = core.sem("small_loaded")
    proj_loaded = core.sem("proj_loaded")
    rows_loaded = core.sem("rows_loaded")
    consts_ready = core.sem("consts_ready")
    ident_zeroed = core.sem("ident_zeroed")
    pads_ready = core.sem("c_pads_ready")
    conv_hi_ready = core.sem("conv_hi_ready")
    conv_lo_ready = core.sem("conv_lo_ready")
    projw_hi_ready = core.sem("projw_hi_ready")
    projw_lo_ready = core.sem("projw_lo_ready")
    convolved = core.sem("convolved")
    qkv_hi_ready = core.sem("qkv_hi_ready")
    qkv_lo_ready = core.sem("qkv_lo_ready")
    chain_sem = core.sem("c_chain")
    x_dram = d["x"].rearrange("o (i p) d -> (o i) p d", p=P)
    conv_dram = d["conv_w"].rearrange("s (k p) m -> s p k m", p=P)
    projw = [(qkv_raw[:, s, :], wa["qkv_hi"][:, s, :], wa["qkv_lo"][:, s, :]) for s in range(3)]
    projw += [(out_raw[:, 0:1024], wa["wo_hi"], wa["wo_lo"]), (out_raw[:, 1024:1536], wa["pw_hi"], wa["pw_lo"])]
    units = [(h, m) for h in range(2) for m in range(M3)]

    with nc.Block() as block:
        @block.sync
        def _(sp):
            for i in (0, 2):
                sp.dma_start(core.x[:, i, :], x_dram[i]).then_inc(x_loaded[i], 16)
            for s in range(TAPS):
                sp.dma_start(conv_raw[:, s], conv_dram[s]).then_inc(conv_loaded[s], 16)
                if s == 0:
                    for i in (4, 6):
                        sp.dma_start(core.x[:, i, :], x_dram[i]).then_inc(x_loaded[i], 16)
            sp.dma_start(core.bias_cols[:, :], d["bias_cols"]).then_inc(small_loaded, 16)
            for s, name in enumerate(("wq", "wk", "wv")):
                sp.dma_start(qkv_raw[:, s, :], d[name].rearrange("w h e -> w (h e)")).then_inc(proj_loaded, 16)
            sp.dma_start(out_raw[:, 0:1024].rearrange("p (c w) -> p c w", w=P),
                         d["wo"].rearrange("h e w -> (h e) w").rearrange("(c p) w -> p c w", p=P))\
              .then_inc(proj_loaded, 16)
            sp.dma_start(out_raw[:, 1024:1536], d["proj_w"]).then_inc(proj_loaded, 16)
            for dst, a, n in ((wa["bv_row"], 0, 1024), (wa["pb_row"], 1024, HALF)):
                sp.dma_start(dst, d["bias_rows"][0:1, a:a + n].broadcast_to([P, n])).then_inc(rows_loaded, 16)
            sp.wait_ge(rows_loaded, 32)

        @block.gpsimd
        def _(pool):
            pool.memset(core.ident[:, :], 0.0).then_inc(ident_zeroed, 1)
            pool.memset(core.eps[:, :], EPS).then_inc(consts_ready, 1)
            pool.wait_ge(ident_zeroed, 1)
            pool.affine_select(out=core.ident[:, :], in_=core.ident[:, :], compare_op=ALU.not_equal, fill=1.0,
                               base=0, pattern=[[-1, P]], channel_multiplier=1).then_inc(consts_ready, 1)
            for part in (ln.hi, ln.lo):
                for column in (0, core.T + 1):
                    pool.memset(part[:, :, column:column + 1].bitcast(F32), 0.0).then_inc(pads_ready, 1)
            for s in range(TAPS):
                for k in range(dk):
                    pool.wait_ge(conv_hi_ready, s * dk + k + 1)
                    pool.tensor_tensor(conv_lo[:, s, k, :], conv_raw[:, s, k, :],
                                       conv_hi[:, s, k, :].bitcast(F32), ALU.subtract).then_inc(conv_lo_ready, 1)
            for n, (raw, hi, lo) in enumerate(projw):
                pool.wait_ge(projw_hi_ready, n + 1)
                pool.tensor_tensor(lo, raw, hi.bitcast(F32), ALU.subtract).then_inc(projw_lo_ready, 1)
            pool.wait_ge(projw_lo_ready, len(projw))

        @block.vector
        def _(dve):
            chain = Chain(dve, chain_sem)
            ln.vector_all(dve, chain, rows, x_loaded=x_loaded)
            dve.wait_ge(proj_loaded, 16 * len(projw))
            for n, (raw, hi, lo) in enumerate(projw):
                dve.tensor_copy(hi, raw).then_inc(projw_hi_ready, 1)
            dve.wait_ge(small_loaded, 16)
            for u, (h, m) in enumerate(units):
                dve.wait_ge(qkv_hi_ready, u + 1)
                dve.scalar_tensor_tensor(
                    out=qkvT[1][:, m, h * HALF:(h + 1) * HALF], in0=conv_ps[u % 4][:, :],
                    scalar=core.bias_cols[:, m:m + 1], in1=qkvT[0][:, m, h * HALF:(h + 1) * HALF].bitcast(F32),
                    op0=ALU.add, op1=ALU.subtract).then_inc(qkv_lo_ready, 1)
            dve.wait_ge(qkv_lo_ready, len(units))

        @block.scalar
        def _(act):
            for i in range(1, tiles, 2):
                act.dma_start(core.x[:, i, :], x_dram[i]).then_inc(x_loaded[i], 16)
            act.wait_ge(consts_ready, 2)
            rows.scalar_std(act, range(0, 4), 4)
            for s in range(TAPS):
                act.wait_ge(conv_loaded[s], 16)
                for k in range(dk):
                    act.copy(conv_hi[:, s, k, :], conv_raw[:, s, k, :]).then_inc(conv_hi_ready, 1)
                if s == 0:
                    for i in range(0, 4):
                        ln.scalar_hi(act, i)
            rows.scalar_std(act, range(4, 8), 8)
            for i in range(4, tiles):
                ln.scalar_hi(act, i)
            act.wait_ge(small_loaded, 16)
            for u, (h, m) in enumerate(units):
                act.wait_ge(convolved, u + 1)
                act.activation(qkvT[0][:, m, h * HALF:(h + 1) * HALF], conv_ps[u % 4][:, :], ACT.Identity,
                               bias=core.bias_cols[:, m:m + 1]).then_inc(qkv_hi_ready, 1)
            act.wait_ge(qkv_hi_ready, len(units))

        @block.tensor
        def _(pe):
            pe.wait_ge(consts_ready, 2)
            for i in range(4):
                ln.tensor_turn(pe, i)
            turns_before = {(0, 2): 4, (1, 0): 5, (1, 1): 6, (1, 2): 7}
            for u, (h, m) in enumerate(units):
                if u >= 4:
                    pe.wait_ge(qkv_lo_ready, u - 3)
                pe.wait_ge(pads_ready, 4)
                for s in range(TAPS):
                    if (u, s) in turns_before:
                        ln.tensor_turn(pe, turns_before[u, s])
                    pe.wait_ge(ln.lo_ready, (4, 4, 5)[s] if h == 0 else tiles)
                    for k in range(dk):
                        pe.wait_ge(conv_lo_ready, s * dk + k + 1)
                        w = slice(m * P, (m + 1) * P)
                        last = parts_matmul(pe, conv_ps[u % 4][:, :],
                                            (conv_hi[:, s, k, w], conv_lo[:, s, k, w]),
                                            ln.columns(k, h * HALF + s - 1, HALF),
                                            start=(s == 0 and k == 0), stop=(s == TAPS - 1 and k == dk - 1))
                last.then_inc(convolved, 1)


def phase_block_attention(core, scope, qkvT, wa, d, ffn_raw_loaded):
    nc, tiles = core.nc, core.tiles
    sb = lambda name, shape, dt: scope.enter_context(nc.sbuf_tensor(name, shape, dt))
    ps = lambda name: scope.enter_context(nc.psum_tensor(name, [P, HALF], F32))
    CH = 8
    G = 4 * CH
    V = sb("a_v", [P, tiles, 1024], F32)
    bv_row, pb_row = wa["bv_row"], wa["pb_row"]
    q_pad = sb("q_pad", [P, 2, 2, core.T], F32)
    kT = sb("a_kT", [P, 2, core.T], F32)
    prob = sb("a_prob", [P, 3, HALF], F32)
    probT = sb("a_probT", [P, 2, HALF], F32)
    neg_max = sb("a_neg_max", [P, G, 4], F32)
    row_sum = sb("a_row_sum", [P, G, 4], F32)
    row_inv = sb("a_row_inv", [P, G, 4], F32)
    oT_hi = sb("a_oT_hi", [P, 2, HALF], F32R)
    oT_lo = sb("a_oT_lo", [P, 2, HALF], F32R)
    yT_hi = sb("a_yT_hi", [P, core.T], F32R)
    yT_lo = sb("a_yT_lo", [P, core.T], F32R)
    ident16 = sb("ident16", [P, P], BF16)
    mask = sb("a_mask", [P, 4, P], BF16)
    S_ps = [ps(f"a_S{i}") for i in range(2)]
    T_ps = ps("a_T")
    O_ps = [ps(f"a_O{i}") for i in range(2)]
    proj_ps = ps("a_proj")
    acc_ps = [ps(f"a_acc{i}") for i in range(2)]

    consts = core.sem("a_consts")
    const_chain = core.sem("a_const_chain")
    v_done = core.sem("a_v_done")
    v_ready = core.sem("a_v_ready")
    q_done = core.sem("a_q_done")
    k_done = core.sem("a_k_done")
    q_ready = core.sem("a_q_ready")
    k_ready = core.sem("a_k_ready")
    scored = core.sem("a_scored")
    max_ready = core.sem("a_max_ready")
    exp_ready = core.sem("a_exp_ready")
    inv_ready = core.sem("a_inv_ready")
    prob_ready = core.sem("a_prob_ready")
    prob_turned = core.sem("a_prob_turned")
    probT_ready = core.sem("a_probT_ready")
    mixed = core.sem("a_mixed")
    oT_hi_ready = core.sem("a_oT_hi_ready")
    oT_lo_ready = core.sem("a_oT_lo_ready")
    projected = core.sem("a_projected")
    yT_hi_ready = core.sem("a_yT_hi_ready")
    yT_lo_ready = core.sem("a_yT_lo_ready")
    expanded = core.sem("a_expanded")
    residual = core.sem("a_residual")
    x_biased = core.sem("a_x_biased")
    chain_sem = core.sem("a_chain")

    def pair(j):
        return j // 2, j % 2

    rows = RowStats(core, "a")

    LAG_T, LAG_O = 2, 3

    with nc.Block() as block:
        @block.sync
        def _(sp):
            load_ffn_weights(core, sp, d, ffn_raw_loaded)

        @block.gpsimd
        def _(pool):
            count = [0]

            def link(instruction):
                count[0] += 1
                instruction.then_inc(const_chain, 1)
                pool.wait_ge(const_chain, count[0])

            link(pool.tensor_copy(ident16[:, :], core.ident[:, :]))
            link(pool.memset(mask[:, :, :], 0.0))
            pool.affine_select(out=mask[:, :, :], in_=mask[:, :, :], compare_op=ALU.is_ge, fill=-1e9,
                               base=0, pattern=[[0, 4], [-1, P]], channel_multiplier=1).then_inc(consts, 1)
            for slot in range(2):
                pool.wait_ge(consts, 1 + 2 * slot)
                pool.memset(q_pad[64:128, slot, 0, :], 0.0).then_inc(consts, 1)
                pool.wait_ge(consts, 2 + 2 * slot)
                pool.memset(q_pad[0:64, slot, 1, :], 0.0).then_inc(consts, 1)
            pool.wait_ge(consts, 5)
            for i in range(tiles):
                pool.tensor_tensor(core.x[:, i, :], core.x[:, i, :], pb_row[:, :], ALU.add).then_inc(x_biased, 1)
            for n in range(G):
                pool.wait_ge(inv_ready, n + 1)
                p = prob[:, n % 3, :].rearrange("p (j k) -> p j k", k=P)
                pool.tensor_tensor(p, p, bcast(row_inv[:, n, :], P), ALU.mult).then_inc(prob_ready, 1)

        @block.tensor
        def _(pe):
            def project_q(c, h):
                w, t = slice(c * P, (c + 1) * P), slice(h * HALF, (h + 1) * HALF)
                if c or h:
                    pe.wait_ge(k_ready, 2 * c + h)
                parts_matmul(pe, proj_ps[:, :], (wa["qkv_hi"][:, 0, w], wa["qkv_lo"][:, 0, w]),
                             (qkvT[0][:, 0, t], qkvT[1][:, 0, t]), True, True).then_inc(q_done, 1)

            def project_k(c, h):
                w, t = slice(c * P, (c + 1) * P), slice(h * HALF, (h + 1) * HALF)
                pe.wait_ge(q_ready, 2 * (2 * c + h + 1))
                parts_matmul(pe, proj_ps[:, :], (wa["qkv_hi"][:, 1, w], wa["qkv_lo"][:, 1, w]),
                             (qkvT[0][:, 1, t], qkvT[1][:, 1, t]), True, True).then_inc(k_done, 1)

            def score(n):
                c, g = n // 4, n % 4
                bank = S_ps[n % 2]
                if n < 2:
                    pe.wait_ge(v_ready, 2 * tiles)
                    pe.wait_ge(consts, 5)
                else:
                    pe.wait_ge(exp_ready, n - 1)
                pe.wait_ge(q_ready, 2 * (2 * c + g // 2 + 1))
                pe.wait_ge(k_ready, 2 * c + g // 2 + 1)
                pe.matmul(bank[:, :], ident16[:, :], mask[:, :, :].rearrange("p j k -> p (j k)"),
                          start=True, stop=True, skip_group_check=True)
                for j in range(4):
                    b, head = pair(j)
                    t = slice((2 * g + b) * P, (2 * g + b + 1) * P)
                    last = pe.matmul(bank[:, j * P:(j + 1) * P], q_pad[:, c % 2, head, t], kT[:, c % 2, t],
                                     start=False, stop=True, skip_group_check=True)
                last.then_inc(scored, 1)

            def turn(n):
                pe.wait_ge(prob_ready, n + 1)
                if n >= 1:
                    pe.wait_ge(probT_ready, n)
                for j in range(4):
                    t = slice(j * P, (j + 1) * P)
                    last = pe.transpose(T_ps[:, t], prob[:, n % 3, t], core.ident[:, :])
                last.then_inc(prob_turned, 1)

            def mix(n):
                c, g = n // 4, n % 4
                pe.wait_ge(probT_ready, n + 1)
                if n >= 2:
                    pe.wait_ge(oT_lo_ready, n - 1)
                for j in range(4):
                    b, head = pair(j)
                    e = (2 * c + head) * 64
                    out = O_ps[n % 2][64 * head:64 * head + 64, b * P:(b + 1) * P]
                    last = pe.matmul(out, V[:, 2 * g + b, e:e + 64],
                                     probT[:, n % 2, j * P:(j + 1) * P], start=True, stop=True,
                                     skip_group_check=True)
                last.then_inc(mixed, 1)

            def project_out(c, h):
                pe.wait_ge(oT_lo_ready, 4 * c + 2 * h + 2)
                w = slice(c * P, (c + 1) * P)
                parts_matmul(pe, acc_ps[h][:, :], (wa["wo_hi"][:, w], wa["wo_lo"][:, w]),
                             (oT_hi[:, h, :], oT_lo[:, h, :]), start=(c == 0), stop=(c == CH - 1))\
                    .then_inc(projected, 1)

            for u in range(2 * tiles):
                i, c = u // 2, u % 2
                if u >= 4:
                    pe.wait_ge(v_ready, u - 3)
                bank = (*S_ps, T_ps, O_ps[0])[u % 4]
                cols = slice(c * HALF, (c + 1) * HALF)
                parts_matmul(pe, bank[:, :], (qkvT[0][:, 2, i * P:(i + 1) * P], qkvT[1][:, 2, i * P:(i + 1) * P]),
                             (wa["qkv_hi"][:, 2, cols], wa["qkv_lo"][:, 2, cols]), True, True).then_inc(v_done, 1)
                if u % 4 == 3:
                    (project_q, project_k)[u // 4 % 2](0, u // 8)

            for n in range(G + LAG_O + 1):
                if n < G:
                    score(n)
                if n // 4 + 1 < CH:
                    (project_q, project_k)[n % 2](n // 4 + 1, n % 4 // 2)
                if LAG_O <= n < G + LAG_O:
                    mix(n - LAG_O)
                if LAG_T <= n < G + LAG_T:
                    turn(n - LAG_T)
                done = n - LAG_O - 1
                if done >= 0 and done % 2 == 1:
                    project_out(done // 4, done % 4 // 2)
            for i in range(tiles):
                pe.wait_ge(yT_lo_ready, i // 4 + 1)
                if i >= 4:
                    pe.wait_ge(residual, i - 3)
                t = slice(i * P, (i + 1) * P)
                bank = (*S_ps, T_ps, proj_ps)[i % 4]
                parts_matmul(pe, bank[:, :], (yT_hi[:, t], yT_lo[:, t]), (wa["pw_hi"], wa["pw_lo"]),
                             True, True).then_inc(expanded, 1)

        @block.scalar
        def _(act):
            def k_out(c, h):
                n = 2 * c + h
                act.wait_ge(k_done, n + 1)
                if c >= 2:
                    act.wait_ge(scored, 4 * (c - 1))
                act.activation(kT[:, c % 2, h * HALF:(h + 1) * HALF], proj_ps[:, :], ACT.Identity,
                               bias=core.bias_cols[:, 11 + c:12 + c]).then_inc(k_ready, 1)

            def exponent(n):
                act.wait_ge(max_ready, n + 1)
                if n >= 3:
                    act.wait_ge(prob_turned, n - 2)
                for j in range(4):
                    last = act.activation(prob[:, n % 3, j * P:(j + 1) * P], S_ps[n % 2][:, j * P:(j + 1) * P],
                                          ACT.Exp, bias=neg_max[:, n, j:j + 1], accum_out=row_sum[:, n, j:j + 1])
                last.then_inc(exp_ready, 1)

            def turned_out(n):
                act.wait_ge(prob_turned, n + 1)
                if n >= 2:
                    act.wait_ge(mixed, n - 1)
                act.copy(probT[:, n % 2, :], T_ps[:, :]).then_inc(probT_ready, 1)

            def mixed_out(n):
                c, g = n // 4, n % 4
                act.wait_ge(mixed, n + 1)
                if c >= 1:
                    act.wait_ge(projected, 2 * (c - 1) + g // 2 + 1)
                cols = slice((g % 2) * 256, (g % 2) * 256 + 256)
                act.copy(oT_hi[:, g // 2, cols], O_ps[n % 2][:, 0:256]).then_inc(oT_hi_ready, 1)

            k_out(0, 0)
            k_out(0, 1)
            for n in range(G + LAG_O + 1):
                if n >= LAG_O + 1:
                    mixed_out(n - LAG_O - 1)
                if n < G:
                    exponent(n)
                if n % 2 == 1 and n // 4 + 1 < CH:
                    k_out(n // 4 + 1, n % 4 // 2)
                if LAG_T <= n < G + LAG_T:
                    turned_out(n - LAG_T)
            for h in range(2):
                act.wait_ge(projected, 2 * (CH - 1) + h + 1)
                act.activation(yT_hi[:, h * HALF:(h + 1) * HALF], acc_ps[h][:, :], ACT.Identity,
                               bias=core.bias_cols[:, 19:20]).then_inc(yT_hi_ready, 1)
            rows.scalar_std(act, range(0, 4), 4)

        @block.vector
        def _(dve):
            def q_out(c, h):
                n = 2 * c + h
                dve.wait_ge(q_done, n + 1)
                if c >= 2:
                    dve.wait_ge(scored, 4 * (c - 1))
                for head in range(2):
                    r = slice(64 * head, 64 * head + 64)
                    dve.tensor_scalar(q_pad[r, c % 2, head, h * HALF:(h + 1) * HALF], proj_ps[r, :],
                                      core.bias_cols[r, 3 + c:4 + c], 0.125, ALU.add, ALU.mult).then_inc(q_ready, 1)

            def maximum(n):
                dve.wait_ge(scored, n + 1)
                dve.tensor_reduce(neg_max[:, n, :], S_ps[n % 2][:, :].rearrange("p (j k) -> p j k", k=P),
                                  AX_X, ALU.max, negate=True).then_inc(max_ready, 1)

            def inverse(n):
                dve.wait_ge(exp_ready, n + 1)
                dve.reciprocal(row_inv[:, n, :], row_sum[:, n, :]).then_inc(inv_ready, 1)

            def mixed_lo(n):
                g = n % 4
                dve.wait_ge(oT_hi_ready, n + 1)
                cols = slice((g % 2) * 256, (g % 2) * 256 + 256)
                dve.tensor_tensor(oT_lo[:, g // 2, cols], O_ps[n % 2][:, 0:256], oT_hi[:, g // 2, cols].bitcast(F32),
                                  ALU.subtract).then_inc(oT_lo_ready, 1)

            chain = Chain(dve, chain_sem)
            for u in range(2 * tiles):
                i, c = u // 2, u % 2
                dve.wait_ge(v_done, u + 1)
                bank = (*S_ps, T_ps, O_ps[0])[u % 4]
                cols = slice(c * HALF, (c + 1) * HALF)
                dve.tensor_tensor(V[:, i, cols], bank[:, :], bv_row[:, cols], ALU.add).then_inc(v_ready, 1)
                if u % 8 == 3:
                    q_out(0, u // 8)
            for n in range(G + LAG_O + 1):
                if n < G:
                    maximum(n)
                if n >= LAG_O + 1:
                    mixed_lo(n - LAG_O - 1)
                if 1 <= n <= G:
                    inverse(n - 1)
                if n % 2 == 0 and n // 4 + 1 < CH:
                    q_out(n // 4 + 1, n % 4 // 2)
            for h in range(2):
                t = slice(h * HALF, (h + 1) * HALF)
                dve.wait_ge(yT_hi_ready, h + 1)
                dve.scalar_tensor_tensor(out=yT_lo[:, t], in0=acc_ps[h][:, :], scalar=core.bias_cols[:, 19:20],
                                         in1=yT_hi[:, t].bitcast(F32), op0=ALU.add, op1=ALU.subtract)\
                   .then_inc(yT_lo_ready, 1)
            dve.wait_ge(x_biased, tiles)
            for i in range(tiles):
                dve.wait_ge(expanded, i + 1)
                bank = (*S_ps, T_ps, proj_ps)[i % 4]
                dve.tensor_tensor(core.x[:, i, :], bank[:, :], core.x[:, i, :], ALU.add).then_inc(residual, 1)
                if i == 3:
                    dve.wait_ge(residual, 4)
                    rows.vector_stats(dve, chain, range(0, 4))
            rows.vector_rstd(dve, chain, range(0, 4))
            dve.wait_ge(residual, tiles)


RAW_WR, RAW_A, RAW_B = 0, 256, 4352


def load_ffn_weights(core, sp, d, loaded, pieces=(0, 1, 2)):
    places = ((RAW_WR, "WrT", 64), (RAW_A, "AT", 1024), (RAW_B, "Bm", 512))
    for s in pieces:
        at, name, n = places[s]
        chunks = d[name].shape[0] // P
        sp.dma_start(core.raw[:, at:at + chunks * n].rearrange("p (k n) -> p k n", n=n),
                     d[name].rearrange("(k p) n -> p k n", p=P)).then_inc(loaded[s], 16)


def phase_ffn(core, scope, name, loaded, after_split=None, store=None):
    nc, tiles, dk = core.nc, core.tiles, core.dk
    sb = lambda what, shape, dt: scope.enter_context(nc.sbuf_tensor(f"{name}_{what}", shape, dt))
    ps = lambda what: scope.enter_context(nc.psum_tensor(f"{name}_{what}", [P, HALF], F32))
    sem = lambda what: core.sem(f"{name}_{what}")
    K, C = 64, 8
    UNITS = 2 * C
    AHEAD = 4
    wr_hi, wr_lo = (sb(f"wr_{s}", [P, dk, 2 * K], F32R) for s in ("hi", "lo"))
    a_hi, a_lo = (sb(f"a_{s}", [P, dk, C * P], F32R) for s in ("hi", "lo"))
    b_hi, b_lo = (sb(f"b_{s}", [P, C, HALF], F32R) for s in ("hi", "lo"))
    spread_f = sb("spread_f", [P, C, P], F32)
    spread = sb("spread", [P, C, P], F32R)
    scoreT = sb("scoreT", [K, HALF], F32)
    score = sb("score", [P, 4, K], F32)
    rest = sb("rest", [P, 4, K], F32)
    top = sb("top", [P, 4, 16], F32)
    gate = sb("gate", [P, 4, K], F32)
    chosen = sb("chosen", [P, 4, K], F32)
    total = sb("total", [P, 8], F32)
    gate2 = sb("gate2", [P, 4, 2, K], F32)
    gateT = sb("gateT", [P, 2, HALF], F32R)
    h_sb = sb("h_sb", [P, AHEAD + 2, HALF], F32)
    hg = sb("hg", [P, 2, HALF], F32)
    hg_hi = sb("hg_hi", [P, 2, HALF], F32R)
    hg_lo = sb("hg_lo", [P, 2, HALF], F32R)
    acc = [ps(f"acc{i}") for i in range(4)]
    up_ps = [ps(f"up{i}") for i in range(2)]
    spread_ps = ps("spread_ps")
    aux = ps("aux")
    ln = LayerNorm(core, scope, name, 0, acc)
    rows, next_rows = RowStats(core, name), RowStats(core, name + "_next")

    w_hi, w_lo = sem("w_hi"), sem("w_lo")
    spread_chain, spread_built, spread_ready = sem("spread_chain"), sem("spread_built"), sem("spread_ready")
    routed, scoreT_ready, score_turned = sem("routed"), sem("scoreT_ready"), sem("score_turned")
    shifted, expd, gate_ready, gate_turned = sem("shifted"), sem("expd"), sem("gate_ready"), sem("gate_turned")
    gateT_hi_ready, gateT_ready = sem("gateT_hi"), sem("gateT_ready")
    up_done, h_ready, spread_done = sem("up_done"), sem("h_ready"), sem("spread_done")
    hg_ready, hg_hi_ready, hg_lo_ready = sem("hg_ready"), sem("hg_hi_ready"), sem("hg_lo_ready")
    acc_done = sem("acc_done")
    down_done, residual, chain_sem = sem("down_done"), sem("residual"), sem("chain")

    wr_raw = core.raw[:, RAW_WR:RAW_A].rearrange("p (k n) -> p k n", k=dk)
    a_raw = core.raw[:, RAW_A:RAW_B].rearrange("p (k n) -> p k n", k=dk)
    b_raw = core.raw[:, RAW_B:RAW_B + 4096].rearrange("p (c n) -> p c n", c=C)
    pieces = [(wr_raw, wr_hi[:, :, 0:K], wr_lo[:, :, 0:K], 0), (wr_raw, wr_hi[:, :, K:], wr_lo[:, :, K:], 0)]
    for c in range(C):
        cols = slice(c * P, (c + 1) * P)
        pieces.append((a_raw[:, :, cols], a_hi[:, :, cols], a_lo[:, :, cols], 1))
        pieces.append((b_raw[:, c, :], b_hi[:, c, :], b_lo[:, c, :], 2))
    A_AT = lambda c: 2 + 2 * c + 1
    B_AT = lambda c: 2 + 2 * c + 2

    with nc.Block() as block:
        @block.sync
        def _(sp):
            if after_split is not None:
                sp.wait_ge(w_lo, len(pieces))
                after_split(sp)
            if store is not None:
                stored, out = store
                for i in range(tiles):
                    sp.wait_ge(residual, i + 1)
                    sp.dma_start(out[i], core.x[:, i, :]).then_inc(stored, 16)
                sp.wait_ge(stored, 16 * tiles)

        @block.gpsimd
        def _(pool):
            def split_lo(n):
                raw, hi, lo, _ = pieces[n]
                pool.wait_ge(w_hi, n + 1)
                pool.tensor_tensor(lo, raw, hi.bitcast(F32), ALU.subtract).then_inc(w_lo, 1)

            for n in range(3):
                split_lo(n)
            pool.memset(spread_f[:, :, :], 0.0).then_inc(spread_chain, 1)
            for r in range(2):
                pool.wait_ge(spread_chain, r + 1)
                v = spread_f[:, :, :].rearrange("p c (k r) -> p c k r", r=16)
                pool.affine_select(out=v, in_=v, compare_op=ALU.not_equal, fill=1.0, base=-K * r,
                                   pattern=[[-8, C], [-1, 8], [0, 16]], channel_multiplier=1)\
                    .then_inc(spread_chain if r == 0 else spread_built, 1)
            for n in range(3, len(pieces)):
                split_lo(n)

        @block.vector
        def _(dve):
            chain = Chain(dve, chain_sem)

            def split_hi(n):
                raw, hi, lo, load = pieces[n]
                dve.wait_ge(loaded[load], 16)
                dve.tensor_copy(hi, raw).then_inc(w_hi, 1)

            def top8(half):
                dve.wait_ge(score_turned, half + 1)
                chain.link(dve.tensor_copy(score[:, :, :], aux[:, 0:4 * K].rearrange("p (i k) -> p i k", k=K)))
                for i in range(4):
                    last = dve.max(top[:, i, 0:8], score[:, i, :])
                chain.link(last)
                for i in range(4):
                    last = dve.match_replace(out=rest[:, i, :], in_to_replace=top[:, i, 0:8],
                                             in_values=score[:, i, :], imm_value=-3e38)
                chain.link(last)

            def top16(half):
                for i in range(4):
                    last = dve.max(top[:, i, 8:16], rest[:, i, :])
                chain.link(last)
                for i in range(4):
                    last = dve.match_replace(out=rest[:, i, :], in_to_replace=top[:, i, 8:16],
                                             in_values=rest[:, i, :], imm_value=-3e38)
                chain.link(last)
                dve.tensor_tensor(gate[:, :, :], score[:, :, :], bcast(top[:, :, 0], K), ALU.subtract)\
                   .then_inc(shifted, 1)
                chain.link(dve.tensor_tensor(chosen[:, :, :], rest[:, :, :], score[:, :, :], ALU.not_equal))

            def weigh(half):
                dve.wait_ge(expd, half + 1)
                chain.link(dve.tensor_tensor(gate[:, :, :], gate[:, :, :], chosen[:, :, :], ALU.mult))
                chain.link(dve.tensor_reduce(total[:, 0:4], gate[:, :, :], AX_X, ALU.add))
                chain.link(dve.reciprocal(total[:, 4:8], total[:, 0:4]))
                for r in range(2):
                    dve.scalar_tensor_tensor(out=gate2[:, :, r, :], in0=gate[:, :, :], scalar=2.0,
                                             in1=bcast(total[:, 4:8], K), op0=ALU.mult, op1=ALU.mult)\
                       .then_inc(gate_ready, 1)

            def gateT_lo(half):
                dve.wait_ge(gateT_hi_ready, half + 1)
                g = gateT[K:2 * K, half, :]
                dve.tensor_tensor(g, aux[K:2 * K, :], g.bitcast(F32), ALU.subtract).then_inc(gateT_ready, 1)

            def scale(u):
                dve.wait_ge(h_ready, u + 1)
                dve.wait_ge(spread_done, u + 1)
                if u >= 2:
                    dve.wait_ge(hg_hi_ready, u - 1)
                dve.tensor_tensor(hg[:, u % 2, :], spread_ps[:, :], h_sb[:, u % (AHEAD + 2), :], ALU.mult)\
                   .then_inc(hg_ready, 1)

            def scale_lo(u):
                dve.wait_ge(hg_hi_ready, u + 1)
                dve.tensor_tensor(hg_lo[:, u % 2, :], hg[:, u % 2, :], hg_hi[:, u % 2, :].bitcast(F32),
                                  ALU.subtract).then_inc(hg_lo_ready, 1)

            def add_residual(half):
                for i in range(4 * half, 4 * half + 4):
                    dve.wait_ge(acc_done, i + 1)
                    dve.tensor_tensor(core.x[:, i, :], acc[i % 4][:, :], core.x[:, i, :], ALU.add)\
                       .then_inc(residual, 1)

            def first_top16():
                top8(0)
                top16(0)

            ln.vector_all(dve, chain, rows, lambda: [split_hi(n) for n in range(3)], first_top16)
            weigh(0)
            gateT_lo(0)
            for u in range(UNITS):
                for n in range(A_AT(u + AHEAD), min(A_AT(u + AHEAD + 1), len(pieces))):
                    split_hi(n)
                scale(u)
                scale_lo(u)
                if u == 3:
                    top8(1)
                if u == 4:
                    top16(1)
                if u == 5:
                    weigh(1)
                if u == 6:
                    gateT_lo(1)
                if u == C:
                    add_residual(0)
                if u == C + 2 and store is None:
                    next_rows.vector_stats(dve, chain, range(0, 4))
                if u == C + 4 and store is None:
                    next_rows.vector_rstd(dve, chain, range(0, 4))
            add_residual(1)
            dve.wait_ge(residual, tiles)

        @block.scalar
        def _(act):
            def scoreT_out(half):
                act.wait_ge(routed, half + 1)
                if half:
                    act.wait_ge(score_turned, half)
                act.copy(scoreT[:, :], aux[0:K, :]).then_inc(scoreT_ready, 1)

            def exponent(half):
                act.wait_ge(shifted, half + 1)
                act.activation(gate[:, :, :], gate[:, :, :], ACT.Exp).then_inc(expd, 1)

            def gateT_hi(half):
                act.wait_ge(gate_turned, half + 1)
                act.copy(gateT[:, half, :], aux[:, :]).then_inc(gateT_hi_ready, 1)

            def h_out(u):
                act.wait_ge(up_done, u + 1)
                if u > AHEAD + 1:
                    act.wait_ge(hg_ready, u - AHEAD - 1)
                act.copy(h_sb[:, u % (AHEAD + 2), :], up_ps[u % 2][:, :]).then_inc(h_ready, 1)

            def hg_high(u):
                act.wait_ge(hg_ready, u + 1)
                if u >= 2 and u % C == 1:
                    act.wait_ge(acc_done, 4 * (u // C))
                elif u >= 2:
                    act.wait_ge(down_done, u - 1 - (u - 2) // C)
                act.copy(hg_hi[:, u % 2, :], hg[:, u % 2, :]).then_inc(hg_hi_ready, 1)

            def split_hi(n):
                raw, hi, lo, load = pieces[n]
                act.wait_ge(loaded[load], 16)
                act.copy(hi, raw).then_inc(w_hi, 1)

            for i in range(0, 4):
                ln.scalar_hi(act, i)
            act.wait_ge(w_hi, 3)
            for n in range(3, 8):
                split_hi(n)
            rows.scalar_std(act, range(4, 8), 4)
            scoreT_out(0)
            for n in range(8, A_AT(AHEAD)):
                split_hi(n)
            h_out(0)
            ln.scalar_hi(act, 4)
            ln.scalar_hi(act, 5)
            exponent(0)
            act.wait_ge(spread_built, 1)
            act.copy(spread[:, :, :], spread_f[:, :, :]).then_inc(spread_ready, 1)
            h_out(1)
            ln.scalar_hi(act, 6)
            ln.scalar_hi(act, 7)
            h_out(2)
            gateT_hi(0)
            h_out(3)
            h_out(AHEAD)
            for u in range(UNITS):
                hg_high(u)
                if u + AHEAD + 1 < UNITS:
                    h_out(u + AHEAD + 1)
                if u == 2:
                    scoreT_out(1)
                if u == 4:
                    exponent(1)
                if u == 5:
                    gateT_hi(1)
                if u == C + 3 and store is None:
                    next_rows.scalar_std(act, range(0, 4), 4)

        @block.tensor
        def _(pe):
            def route(half):
                pe.wait_ge(ln.lo_ready, 4 * half + 4)
                pe.wait_ge(w_lo, 2)
                if half:
                    pe.wait_ge(gateT_ready, half)
                for k in range(dk):
                    last = parts_matmul(pe, aux[:, :], (wr_hi[:, k, :], wr_lo[:, k, :]),
                                        ln.columns(k, half * HALF, HALF), start=(k == 0), stop=(k == dk - 1))
                last.then_inc(routed, 1)

            def turn_scores(half):
                pe.wait_ge(scoreT_ready, half + 1)
                for i in range(4):
                    last = pe.transpose(aux[:, i * K:(i + 1) * K], scoreT[:, i * P:(i + 1) * P], core.ident[0:K, 0:K])
                last.then_inc(score_turned, 1)

            def turn_gates(half):
                pe.wait_ge(gate_ready, 2 * half + 2)
                for i in range(4):
                    last = pe.transpose(aux[:, i * P:(i + 1) * P],
                                        gate2[:, i, :, :].rearrange("p r k -> p (r k)"), core.ident[:, :])
                last.then_inc(gate_turned, 1)

            def up(u):
                half, c = u // C, u % C
                pe.wait_ge(ln.lo_ready, 4 * half + 4)
                if half == 0:
                    pe.wait_ge(w_lo, A_AT(c))
                if u >= 2:
                    pe.wait_ge(h_ready, u - 1)
                cols = slice(c * P, (c + 1) * P)
                for k in range(dk):
                    last = parts_matmul(pe, up_ps[u % 2][:, :], (a_hi[:, k, cols], a_lo[:, k, cols]),
                                        ln.columns(k, half * HALF, HALF), start=(k == 0), stop=(k == dk - 1))
                last.then_inc(up_done, 1)

            def spread_gates(u):
                half, c = u // C, u % C
                pe.wait_ge(gateT_ready, half + 1)
                if u >= 1:
                    pe.wait_ge(hg_ready, u)
                pe.matmul(spread_ps[:, :], spread[:, c, :], gateT[:, half, :], start=True, stop=True)\
                  .then_inc(spread_done, 1)

            def down(u):
                half, c = u // C, u % C
                pe.wait_ge(hg_lo_ready, u + 1)
                if half == 0:
                    pe.wait_ge(w_lo, B_AT(c))
                for i in range(4):
                    t = slice(i * P, (i + 1) * P)
                    if c == 0 and half:
                        pe.wait_ge(residual, i + 1)
                    last = parts_matmul(pe, acc[i][:, :], (hg_hi[:, u % 2, t], hg_lo[:, u % 2, t]),
                                        (b_hi[:, c, :], b_lo[:, c, :]), start=(c == 0), stop=(c == C - 1))
                    if c == C - 1:
                        last.then_inc(acc_done, 1)
                    elif i == 3:
                        last.then_inc(down_done, 1)

            for i in range(4):
                ln.tensor_turn(pe, i)
            route(0)
            turn_scores(0)
            up(0)
            ln.tensor_turn(pe, 4)
            ln.tensor_turn(pe, 5)
            up(1)
            ln.tensor_turn(pe, 6)
            ln.tensor_turn(pe, 7)
            up(2)
            turn_gates(0)
            up(3)
            pe.wait_ge(spread_ready, 1)
            spread_gates(0)
            up(AHEAD)
            pe.wait_ge(ln.lo_ready, tiles)
            for u in range(UNITS):
                if u + AHEAD + 1 < UNITS:
                    up(u + AHEAD + 1)
                if u + 1 < UNITS:
                    spread_gates(u + 1)
                down(u)
                if u == 1:
                    route(1)
                if u == 2:
                    turn_scores(1)
                if u == 5:
                    turn_gates(1)


RAW_Q, RAW_K, RAW_V, RAW_O = 0, 2048, 2560, 6400
HEADS, GROUPS, DH = 32, 8, 16
PER = HEADS // GROUPS
OPERAND = 96


def load_gqa_weights(core, sp, d, loaded):
    for s, (at, name, n) in enumerate(((RAW_K, "kwT", 128), (RAW_V, "vwT", 128), (RAW_Q, "qwT", 512),
                                       (RAW_O, "owT", 512))):
        sp.dma_start(core.raw[:, at:at + core.dk * n].rearrange("p (k n) -> p k n", n=n),
                     d[name].rearrange("(k p) n -> p k n", p=P)).then_inc(loaded[s], 16)


def stack_keys(queue, b, g, loaded):
    for r in range(4):
        src = b["kT"][r % 2][DH * g:DH * (g + 1), :].bitcast(F32)
        queue.dma_start(b["k_op"][DH * r:DH * (r + 1), g, :].bitcast(F32), src).then_inc(loaded, 16)


def stack_queries(queue, b, g, rows, loaded, heads=range(4)):
    for j in heads:
        head = PER * g + j
        at = slice(DH * (head % 8), DH * (head % 8) + DH)
        for r in rows:
            src = b["qT"][r // 2][at, head // 8, :].bitcast(F32).rearrange("d (h t) -> d h t", h=2)
            to = (b["q_op"], b["q_op_odd"])[g % 2] if g else b["q_op"]
            queue.dma_start(to[DH * r:DH * (r + 1), :, j, :].bitcast(F32), src).then_inc(loaded, 16)


def phase_gqa_projections(core, scope, b, loaded):
    nc, tiles, dk = core.nc, core.tiles, core.dk
    sb = lambda what, shape, dt: scope.enter_context(nc.sbuf_tensor(f"p_{what}", shape, dt))
    ps = lambda what: scope.enter_context(nc.psum_tensor(f"p_{what}", [P, HALF], F32))
    kT_hi, kT_lo = b["kT"] = [sb(f"kT_{s}", [P, core.T], F32R) for s in ("hi", "lo")]
    w_hi, w_lo = (sb(f"w_{s}", [P, 3, dk, P], F32R) for s in ("hi", "lo"))
    turn_ps = [ps(f"turn{i}") for i in range(4)]
    out_ps = [ps(f"out{i}") for i in range(3)]
    v_ps = ps("v")
    ln = LayerNorm(core, scope, "p", 0, turn_ps, b["xT"])
    rows = RowStats(core, "p")
    vT = ln.xn[:, :, :].rearrange("p s t -> p (s t)")
    sem = lambda what: core.sem(f"p_{what}")
    w_hi_ready, w_lo_ready, projected = sem("w_hi"), sem("w_lo"), sem("projected")
    hi_ready, lo_ready, v_turned, v_ready = sem("hi_ready"), sem("lo_ready"), sem("v_turned"), sem("v_ready")
    zeroed, q_op_zeroed, chain_sem = sem("zeroed"), sem("q_op_zeroed"), sem("chain")
    b["consts_ready"] = sem("consts_ready")
    raw = lambda at, n: core.raw[:, at:at + dk * n].rearrange("p (k n) -> p k n", n=n)
    K, Q, V = range(3)
    q_piece = lambda m: (raw(RAW_Q, 512)[:, :, m * P:(m + 1) * P], 2)
    pieces = [(raw(RAW_K, P), 0), q_piece(0), (raw(RAW_V, P), 1), q_piece(1), q_piece(2), q_piece(3)]
    parts_of = lambda n, w, later: w[:, n, :, :] if n < 3 else later[:, n - 3, :, :]
    hi_of = lambda n: parts_of(n, w_hi, b["qw"][0])
    lo_of = lambda n: parts_of(n, w_lo, b["qw"][1])
    units = [(w, h) for h in range(2) for w in (K, Q, V)]
    bias = lambda w: core.bias_cols[:, (24, 20, 25)[w]:(24, 20, 25)[w] + 1]

    def target(w, h, part):
        t = slice(h * HALF, (h + 1) * HALF)
        return (kT_hi, kT_lo)[part][:, t] if w == K else b["qT"][part][:, 0, t]

    with nc.Block() as block:
        @block.sync
        def _(sp):
            sp.wait_ge(lo_ready, 3)
            stack_keys(sp, b, 0, b["first_k_loaded"])
            sp.wait_ge(lo_ready, 4)
            stack_queries(sp, b, 0, range(2, 4), b["q_loaded"][0])
            stack_queries(sp, b, 0, range(0, 2), b["q_loaded"][0], heads=range(3, PER))

        @block.gpsimd
        def _(pool):
            def split_lo(n):
                pool.wait_ge(w_hi_ready, n + 1)
                pool.tensor_tensor(lo_of(n), pieces[n][0], hi_of(n).bitcast(F32), ALU.subtract)\
                    .then_inc(w_lo_ready, 1)

            split_lo(0)
            pool.wait_ge(w_lo_ready, 1)
            pool.memset(b["k_op"][64:OPERAND, :, :].bitcast(F32), 0.0).then_inc(zeroed, 1)
            pool.wait_ge(zeroed, 1)
            split_lo(1)
            split_lo(2)
            pool.memset(b["v"][:, :, :, :], 0.0).then_inc(zeroed, 1)
            pool.wait_ge(zeroed, 2)
            pool.wait_ge(w_lo_ready, 3)
            pool.memset(b["v"][:, :, :, DH:DH + 1], 1.0).then_inc(b["consts_ready"], 1)
            pool.wait_ge(b["consts_ready"], 1)
            pool.memset(b["k_op"][64:66, :, :].bitcast(F32), 1.0).then_inc(b["consts_ready"], 1)
            pool.wait_ge(b["consts_ready"], 2)
            for n in range(3, 6):
                split_lo(n)
            pool.wait_ge(w_lo_ready, 6)
            pool.wait_ge(hi_ready, 5)
            stack_queries(pool, b, 0, range(0, 2), b["first_q_loaded"], heads=range(0, 3))

        @block.vector
        def _(dve):
            chain = Chain(dve, chain_sem)

            def split_hi(n):
                piece, load = pieces[n]
                dve.wait_ge(loaded[load], 16)
                dve.tensor_copy(hi_of(n), piece).then_inc(w_hi_ready, 1)

            def unit(u):
                w, h = units[u]
                if w == V:
                    dve.wait_ge(v_turned, h + 1)
                    dve.tensor_copy(b["v"][:, 4 * h:4 * h + 4, :, 0:DH],
                                    v_ps[:, :].rearrange("p (i g e) -> p i g e", i=4, g=GROUPS)).then_inc(v_ready, 1)
                    return
                dve.wait_ge(hi_ready, u + 1)
                dve.scalar_tensor_tensor(out=target(w, h, 1), in0=out_ps[u % 3][:, :], scalar=bias(w),
                                         in1=target(w, h, 0).bitcast(F32), op0=ALU.add, op1=ALU.subtract)\
                   .then_inc(lo_ready, 1)

            ln.vector_all(dve, chain, rows, lambda: [split_hi(n) for n in range(3)],
                          late=lambda: [unit(u) for u in range(2)])
            dve.wait_ge(b["consts_ready"], 1)
            for u in range(2, len(units)):
                if u in (2, 4):
                    dve.memset(b["q_op"][64:OPERAND, u // 2 - 1, :, :].bitcast(F32), 0.0).then_inc(q_op_zeroed, 1)
                unit(u)
            dve.wait_ge(lo_ready, 4)
            dve.wait_ge(v_ready, 2)
            dve.wait_ge(q_op_zeroed, 2)

        @block.scalar
        def _(act):
            for i in range(4):
                ln.scalar_hi(act, i)
            act.wait_ge(w_hi_ready, 3)
            for n in range(3, 6):
                piece, load = pieces[n]
                act.wait_ge(loaded[load], 16)
                act.copy(hi_of(n), piece).then_inc(w_hi_ready, 1)
            rows.scalar_std(act, range(4, 8), 4)
            for i in range(4, 6):
                ln.scalar_hi(act, i)
            for u, (w, h) in enumerate(units):
                if u == 2:
                    for i in range(6, 8):
                        ln.scalar_hi(act, i)
                act.wait_ge(projected, u + 1)
                out = vT[:, h * HALF:(h + 1) * HALF] if w == V else target(w, h, 0)
                act.activation(out, out_ps[u % 3][:, :], ACT.Identity, bias=bias(w)).then_inc(hi_ready, 1)

        @block.tensor
        def _(pe):
            def turn_v(h):
                pe.wait_ge(hi_ready, 3 * h + 3)
                if h:
                    pe.wait_ge(v_ready, h)
                for i in range(4):
                    t = slice((4 * h + i) * P, (4 * h + i + 1) * P)
                    last = pe.transpose(v_ps[:, i * P:(i + 1) * P], vT[:, t], core.ident[:, :])
                last.then_inc(v_turned, 1)

            for i in range(4):
                ln.tensor_turn(pe, i)
            for u, (w, h) in enumerate(units):
                pe.wait_ge(ln.lo_ready, 4 * h + 4)
                pe.wait_ge(w_lo_ready, w + 1)
                if u >= 3:
                    pe.wait_ge(*((hi_ready, 3) if u == 5 else (lo_ready, u - 2)))
                for k in range(dk):
                    last = parts_matmul(pe, out_ps[u % 3][:, :], (w_hi[:, w, k, :], w_lo[:, w, k, :]),
                                        ln.columns(k, h * HALF, HALF), start=(k == 0), stop=(k == dk - 1))
                last.then_inc(projected, 1)
                for i in {1: (4, 5), 2: (6, 7)}.get(u, ()):
                    ln.tensor_turn(pe, i)
                if u == 3:
                    turn_v(0)
            turn_v(1)


class HeadOutput:

    def __init__(self, core, b, name, first, turn_banks, out_banks):
        self.core, self.b, self.first = core, b, first
        self.turn_banks, self.out_banks = turn_banks, out_banks
        self.turned, self.hi_ready = core.sem(name + "_turned"), core.sem(name + "_hi_ready")
        self.lo_ready, self.projected = core.sem(name + "_lo_ready"), core.sem(name + "_projected")
        self.residual = core.sem(name + "_residual")

    def turned_view(self, i):
        return self.turn_banks[i - self.first][:, :].rearrange("p (k t) -> p k t", t=P)

    def part(self, which, i):
        return self.b["qT"][which][:, :, i * P:(i + 1) * P]

    def tensor_turn(self, pe, i):
        for k in range(self.core.dk):
            last = pe.transpose(self.turn_banks[i - self.first][:, k * P:(k + 1) * P],
                                self.b["o"][:, i, k * P:(k + 1) * P], self.core.ident[:, :])
        last.then_inc(self.turned, 1)

    def scalar_hi(self, act, i):
        act.wait_ge(self.turned, i - self.first + 1)
        act.copy(self.part(0, i), self.turned_view(i)).then_inc(self.hi_ready, 1)

    def vector_lo(self, dve, i):
        dve.wait_ge(self.hi_ready, i - self.first + 1)
        dve.tensor_tensor(self.part(1, i), self.turned_view(i), self.part(0, i).bitcast(F32), ALU.subtract)\
           .then_inc(self.lo_ready, 1)

    def tensor_project(self, pe, i):
        pe.wait_ge(self.lo_ready, i - self.first + 1)
        for k in range(self.core.dk):
            last = parts_matmul(pe, self.out_banks[i - self.first][:, :],
                                (self.part(0, i)[:, k, :], self.part(1, i)[:, k, :]), self.b["ow"][k],
                                start=(k == 0), stop=(k == self.core.dk - 1))
        last.then_inc(self.projected, 1)

    def vector_residual(self, dve, i):
        x = self.core.x[:, i, :]
        dve.wait_ge(self.projected, i - self.first + 1)
        dve.tensor_tensor(x, self.out_banks[i - self.first][:, :], x, ALU.add).then_inc(self.residual, 1)


def phase_gqa_core(core, scope, banks, b, d, weights_loaded, ffn_loaded):
    nc, tiles = core.nc, core.tiles
    sb = lambda what, shape, dt: scope.enter_context(nc.sbuf_tensor(f"g_{what}", shape, dt))
    sem = lambda what: core.sem(f"g_{what}")
    STAGES, UNITS, RING = 2 * GROUPS, tiles, 3
    SCALE = 0.25 * LN2
    prob = sb("prob", [P, 2, PER, HALF], F32)
    b["q_op_odd"] = sb("q_op_odd", [OPERAND, 2, PER, HALF], F32R)
    q_op = (b["q_op"], b["q_op_odd"])
    neg_part = sb("neg_part", [P, 2, 16], F32)
    neg_max = sb("neg_max", [P, 2, 16], F32)
    ob_at = nc.sbuf_base
    ob_row = sb("ob_row", [P, HALF], F32)
    ow_hi_last = sb("ow_hi_last", [P, HALF], F32R)
    ow_lo_last = nc.alloc_sbuf_tensor_at("g_ow_lo_last", [P, HALF], F32R, offset=ob_at)
    b["ow"] = [tuple(w[:, k, :, :].rearrange("p c n -> p (c n)") for w in b["qw"]) for k in range(3)]
    b["ow"].append((ow_hi_last[:, :], ow_lo_last[:, :]))
    ow_raw = core.raw[:, RAW_O:RAW_O + 2048].rearrange("p (k n) -> p k n", k=core.dk)
    maxT_hi, maxT_lo = (sb(f"maxT_{s}", [16, 2, P], F32R) for s in ("hi", "lo"))
    mixT = sb("mixT", [P, HALF], F32)
    den_inv = sb("den_inv", [P, 16], F32)
    S_ps = [banks.enter_context(nc.psum_tensor(f"g_S{i}", [P, HALF], F32)) for i in range(RING)]
    E_ps = [banks.enter_context(nc.psum_tensor(f"g_E{i}", [P, HALF], F32)) for i in range(RING)]
    mix_ps = banks.enter_context(nc.psum_tensor("g_mix", [P, HALF], F32))
    turn_ps = banks.enter_context(nc.psum_tensor("g_turn", [P, HALF], F32))
    q_loaded = b["q_loaded"]
    projected, hi_ready, lo_ready = sem("projected"), sem("hi_ready"), sem("lo_ready")
    m_loaded = [sem(f"m_loaded{s}") for s in range(2)]
    rows_zeroed, scored, part_ready = sem("rows_zeroed"), sem("scored"), sem("part_ready")
    max_ready = sem("max_ready")
    max_turned, maxT_ready, maxT_hi_ready = sem("max_turned"), sem("maxT_ready"), sem("maxT_hi_ready")
    keyed, exp_ready, mixed, mixT_ready = sem("keyed"), sem("exp_ready"), sem("mixed"), sem("mixT_ready")
    mix_turned, inv_ready, o_ready = sem("mix_turned"), sem("inv_ready"), sem("o_ready")
    ob_loaded, x_biased = sem("ob_loaded"), sem("x_biased")
    ow_hi_ready, ow_lo_ready = sem("ow_hi_ready"), sem("ow_lo_ready")
    early = HeadOutput(core, b, "g_early", 0, [S_ps[i] for i in (0, 1, 2, 0)], [S_ps[i] for i in (1, 2, 0, 1)])
    LEAD = UNITS + 2
    SLOTS = STAGES * UNITS + LEAD + 1
    turns_maxima = lambda s: s // UNITS - 1 if s % UNITS == 0 and 1 <= s // UNITS <= STAGES else -1
    EARLY = STAGES * UNITS - UNITS + LEAD + 3
    turns_mix = lambda s: (s - LEAD - 2) // UNITS - 1 if (s - LEAD - 2) % UNITS == 0 else -1

    dk = core.dk
    PROJECTIONS = 2 * (dk - 1)
    projects = lambda s, j: 3 * s + j if j < 3 and 3 * s + j < PROJECTIONS * dk else -1
    splits = lambda s: [x for x in range(PROJECTIONS) if (dk * x + dk - 1) // 3 + 1 == s]
    q_target = lambda x, part: b["qT"][part][:, 1 + x // 2, x % 2 * HALF:(x % 2 + 1) * HALF]
    q_bias = lambda x: core.bias_cols[:, 21 + x // 2:22 + x // 2]

    with nc.Block() as block:
        @block.sync
        def _(sp):
            def load_queries(g):
                slot = g % 2
                if g >= 2:
                    sp.wait_ge(keyed, PER * UNITS * 2 * (g - 1))
                    sp.wait_ge(lo_ready, 2 * (g // 2))
                stack_queries(sp, b, g, range(4), q_loaded[slot])
                if g >= 2:
                    sp.dma_start(q_op[slot][64:66].bitcast(F32), q_op[slot][66:68].bitcast(F32))\
                      .then_inc(q_loaded[slot], 16)

            def load_maxima(n):
                slot, half = n // 2 % 2, n % 2
                sp.wait_ge(maxT_ready, n + 1)
                for r, part in enumerate((maxT_hi, maxT_lo)):
                    sp.dma_start(q_op[slot][64 + r:65 + r, half, :, :].bitcast(F32).rearrange("p j t -> p (j t)"),
                                 part[:, n % 2, :].bitcast(F32)).then_inc(m_loaded[n % 2], 16)

            for g in range(1, GROUPS):
                stack_keys(sp, b, g, b["k_loaded"])
            sp.dma_start(ob_row[:, :], d["bias_rows"][0:1, 1536:2048].broadcast_to([P, HALF])).then_inc(ob_loaded, 16)
            for n in range(STAGES):
                load_maxima(n)
                if n == 0:
                    sp.wait_ge(b["k_loaded"], 16 * 4 * (GROUPS - 1))
                    load_queries(1)
                elif n == 1:
                    sp.wait_ge(rows_zeroed, 1)
                elif n % 2 == 0 and n // 2 + 1 < GROUPS:
                    load_queries(n // 2 + 1)
                if n == 2:
                    load_ffn_weights(core, sp, d, ffn_loaded, pieces=(0, 1))
            sp.wait_ge(ow_lo_ready, core.dk)
            load_ffn_weights(core, sp, d, ffn_loaded, pieces=(2,))

        @block.gpsimd
        def _(pool):
            pool.wait_ge(b["k_loaded"], 16 * 4 * (GROUPS - 1))
            pool.memset(q_op[1][64:OPERAND].bitcast(F32), 0.0).then_inc(rows_zeroed, 1)
            pool.wait_ge(rows_zeroed, 1)
            pool.wait_ge(ob_loaded, 16)
            for i in range(tiles):
                pool.tensor_tensor(core.x[:, i, :], core.x[:, i, :], ob_row[:, :], ALU.add).then_inc(x_biased, 1)
            pool.wait_ge(x_biased, tiles)
            for k in range(core.dk):
                pool.wait_ge(ow_hi_ready, k + 1)
                pool.tensor_tensor(b["ow"][k][1], ow_raw[:, k, :], b["ow"][k][0].bitcast(F32), ALU.subtract)\
                    .then_inc(ow_lo_ready, 1)
            pool.wait_ge(ow_lo_ready, core.dk)

        @block.tensor
        def _(pe):
            def score(m):
                n, t = m // 32, m % 32
                g, half, i, j, h = n // 2, n % 2, t // 8, t // 2 % PER, t % 2
                if t == 0:
                    if n == 0:
                        pe.wait_ge(b["first_k_loaded"], 16 * 4)
                        pe.wait_ge(b["first_q_loaded"], 16 * 2 * 3)
                    elif n == 2:
                        pe.wait_ge(rows_zeroed, 1)
                        pe.wait_ge(b["k_loaded"], 16 * 4 * (GROUPS - 1))
                    slot_loads = [16 * (10 if k == 0 else 16 if k == 1 else 17) for k in range(GROUPS)]
                    pe.wait_ge(q_loaded[g % 2], sum(slot_loads[g % 2:g + 1:2]))
                if m >= RING:
                    pe.wait_ge(part_ready, m - RING + 1)
                pe.matmul(S_ps[m % RING][:, :], q_op[g % 2][:, half, j, i * P:(i + 1) * P],
                          b["k_op"][:, g, h * HALF:(h + 1) * HALF], start=True, stop=True).then_inc(scored, 1)

            def project(c):
                x, k = c // dk, c % dk
                w, h = x // 2, x % 2
                if x >= RING and k == 0:
                    pe.wait_ge(lo_ready, x - RING + 1)
                t = slice(h * HALF, (h + 1) * HALF)
                last = parts_matmul(pe, E_ps[x % RING][:, :], (b["qw"][0][:, w, k, :], b["qw"][1][:, w, k, :]),
                                    (b["xT"][0][:, k, t], b["xT"][1][:, k, t]), start=(k == 0), stop=(k == dk - 1))
                if k == dk - 1:
                    last.then_inc(projected, 1)

            def key_scores(n, u, j):
                g, half = n // 2, n % 2
                e = PER * (UNITS * n + u) + j
                if u == 0 and j == 0:
                    pe.wait_ge(m_loaded[n % 2], 32 * (n // 2 + 1))
                if e == 0:
                    pe.wait_ge(lo_ready, PROJECTIONS)
                if e >= RING:
                    pe.wait_ge(exp_ready, e - RING + 1)
                pe.matmul(E_ps[e % RING][:, :], b["k_op"][:, g, u * P:(u + 1) * P], q_op[g % 2][:, half, j, :],
                          start=True, stop=True).then_inc(keyed, 1)

            def mix(k):
                n, u = k // UNITS, k % UNITS
                pe.wait_ge(exp_ready, PER * (k + 1))
                if u == 0 and n >= 1:
                    pe.wait_ge(mixT_ready, n)
                for j in range(PER):
                    last = pe.matmul(mix_ps[32 * j:32 * j + 32, :], b["v"][:, u, n // 2, :], prob[:, k % 2, j, :],
                                     start=(u == 0), stop=(u == UNITS - 1), skip_group_check=True)
                last.then_inc(mixed, 1)

            def turn_maxima(n):
                pe.wait_ge(max_ready, n + 1)
                if n >= 2:
                    pe.wait_ge(o_ready, n - 1)
                pe.transpose(turn_ps[0:16, 0:P], neg_max[:, n % 2, :], core.ident[:, :]).then_inc(max_turned, 1)

            def turn_mix(n):
                pe.wait_ge(mixT_ready, n + 1)
                pe.wait_ge(maxT_ready, min(n + 2, STAGES))
                if n >= 1:
                    pe.wait_ge(o_ready, n)
                for i in range(4):
                    last = pe.transpose(turn_ps[:, i * P:(i + 1) * P], mixT[:, i * P:(i + 1) * P], core.ident[:, :])
                last.then_inc(mix_turned, 1)

            def early_output(s):
                if s == EARLY:
                    pe.wait_ge(part_ready, 32 * STAGES)
                    pe.wait_ge(o_ready, STAGES - 1)
                    early.tensor_turn(pe, 0)
                    early.tensor_turn(pe, 1)
                if s == EARLY + 1:
                    early.tensor_turn(pe, 2)
                    pe.wait_ge(early.lo_ready, 1)
                    early.tensor_turn(pe, 3)
                    pe.wait_ge(ow_lo_ready, core.dk)
                if 0 <= s - EARLY - 2 < 4:
                    i = s - EARLY - 2
                    pe.wait_ge(*((early.lo_ready, i + 2) if i < 3 else (early.residual, 1)))
                    early.tensor_project(pe, i)

            for s in range(SLOTS):
                k = s - LEAD
                keys = 0 <= k < STAGES * UNITS
                queries = s < STAGES * UNITS
                for j in range(PER):
                    if keys:
                        key_scores(k // UNITS, k % UNITS, j)
                    if queries:
                        score(PER * s + j)
                    if projects(s, j) >= 0:
                        project(projects(s, j))
                    if j == 2 and turns_maxima(s) >= 0:
                        turn_maxima(turns_maxima(s))
                    if j == 2 and s >= EARLY:
                        early_output(s)
                if k >= 1:
                    mix(k - 1)
                if turns_mix(s) >= 0:
                    turn_mix(turns_mix(s))
            turn_mix(STAGES - 1)

        @block.scalar
        def _(act):
            for x in range(PROJECTIONS):
                act.wait_ge(projected, x + 1)
                act.activation(q_target(x, 0), E_ps[x % RING][:, :], ACT.Identity, bias=q_bias(x))\
                   .then_inc(hi_ready, 1)
            act.wait_ge(lo_ready, PROJECTIONS)
            for n in range(STAGES):
                for u in range(UNITS):
                    for j in range(PER):
                        k = UNITS * n + u
                        e = PER * k + j
                        act.wait_ge(keyed, e + 1)
                        if k >= 2 and j == 0:
                            act.wait_ge(mixed, k - 1)
                        act.activation(prob[:, k % 2, j, :], E_ps[e % RING][:, :], ACT.Exp, scale=SCALE)\
                           .then_inc(exp_ready, 1)
                    if u == 4 and STAGES // 2 <= n < STAGES // 2 + core.dk:
                        act.wait_ge(weights_loaded, 16)
                        act.copy(b["ow"][n - STAGES // 2][0], ow_raw[:, n - STAGES // 2, :]).then_inc(ow_hi_ready, 1)
                    for i in range(4):
                        if UNITS * n + u + LEAD == EARLY + i // 2:
                            early.scalar_hi(act, i)
                    if u == 0 and n >= 1:
                        act.wait_ge(mixed, UNITS * n)
                        if n >= 2:
                            act.wait_ge(mix_turned, n - 1)
                        act.copy(mixT[:, :], mix_ps[:, :]).then_inc(mixT_ready, 1)
            act.wait_ge(mixed, UNITS * STAGES)
            act.wait_ge(mix_turned, STAGES - 1)
            act.copy(mixT[:, :], mix_ps[:, :]).then_inc(mixT_ready, 1)

        @block.vector
        def _(dve):
            def maximum(m):
                n, t = m // 32, m % 32
                i, j, h = t // 8, t // 2 % PER, t % 2
                dve.wait_ge(scored, m + 1)
                if t == 0 and n >= 1:
                    dve.wait_ge(max_ready, n)
                at = PER * j + i
                dve.tensor_reduce(neg_part[:, h, at:at + 1], S_ps[m % RING][:, :], AX_X, ALU.max,
                                  negate=True).then_inc(part_ready, 1)
                if t == 31:
                    dve.wait_ge(part_ready, 32 * (n + 1))
                    if n >= 2:
                        dve.wait_ge(max_turned, n - 1)
                    dve.tensor_tensor(neg_max[:, n % 2, :], neg_part[:, 0, :], neg_part[:, 1, :], ALU.min)\
                       .then_inc(max_ready, 1)

            def split_q(x):
                dve.wait_ge(hi_ready, x + 1)
                dve.scalar_tensor_tensor(out=q_target(x, 1), in0=E_ps[x % RING][:, :], scalar=q_bias(x),
                                         in1=q_target(x, 0).bitcast(F32), op0=ALU.add, op1=ALU.subtract)\
                   .then_inc(lo_ready, 1)

            def maxima_out(n):
                dve.wait_ge(max_turned, n + 1)
                if n >= 2:
                    dve.wait_ge(m_loaded[n % 2], 32 * (n // 2))
                hi, lo = maxT_hi[:, n % 2, :], maxT_lo[:, n % 2, :]
                dve.tensor_copy(hi, turn_ps[0:16, 0:P]).then_inc(maxT_hi_ready, 1)
                dve.wait_ge(maxT_hi_ready, n + 1)
                dve.tensor_tensor(lo, turn_ps[0:16, 0:P], hi.bitcast(F32), ALU.subtract).then_inc(maxT_ready, 1)

            def normalise(n):
                g, half = n // 2, n % 2
                dve.wait_ge(mix_turned, n + 1)
                v = turn_ps[:, :].rearrange("p (i j e) -> p i j e", i=4, e=32)
                dve.reciprocal(den_inv[:, :], turn_ps[:, :].rearrange("p (a e) -> p a e", e=32)[:, :, DH])\
                   .then_inc(inv_ready, 1)
                dve.wait_ge(inv_ready, n + 1)
                out = b["o"][:, 4 * half:4 * half + 4, PER * DH * g:PER * DH * (g + 1)]
                inv = den_inv[:, :].rearrange("p (i j) -> p i j", j=PER)
                dve.tensor_tensor(out.rearrange("p i (j e) -> p i j e", e=DH), v[:, :, :, 0:DH], bcast(inv, DH),
                                  ALU.mult).then_inc(o_ready, 1)

            for s in range(SLOTS):
                for j in range(PER):
                    if s < STAGES * UNITS:
                        maximum(PER * s + j)
                    if j == 1:
                        for x in splits(s):
                            split_q(x)
                        if turns_maxima(s) >= 0:
                            maxima_out(turns_maxima(s))
                if turns_mix(s) >= 0:
                    normalise(turns_mix(s))
                if s == EARLY:
                    dve.wait_ge(x_biased, tiles)
                for i in range(4):
                    if s == EARLY + i // 2:
                        early.vector_lo(dve, i)
                    if s == EARLY + 3 + i:
                        early.vector_residual(dve, i)
            early.vector_residual(dve, 3)
            normalise(STAGES - 1)
            dve.wait_ge(early.residual, 4)
            dve.wait_ge(o_ready, STAGES)


def phase_gqa_output(core, scope, b):
    nc, tiles = core.nc, core.tiles
    ps = lambda what: scope.enter_context(nc.psum_tensor(f"o_{what}", [P, HALF], F32))
    late = HeadOutput(core, b, "o", 4, [ps(f"turn{i}") for i in range(4)], [ps(f"out{i}") for i in range(4)])
    rows = RowStats(core, "o")
    chain_sem = core.sem("o_chain")

    with nc.Block() as block:
        @block.tensor
        def _(pe):
            for i in range(4, tiles):
                late.tensor_turn(pe, i)
            for i in range(4, tiles):
                late.tensor_project(pe, i)

        @block.scalar
        def _(act):
            for i in range(4, tiles):
                late.scalar_hi(act, i)
            rows.scalar_std(act, range(0, 4), 4)

        @block.vector
        def _(dve):
            chain = Chain(dve, chain_sem)
            for i in range(4, tiles):
                late.vector_lo(dve, i)
            rows.vector_stats(dve, chain, range(0, 4))
            for i in range(4, tiles):
                late.vector_residual(dve, i)
                if i == 5:
                    rows.vector_rstd(dve, chain, range(0, 4))
            dve.wait_ge(late.residual, tiles - 4)


def hybrid_layer(nc, d, out, T, D, until=99):
    out_dram = out.rearrange("o (i p) d -> (o i) p d", p=P)
    with ExitStack() as ctx:
        core = Core(nc, ctx, T, D)
        ffn1_loaded = [core.lasting_sem(f"ffn1_loaded{s}") for s in range(3)]
        ffn2_loaded = [core.lasting_sem(f"ffn2_loaded{s}") for s in range(3)]
        gqa_loaded = [core.lasting_sem(f"gqa_loaded{s}") for s in range(4)]
        stored = core.lasting_sem("stored")
        with ExitStack() as a:
            t = lambda name, shape: a.enter_context(nc.sbuf_tensor(name, shape, F32R))
            wa = {"qkv_hi": t("qkv_hi", [P, 3, 1024]), "qkv_lo": t("qkv_lo", [P, 3, 1024]),
                  "wo_hi": t("wo_hi", [P, 1024]), "wo_lo": t("wo_lo", [P, 1024]),
                  "pw_hi": t("pw_hi", [P, D]), "pw_lo": t("pw_lo", [P, D])}
            wa |= {name: a.enter_context(nc.sbuf_tensor(name, [P, n], F32)) for name, n in
                   (("bv_row", 1024), ("pb_row", D))}
            wa = {k: v[:] for k, v in wa.items()}
            qkvT = (t("qkvT_hi", [P, 3, T]), t("qkvT_lo", [P, 3, T]))
            with ExitStack() as scope:
                phase_conv(core, scope, qkvT, wa, d)
                core.end_phase()
            with ExitStack() as scope:
                phase_block_attention(core, scope, qkvT, wa, d, ffn1_loaded)
                core.end_phase()
        if until > 1:
            with ExitStack() as scope:
                phase_ffn(core, scope, "f1", ffn1_loaded,
                          after_split=lambda sp: load_gqa_weights(core, sp, d, gqa_loaded))
                core.end_phase()
        if until > 2:
            with ExitStack() as outer:
                t = lambda name, shape, dt: outer.enter_context(nc.sbuf_tensor(name, shape, dt))
                b = {"v": t("b_v", [P, core.tiles, GROUPS, 32], F32), "k_op": t("b_k_op", [OPERAND, GROUPS, T], F32R),
                     "qT": (t("b_qT_hi", [P, core.dk, T], F32R), t("b_qT_lo", [P, core.dk, T], F32R)),
                     "qw": [t(f"b_qw_{s}", [P, core.dk - 1, core.dk, P], F32R) for s in ("hi", "lo")],
                     "q_op": t("b_q_op", [OPERAND, 2, PER, HALF], F32R),
                     "first_k_loaded": core.lasting_sem("first_k_loaded"),
                     "first_q_loaded": core.lasting_sem("first_q_loaded"),
                     "k_loaded": core.lasting_sem("k_loaded"),
                     "q_loaded": [core.lasting_sem(f"q_loaded{s}") for s in range(2)]}
                with ExitStack() as scope:
                    b["xT"] = [scope.enter_context(nc.sbuf_tensor(f"b_xT_{s}", [P, core.dk, T], F32R))
                               for s in ("hi", "lo")]
                    phase_gqa_projections(core, scope, b, gqa_loaded)
                    core.end_phase()
                b["o"] = t("b_o", [P, core.tiles, D], F32)
                with ExitStack() as scope:
                    with ExitStack() as banks:
                        phase_gqa_core(core, scope, banks, b, d, gqa_loaded[3], ffn2_loaded)
                        core.end_phase()
                    with ExitStack() as banks:
                        phase_gqa_output(core, banks, b)
                        core.end_phase()
        if until > 3:
            with ExitStack() as scope:
                phase_ffn(core, scope, "f2", ffn2_loaded, store=(stored, out_dram))
                core.end_phase()
        else:
            with nc.Block() as block:
                @block.sync
                def _(sp):
                    for i in range(core.tiles):
                        sp.dma_start(out_dram[i], core.x[:, i, :]).then_inc(stored, 16)
                    sp.wait_ge(stored, 16 * core.tiles)


def kernel(**inputs):
    import numpy as np

    import concourse.bacc as bacc
    from concourse.bass_utils import run_bass_kernel_spmd

    w = {name: np.asarray(a) for name, a in inputs.items()}
    x = w["L0_attn_a_inputs"]
    A, B = w["L0_ffn_A"], w["L0_ffn_B"]
    D = x.shape[-1]
    a, g = "L0_attn_a_", "L0_attn_b_"
    columns = [w[a + "conv_b"], w[a + "bq"], w[a + "bk"], w[a + "bo"], w[g + "q_b"], w[g + "k_b"], w[g + "v_b"]]
    rows = [w[a + "bv"], w[a + "proj_b"], w[g + "o_b"]]
    arrays = {
        "x": x,
        "conv_w": w[a + "conv_w"],
        "wq": w[a + "wq"],
        "wk": w[a + "wk"],
        "wv": w[a + "wv"],
        "wo": w[a + "wo"],
        "proj_w": w[a + "proj_w"],
        "bias_cols": np.concatenate([c.reshape(-1, P) for c in columns]).T,
        "bias_rows": np.concatenate([r.reshape(1, -1) for r in rows], axis=1),
        "WrT": w["L0_ffn_Wr"].T,
        "AT": A.reshape(-1, D).T,
        "Bm": B.transpose(0, 2, 1).reshape(-1, D),
        "qwT": w[g + "q_w"].T,
        "kwT": w[g + "k_w"].T,
        "vwT": w[g + "v_w"].T,
        "owT": w[g + "o_w"].T,
    }
    arrays = {"in_" + name: np.ascontiguousarray(v) for name, v in arrays.items()}
    nc = bacc.Bacc("TRN2", target_bir_lowering=False, num_devices=1)
    d = {name[3:]: nc.dram_tensor(name, v.shape, mybir.dt.from_np(v.dtype), kind="ExternalInput").ap()
         for name, v in arrays.items()}
    out = nc.dram_tensor("out", x.shape, F32, kind="ExternalOutput").ap()
    hybrid_layer(nc, d, out, x.shape[1], D)
    result = run_bass_kernel_spmd(nc, [arrays], core_ids=[0])
    return result.results[0]["out"]
```
